# Optimizing a Trainium2 kernel written in Bass

```python
import numpy as np
import jax
import jax.numpy as jnp

def _softmax(x, axis=-1):
    return jax.nn.softmax(x, axis=axis)

def _gelu(x):
    return jax.nn.gelu(x, approximate=True)

def _silu(x):
    return jax.nn.silu(x)

def _sigmoid(x):
    return jax.nn.sigmoid(x)

def _layernorm(x, axis=-1, eps=1e-05):
    m = jnp.mean(x, axis=axis, keepdims=True)
    v = jnp.var(x, axis=axis, keepdims=True)
    return (x - m) / jnp.sqrt(v + eps)

def _scatter_add(tgt, idx, src, axis=0):
    return tgt.at[idx].add(src)

def _segment_sum(src, seg, n):
    return jax.ops.segment_sum(src, seg, n)
kernel_name = 'mk_perceiver_d2_seqx_r4_240593'

def setup_inputs(seed: int=0):
    np.random.seed(seed)
    _w = jnp.asarray

    def _rec_inputs():
        import jax
        import jax.numpy as jnp
        _rk = jax.random.key(seed)
        x = -0.0005146 + 1 * jax.random.normal(jax.random.fold_in(_rk, 1), (64, 32, 256), jnp.float32)
        _lenS = 32 - jax.random.randint(jax.random.fold_in(_rk, 7), (64,), 0, max(1, 32 // 4) + 1, jnp.int32)
        _lenS2 = 257 - jax.random.randint(jax.random.fold_in(_rk, 8), (64,), 0, max(1, 257 // 4) + 1, jnp.int32)
        _ctx_1024P = jax.random.normal(jax.random.fold_in(_rk, 11), (64, 16, 256), jnp.float32)
        _ctx_1024c = jax.random.dirichlet(jax.random.fold_in(_rk, 511), 0.3 * jnp.ones((16,), jnp.float32), (64, 257))
        _ctx_1024t = jnp.einsum('bsk,bkd->bsd', _ctx_1024c, _ctx_1024P)
        _ctx_1024t = _ctx_1024t * jax.lax.rsqrt(jnp.mean(jnp.square(_ctx_1024t)) + 1e-12) * 0.953939
        ctx_1024 = -0.000392918 + 0.999932 * (_ctx_1024t + 0.3 * jax.random.normal(jax.random.fold_in(_rk, 611), (64, 257, 256), jnp.float32))
        _validS = jnp.arange(32)[None, :] < _lenS[:, None]
        _validS2 = jnp.arange(257)[None, :] < _lenS2[:, None]
        _causal = jnp.tril(jnp.ones((32, 32), dtype=bool))
        mask_BxS2_bf1 = jnp.ones((64, 257), dtype=bool)
        return (x, ctx_1024, mask_BxS2_bf1)
    x, ctx_1024, mask_BxS2_bf1 = _rec_inputs()

    def _L0_xattn_setup():
        import jax, jax.numpy as jnp
        import numpy as np
        DIM = 256
        DIM_LATENT = 256
        DIM_HEAD = 64
        HEADS = 16
        INNER = HEADS * DIM_HEAD

        def layernorm(x, g, b, eps=1e-05):
            m = jnp.mean(x, axis=-1, keepdims=True)
            v = jnp.mean((x - m) ** 2, axis=-1, keepdims=True)
            return (x - m) / jnp.sqrt(v + eps) * g + b

        def rmsnorm(x, gamma, eps=1e-08):
            n = jnp.linalg.norm(x, axis=-1, keepdims=True) * x.shape[-1] ** (-0.5)
            return x / jnp.maximum(n, eps) * gamma
        key = jax.random.key(seed)
        ks = jax.random.split(key, 8)
        b, n, m = (4, 1024, 128)
        x = jax.random.normal(ks[0], (b, n, DIM), dtype=jnp.float32)
        latents = jax.random.normal(ks[1], (b, m, DIM_LATENT), dtype=jnp.float32)
        mask = jnp.ones((b, n), dtype=bool)
        s = 0.02
        return {'x': x, 'latents': latents, 'mask': mask, 'ln_x_g': jnp.ones((DIM,), jnp.float32), 'ln_x_b': jnp.zeros((DIM,), jnp.float32), 'ln_l_g': jnp.ones((DIM_LATENT,), jnp.float32), 'ln_l_b': jnp.zeros((DIM_LATENT,), jnp.float32), 'qn_g': jnp.ones((DIM_HEAD,), jnp.float32), 'kn_g': jnp.ones((DIM_HEAD,), jnp.float32), 'Wq': jax.random.normal(ks[2], (DIM_LATENT, INNER), jnp.float32) * s, 'Wkv': jax.random.normal(ks[3], (DIM, 2 * INNER), jnp.float32) * s, 'Wout': jax.random.normal(ks[4], (INNER, DIM_LATENT), jnp.float32) * s, 'bout': jnp.zeros((DIM_LATENT,), jnp.float32)}
    _L0_xattn_all = _L0_xattn_setup()
    _L0_xattn_in = {k: v for k, v in _L0_xattn_all.items() if k in ('ln_x_g', 'ln_x_b', 'ln_l_g', 'ln_l_b', 'qn_g', 'kn_g', 'Wq', 'Wkv', 'Wout', 'bout')}
    del _L0_xattn_all

    def _L0_attn_setup():
        import jax, jax.numpy as jnp
        import numpy as np
        NUM_HEADS = 16
        EPS = float(jnp.finfo(jnp.float32).eps)

        def rms_norm(x, w):
            ms = jnp.mean(x * x, axis=-1, keepdims=True)
            return x * jax.lax.rsqrt(ms + EPS) * w
        key = jax.random.key(seed)
        k = jax.random.split(key, 5)
        B, N, D = (4, 512, 256)
        Dh = D // NUM_HEADS
        return {'x': jax.random.normal(k[0], (B, N, D), dtype=jnp.float32), 'Wq': jax.random.normal(k[1], (D, D), dtype=jnp.float32) * 0.02, 'Wk': jax.random.normal(k[2], (D, D), dtype=jnp.float32) * 0.02, 'Wv': jax.random.normal(k[3], (D, D), dtype=jnp.float32) * 0.02, 'Wo': jax.random.normal(k[4], (D, D), dtype=jnp.float32) * 0.02, 'qn_w': jnp.ones((Dh,), dtype=jnp.float32), 'kn_w': jnp.ones((Dh,), dtype=jnp.float32)}
    _L0_attn_all = _L0_attn_setup()
    _L0_attn_in = {k: v for k, v in _L0_attn_all.items() if k in ('Wq', 'Wk', 'Wv', 'Wo', 'qn_w', 'kn_w')}
    del _L0_attn_all

    def _L0_ffn_setup():
        import jax, jax.numpy as jnp
        import numpy as np
        TOP_K = 8
        CAPACITY = 128

        def _silu(x):
            return x * jax.nn.sigmoid(x)
        key = jax.random.key(seed)
        ks = jax.random.split(key, 7)
        B, S, H, E, I, Is = (2, 256, 256, 64, 128, 512)
        s = 0.05
        return {'hidden_states': jax.random.normal(ks[0], (B, S, H), jnp.float32), 'gate_w': jax.random.normal(ks[1], (H, E), jnp.float32) * s, 'shared_gate_w': jax.random.normal(ks[2], (H, 1), jnp.float32) * s, 'shared_gate_up_w': jax.random.normal(ks[3], (H, 2 * Is), jnp.float32) * s, 'shared_down_w': jax.random.normal(ks[4], (Is, H), jnp.float32) * s, 'expert_gate_up_w': jax.random.normal(ks[5], (E, H, 2 * I), jnp.float32) * s, 'expert_down_w': jax.random.normal(ks[6], (E, I, H), jnp.float32) * s}
    _L0_ffn_all = _L0_ffn_setup()
    _L0_ffn_in = {k: v for k, v in _L0_ffn_all.items() if k in ('gate_w', 'shared_gate_w', 'shared_gate_up_w', 'shared_down_w', 'expert_gate_up_w', 'expert_down_w')}
    del _L0_ffn_all

    def _L1_xattn_setup():
        import jax, jax.numpy as jnp
        import numpy as np
        B, S, F = (2, 512, 256)
        H, DH = (16, 64)
        O = 256
        key = jax.random.key(seed)
        ks = jax.random.split(key, 7)
        sc = 0.02
        return {'inputs_q': jax.random.normal(ks[0], (B, S, F), jnp.float32), 'inputs_kv': jax.random.normal(ks[1], (B, S, F), jnp.float32), 'wq': jax.random.normal(ks[2], (F, H, DH), jnp.float32) * sc, 'wk': jax.random.normal(ks[3], (F, H, DH), jnp.float32) * sc, 'wv': jax.random.normal(ks[4], (F, H, DH), jnp.float32) * sc, 'wo': jax.random.normal(ks[5], (H, DH, O), jnp.float32) * sc, 'bo': jnp.zeros((O,), jnp.float32)}
    _L1_xattn_all = _L1_xattn_setup()
    _L1_xattn_in = {k: v for k, v in _L1_xattn_all.items() if k in ('wq', 'wk', 'wv', 'wo', 'bo')}
    del _L1_xattn_all

    def _L1_attn_setup():
        import jax, jax.numpy as jnp
        import numpy as np
        N_HEAD = 16
        LATENT = 32

        def _rotate_half(x):
            xe = x[..., ::2]
            xo = x[..., 1::2]
            return jnp.stack((-xo, xe), axis=-1).reshape(x.shape)

        def _rope_tables(T, latent_dim, dtype):
            inv_freq = 1.0 / 10000.0 ** (jnp.arange(0, latent_dim, 2, dtype=jnp.float32) / latent_dim)
            t = jnp.arange(T, dtype=jnp.float32)
            freqs = jnp.outer(t, inv_freq)
            cos = jnp.repeat(jnp.cos(freqs), 2, axis=-1)[:, :latent_dim]
            sin = jnp.repeat(jnp.sin(freqs), 2, axis=-1)[:, :latent_dim]
            return (cos.astype(dtype), sin.astype(dtype))
        key = jax.random.key(seed)
        ks = jax.random.split(key, 14)
        C = 256
        hd = C // N_HEAD
        L = LATENT
        s = 0.02
        return {'x': jax.random.normal(ks[0], (4, 512, C), jnp.float32), 'c_attn_w': jax.random.normal(ks[1], (3 * C, C), jnp.float32) * s, 'c_attn_b': jnp.zeros((3 * C,), jnp.float32), 'q2l_w': jax.random.normal(ks[2], (L, hd), jnp.float32) * s, 'q2l_b': jnp.zeros((L,), jnp.float32), 'kv2l_w': jax.random.normal(ks[3], (L, hd), jnp.float32) * s, 'kv2l_b': jnp.zeros((L,), jnp.float32), 'l2o_w': jax.random.normal(ks[4], (hd, L), jnp.float32) * s, 'l2o_b': jnp.zeros((hd,), jnp.float32), 'wqk_w': jax.random.normal(ks[5], (L, L), jnp.float32) * s, 'wqk_b': jnp.zeros((L,), jnp.float32), 'cproj_w': jax.random.normal(ks[6], (C, C), jnp.float32) * s, 'cproj_b': jnp.zeros((C,), jnp.float32)}
    _L1_attn_all = _L1_attn_setup()
    _L1_attn_in = {k: v for k, v in _L1_attn_all.items() if k in ('c_attn_w', 'c_attn_b', 'q2l_w', 'q2l_b', 'kv2l_w', 'kv2l_b', 'l2o_w', 'l2o_b', 'wqk_w', 'wqk_b', 'cproj_w', 'cproj_b')}
    del _L1_attn_all

    def _L1_ffn_setup():
        import jax, jax.numpy as jnp
        import numpy as np
        D_MODEL = 256
        key = jax.random.key(seed)
        k_x, k_w, k_a1, k_a2 = jax.random.split(key, 4)
        x = jax.random.normal(k_x, (4, 512, D_MODEL), dtype=jnp.float32)
        weight = jax.random.normal(k_w, (D_MODEL, D_MODEL), dtype=jnp.float32) * 0.02
        aux_weight1 = jax.random.normal(k_a1, (D_MODEL, D_MODEL), dtype=jnp.float32) * 0.02
        aux_weight2 = jax.random.normal(k_a2, (D_MODEL, D_MODEL), dtype=jnp.float32) * 0.02
        bias = jnp.zeros((D_MODEL,), dtype=jnp.float32)
        return {'x': x, 'weight': weight, 'aux_weight1': aux_weight1, 'aux_weight2': aux_weight2, 'bias': bias}
    _L1_ffn_all = _L1_ffn_setup()
    _L1_ffn_in = {k: v for k, v in _L1_ffn_all.items() if k in ('weight', 'aux_weight1', 'aux_weight2', 'bias')}
    del _L1_ffn_all
    return {'x': x, 'ctx_1024': ctx_1024, 'mask_BxS2_bf1': mask_BxS2_bf1, 'L0_xattn_ln_x_g': _L0_xattn_in['ln_x_g'], 'L0_xattn_ln_x_b': _L0_xattn_in['ln_x_b'], 'L0_xattn_ln_l_g': _L0_xattn_in['ln_l_g'], 'L0_xattn_ln_l_b': _L0_xattn_in['ln_l_b'], 'L0_xattn_qn_g': _L0_xattn_in['qn_g'], 'L0_xattn_kn_g': _L0_xattn_in['kn_g'], 'L0_xattn_Wq': _L0_xattn_in['Wq'], 'L0_xattn_Wkv': _L0_xattn_in['Wkv'], 'L0_xattn_Wout': _L0_xattn_in['Wout'], 'L0_xattn_bout': _L0_xattn_in['bout'], 'L0_attn_Wq': _L0_attn_in['Wq'], 'L0_attn_Wk': _L0_attn_in['Wk'], 'L0_attn_Wv': _L0_attn_in['Wv'], 'L0_attn_Wo': _L0_attn_in['Wo'], 'L0_attn_qn_w': _L0_attn_in['qn_w'], 'L0_attn_kn_w': _L0_attn_in['kn_w'], 'L0_ffn_gate_w': _L0_ffn_in['gate_w'], 'L0_ffn_shared_gate_w': _L0_ffn_in['shared_gate_w'], 'L0_ffn_shared_gate_up_w': _L0_ffn_in['shared_gate_up_w'], 'L0_ffn_shared_down_w': _L0_ffn_in['shared_down_w'], 'L0_ffn_expert_gate_up_w': _L0_ffn_in['expert_gate_up_w'], 'L0_ffn_expert_down_w': _L0_ffn_in['expert_down_w'], 'L1_xattn_wq': _L1_xattn_in['wq'], 'L1_xattn_wk': _L1_xattn_in['wk'], 'L1_xattn_wv': _L1_xattn_in['wv'], 'L1_xattn_wo': _L1_xattn_in['wo'], 'L1_xattn_bo': _L1_xattn_in['bo'], 'L1_attn_c_attn_w': _L1_attn_in['c_attn_w'], 'L1_attn_c_attn_b': _L1_attn_in['c_attn_b'], 'L1_attn_q2l_w': _L1_attn_in['q2l_w'], 'L1_attn_q2l_b': _L1_attn_in['q2l_b'], 'L1_attn_kv2l_w': _L1_attn_in['kv2l_w'], 'L1_attn_kv2l_b': _L1_attn_in['kv2l_b'], 'L1_attn_l2o_w': _L1_attn_in['l2o_w'], 'L1_attn_l2o_b': _L1_attn_in['l2o_b'], 'L1_attn_wqk_w': _L1_attn_in['wqk_w'], 'L1_attn_wqk_b': _L1_attn_in['wqk_b'], 'L1_attn_cproj_w': _L1_attn_in['cproj_w'], 'L1_attn_cproj_b': _L1_attn_in['cproj_b'], 'L1_ffn_weight': _L1_ffn_in['weight'], 'L1_ffn_aux_weight1': _L1_ffn_in['aux_weight1'], 'L1_ffn_aux_weight2': _L1_ffn_in['aux_weight2'], 'L1_ffn_bias': _L1_ffn_in['bias']}

def reference(x, ctx_1024, mask_BxS2_bf1, L0_xattn_ln_x_g, L0_xattn_ln_x_b, L0_xattn_ln_l_g, L0_xattn_ln_l_b, L0_xattn_qn_g, L0_xattn_kn_g, L0_xattn_Wq, L0_xattn_Wkv, L0_xattn_Wout, L0_xattn_bout, L0_attn_Wq, L0_attn_Wk, L0_attn_Wv, L0_attn_Wo, L0_attn_qn_w, L0_attn_kn_w, L0_ffn_gate_w, L0_ffn_shared_gate_w, L0_ffn_shared_gate_up_w, L0_ffn_shared_down_w, L0_ffn_expert_gate_up_w, L0_ffn_expert_down_w, L1_xattn_wq, L1_xattn_wk, L1_xattn_wv, L1_xattn_wo, L1_xattn_bo, L1_attn_c_attn_w, L1_attn_c_attn_b, L1_attn_q2l_w, L1_attn_q2l_b, L1_attn_kv2l_w, L1_attn_kv2l_b, L1_attn_l2o_w, L1_attn_l2o_b, L1_attn_wqk_w, L1_attn_wqk_b, L1_attn_cproj_w, L1_attn_cproj_b, L1_ffn_weight, L1_ffn_aux_weight1, L1_ffn_aux_weight2, L1_ffn_bias):
    import jax
    import jax.numpy as jnp

    def _L0_xattn_ref(x, latents, mask, ln_x_g, ln_x_b, ln_l_g, ln_l_b, qn_g, kn_g, Wq, Wkv, Wout, bout):
        import jax, jax.numpy as jnp
        import numpy as np
        DIM = 256
        DIM_LATENT = 256
        DIM_HEAD = 64
        HEADS = 16
        INNER = HEADS * DIM_HEAD

        def layernorm(x, g, b, eps=1e-05):
            m = jnp.mean(x, axis=-1, keepdims=True)
            v = jnp.mean((x - m) ** 2, axis=-1, keepdims=True)
            return (x - m) / jnp.sqrt(v + eps) * g + b

        def rmsnorm(x, gamma, eps=1e-08):
            n = jnp.linalg.norm(x, axis=-1, keepdims=True) * x.shape[-1] ** (-0.5)
            return x / jnp.maximum(n, eps) * gamma
        b, n, _ = x.shape
        m = latents.shape[1]
        h, d = (HEADS, DIM_HEAD)
        scale = d ** (-0.5)
        xn = layernorm(x, ln_x_g, ln_x_b)
        ln = layernorm(latents, ln_l_g, ln_l_b)
        q = (ln @ Wq).reshape(b, m, h, d).transpose(0, 2, 1, 3)
        kv = jnp.concatenate([xn @ Wkv, ln @ Wkv], axis=1)
        kv = kv.reshape(b, n + m, 2, h, d)
        k = kv[:, :, 0].transpose(0, 2, 1, 3)
        v = kv[:, :, 1].transpose(0, 2, 1, 3)
        qn = rmsnorm(q, qn_g) * scale
        kn = rmsnorm(k, kn_g)
        sim = jnp.einsum('bhid,bhjd->bhij', qn, kn)
        max_neg = -jnp.finfo(sim.dtype).max
        padded_mask = jnp.concatenate([mask, jnp.ones((b, m), bool)], axis=1)
        sim = jnp.where(padded_mask[:, None, None, :], sim, max_neg)
        attn = jax.nn.softmax(sim.astype(jnp.float32), axis=-1).astype(sim.dtype)
        out = jnp.einsum('bhij,bhjd->bhid', attn, v)
        out = out.transpose(0, 2, 1, 3).reshape(b, m, h * d)
        return out @ Wout + bout

    def _L0_attn_ref(x, Wq, Wk, Wv, Wo, qn_w, kn_w):
        import jax, jax.numpy as jnp
        import numpy as np
        NUM_HEADS = 16
        EPS = float(jnp.finfo(jnp.float32).eps)

        def rms_norm(x, w):
            ms = jnp.mean(x * x, axis=-1, keepdims=True)
            return x * jax.lax.rsqrt(ms + EPS) * w
        B, N, D = x.shape
        H = NUM_HEADS
        Dh = D // H
        scale = Dh ** (-0.5)

        def proj(W):
            return (x @ W.T).reshape(B, N, H, Dh).transpose(0, 2, 1, 3)
        q = rms_norm(proj(Wq), qn_w)
        k = rms_norm(proj(Wk), kn_w)
        v = proj(Wv)
        scores = jnp.einsum('bhnd,bhmd->bhnm', q, k) * scale
        attn = jax.nn.softmax(scores, axis=-1)
        out = jnp.einsum('bhnm,bhmd->bhnd', attn, v)
        out = out.transpose(0, 2, 1, 3).reshape(B, N, D)
        return out @ Wo.T

    def _L0_ffn_ref(hidden_states, gate_w, shared_gate_w, shared_gate_up_w, shared_down_w, expert_gate_up_w, expert_down_w):
        import jax, jax.numpy as jnp
        import numpy as np
        TOP_K = 8
        CAPACITY = 128

        def _silu(x):
            return x * jax.nn.sigmoid(x)
        B, S, H = hidden_states.shape
        x = hidden_states.reshape(-1, H)
        T = x.shape[0]
        E = gate_w.shape[1]
        Is = shared_gate_up_w.shape[1] // 2
        I = expert_gate_up_w.shape[2] // 2
        gu = x @ shared_gate_up_w
        shared = _silu(gu[:, :Is]) * gu[:, Is:] @ shared_down_w
        shared = shared * jax.nn.sigmoid(x @ shared_gate_w)
        logits = x @ gate_w
        probs = jax.nn.softmax(logits.astype(jnp.float32), axis=-1)
        w, idx = jax.lax.top_k(probs, TOP_K)
        w = (w / jnp.sum(w, axis=-1, keepdims=True)).astype(x.dtype)
        e_flat = idx.reshape(-1)
        w_flat = w.reshape(-1)
        A = e_flat.shape[0]
        tok = jnp.arange(A) // TOP_K
        onehot = jax.nn.one_hot(e_flat, E, dtype=jnp.int32)
        pos = jnp.take_along_axis(jnp.cumsum(onehot, axis=0) - 1, e_flat[:, None], axis=1)[:, 0]
        slot = jnp.minimum(pos, CAPACITY)
        buf = jnp.zeros((E, CAPACITY + 1, H), x.dtype).at[e_flat, slot].set(x[tok])
        gu_e = jnp.einsum('ech,ehf->ecf', buf, expert_gate_up_w)
        act = _silu(gu_e[..., :I]) * gu_e[..., I:]
        out_e = jnp.einsum('eci,eih->ech', act, expert_down_w)
        y = out_e[e_flat, slot] * w_flat[:, None]
        y = jnp.where((pos < CAPACITY)[:, None], y, jnp.zeros_like(y))
        y = y.reshape(T, TOP_K, H).sum(axis=1)
        return (y + shared).reshape(B, S, H)

    def _L1_xattn_ref(inputs_q, inputs_kv, wq, wk, wv, wo, bo):
        import jax, jax.numpy as jnp
        import numpy as np
        B, S, F = (2, 512, 256)
        H, DH = (16, 64)
        O = 256
        q = jnp.einsum('bsf,fhd->bshd', inputs_q, wq)
        k = jnp.einsum('bsf,fhd->bshd', inputs_kv, wk)
        v = jnp.einsum('bsf,fhd->bshd', inputs_kv, wv)
        q = q / jnp.sqrt(jnp.asarray(DH, q.dtype))
        scores = jnp.einsum('bqhd,bkhd->bhqk', q, k)
        attn = jax.nn.softmax(scores, axis=-1)
        y = jnp.einsum('bhqk,bkhd->bqhd', attn, v)
        out = jnp.einsum('bqhd,hdo->bqo', y, wo) + bo
        return out

    def _L1_attn_ref(x, c_attn_w, c_attn_b, q2l_w, q2l_b, kv2l_w, kv2l_b, l2o_w, l2o_b, wqk_w, wqk_b, cproj_w, cproj_b):
        import jax, jax.numpy as jnp
        import numpy as np
        N_HEAD = 16
        LATENT = 32

        def _rotate_half(x):
            xe = x[..., ::2]
            xo = x[..., 1::2]
            return jnp.stack((-xo, xe), axis=-1).reshape(x.shape)

        def _rope_tables(T, latent_dim, dtype):
            inv_freq = 1.0 / 10000.0 ** (jnp.arange(0, latent_dim, 2, dtype=jnp.float32) / latent_dim)
            t = jnp.arange(T, dtype=jnp.float32)
            freqs = jnp.outer(t, inv_freq)
            cos = jnp.repeat(jnp.cos(freqs), 2, axis=-1)[:, :latent_dim]
            sin = jnp.repeat(jnp.sin(freqs), 2, axis=-1)[:, :latent_dim]
            return (cos.astype(dtype), sin.astype(dtype))
        B, T, C = x.shape
        H = N_HEAD
        hd = C // H
        L = q2l_w.shape[0]
        qkv = x @ c_attn_w.T + c_attn_b
        q, k, v = jnp.split(qkv, 3, axis=2)

        def heads(t):
            return t.reshape(B, T, H, hd).transpose(0, 2, 1, 3)
        q, k, v = (heads(q), heads(k), heads(v))
        q_lat = q @ q2l_w.T + q2l_b
        k_lat = k @ kv2l_w.T + kv2l_b
        v_lat = v @ kv2l_w.T + kv2l_b
        cos, sin = _rope_tables(T, L, x.dtype)
        cos = cos[None, None]
        sin = sin[None, None]
        q_lat = q_lat * cos + _rotate_half(q_lat) * sin
        k_lat = k_lat * cos + _rotate_half(k_lat) * sin
        q_for_k = q_lat @ wqk_w.T + wqk_b
        att = jnp.einsum('bhql,bhkl->bhqk', q_for_k, k_lat) * L ** (-0.5)
        causal = jnp.tril(jnp.ones((T, T), dtype=bool))
        att = jnp.where(causal[None, None], att, -jnp.inf)
        att = jax.nn.softmax(att, axis=-1)
        y_lat = jnp.einsum('bhqk,bhkl->bhql', att, v_lat)
        y = y_lat @ l2o_w.T + l2o_b
        y = y.transpose(0, 2, 1, 3).reshape(B, T, C)
        return y @ cproj_w.T + cproj_b

    def _L1_ffn_ref(x, weight, aux_weight1, aux_weight2, bias):
        import jax, jax.numpy as jnp
        import numpy as np
        D_MODEL = 256
        h = jnp.einsum('btc,cd->btd', x, weight)
        h = jnp.einsum('btc,cd->btd', h, aux_weight1)
        h = jnp.einsum('btc,cd->btd', h, aux_weight2)
        return jnp.tanh(h + bias)
    x = x + _L0_xattn_ref(ctx_1024, _layernorm(x, axis=-1), mask_BxS2_bf1, L0_xattn_ln_x_g, L0_xattn_ln_x_b, L0_xattn_ln_l_g, L0_xattn_ln_l_b, L0_xattn_qn_g, L0_xattn_kn_g, L0_xattn_Wq, L0_xattn_Wkv, L0_xattn_Wout, L0_xattn_bout)
    x = x + _L0_attn_ref(_layernorm(x, axis=-1), L0_attn_Wq, L0_attn_Wk, L0_attn_Wv, L0_attn_Wo, L0_attn_qn_w, L0_attn_kn_w)
    x = x + _L0_ffn_ref(_layernorm(x, axis=-1), L0_ffn_gate_w, L0_ffn_shared_gate_w, L0_ffn_shared_gate_up_w, L0_ffn_shared_down_w, L0_ffn_expert_gate_up_w, L0_ffn_expert_down_w)
    x = x + _L1_xattn_ref(_layernorm(x, axis=-1), ctx_1024, L1_xattn_wq, L1_xattn_wk, L1_xattn_wv, L1_xattn_wo, L1_xattn_bo)
    x = x + _L1_attn_ref(_layernorm(x, axis=-1), L1_attn_c_attn_w, L1_attn_c_attn_b, L1_attn_q2l_w, L1_attn_q2l_b, L1_attn_kv2l_w, L1_attn_kv2l_b, L1_attn_l2o_w, L1_attn_l2o_b, L1_attn_wqk_w, L1_attn_wqk_b, L1_attn_cproj_w, L1_attn_cproj_b)
    x = x + _L1_ffn_ref(_layernorm(x, axis=-1), L1_ffn_weight, L1_ffn_aux_weight1, L1_ffn_aux_weight2, L1_ffn_bias)
    return x

_drawn_inputs = setup_inputs


def setup_inputs(seed=0):
    import zlib

    import numpy as np

    out = dict(_drawn_inputs(seed))
    spreads = {'L0_xattn_ln_x_g': (1.0, 0.6),
     'L0_xattn_ln_x_b': (0.0, 0.369),
     'L0_xattn_ln_l_g': (1.0, 0.6),
     'L0_xattn_ln_l_b': (0.0, 0.8),
     'L0_xattn_qn_g': (1.0, 0.6),
     'L0_xattn_kn_g': (1.0, 0.6),
     'L0_xattn_bout': (0.0, 0.1),
     'L0_attn_qn_w': (1.0, 0.6),
     'L0_attn_kn_w': (1.0, 0.6),
     'L1_xattn_bo': (0.0, 0.1),
     'L1_attn_c_attn_b': (0.0, 0.8),
     'L1_attn_q2l_b': (0.0, 0.8),
     'L1_attn_kv2l_b': (0.0, 0.8),
     'L1_attn_l2o_b': (0.0, 0.267),
     'L1_attn_wqk_b': (0.0, 0.8),
     'L1_attn_cproj_b': (0.0, 0.1),
     'L1_ffn_bias': (0.0, 0.1)}
    factors = {'L1_xattn_wq': 8.0,
     'L1_xattn_wk': 8.0,
     'L1_attn_c_attn_w': 8.0,
     'L1_attn_q2l_w': 8.0,
     'L1_attn_kv2l_w': 8.0,
     'L1_attn_l2o_w': 8.0,
     'L1_attn_wqk_w': 8.0}
    for name, (base, spread) in spreads.items():
        noise = np.random.default_rng([zlib.crc32(name.encode()), seed]).standard_normal(out[name].shape)
        drawn = base * np.exp(spread * noise) if base else spread * noise
        out[name] = jnp.asarray(drawn.astype(out[name].dtype))
    for name, factor in factors.items():
        out[name] = (out[name] * factor).astype(out[name].dtype)
    return out
```

```python
from collections import namedtuple
from contextlib import ExitStack, contextmanager

import numpy as np
import concourse.bass as bass
from concourse import mybir

F32 = mybir.dt.float32
BF16 = mybir.dt.bfloat16
U32 = mybir.dt.uint32
U8 = mybir.dt.uint8
ALU = mybir.AluOpType
ACT = mybir.ActivationFunctionType
AX = mybir.AxisListType

P = 128
B, S, D = 64, 32, 256
NT = B * S // P
BT = P // S
FC = D // P
H, DH = 16, 64
INNER = H * DH
NP_ = INNER // P
CTX = 257
KF = 2
LEFT = CTX - KF * P
GB = 8
NG = B // GB
GT = GB * S
HC = H // BT
LN_EPS = 1e-5
MASKED = 1e30


def named(things):
    return namedtuple("Named", list(things))(**things)


class Kit:

    def __init__(self, nc, ctx, dram):
        self.nc, self.dram, self.used = nc, dram, []
        self.bank = [ctx.enter_context(nc.psum_tensor(f"bank{i}", [P, 2, 512], F32)) for i in range(4)]
        self.X = ctx.enter_context(nc.sbuf_tensor("residual", [P, NT, D], F32))
        self.ident = ctx.enter_context(nc.sbuf_tensor("ident", [P, P], F32))
        self.neg_half = ctx.enter_context(nc.sbuf_tensor("neg_half", [P, 256], F32))

    @contextmanager
    def stage(self):
        outer, self.used = self.used, []
        with ExitStack() as stack:
            yield stack
            self.nc.clear_and_free_semaphores(self.used)
            self.nc.all_engine_barrier()
        self.used = outer

    def semaphore(self, name):
        self.used.append(self.nc.alloc_semaphore(name=name))
        return self.used[-1]

    def psum(self, i):
        return self.bank[i // 2][:, i % 2, :]

    def buffers(self, stack, **shapes):
        made = {}
        for name, (shape, dtype) in shapes.items():
            made[name] = stack.enter_context(self.nc.sbuf_tensor(f"{name}_{self.nc.next_id()}", shape, dtype))
        return named(made)

    def sems(self, stage, names):
        return named({n: self.semaphore(f"{stage}_{n}") for n in names.split()})

    def pair(self, stage, name):
        return [self.semaphore(f"{stage}_{name}{i}") for i in range(2)]


def hold(engine, sem, value, passed):
    engine.wait_ge(sem, value)
    engine.sem_inc(passed, 1)


def row_stats(nc, dve, rows, stats, mean_var, stats_done, aggr_done, base=0):
    for t, r in enumerate(rows):
        nc.vector.bn_stats(stats[:, t, :], r).then_inc(stats_done, 1)
    for t in range(len(rows)):
        dve.wait_ge(stats_done, base + t + 1)
        nc.vector.bn_aggr(mean_var[:, t, :], stats[:, t, :]).then_inc(aggr_done, 1)


def inv_root(nc, pool, neg_half, out, value, scale, shift, op, done_scaled, n_scaled, done):
    nc.gpsimd.tensor_scalar(out, value, scale, shift, ALU.mult, op).then_inc(done_scaled, 1)
    pool.wait_ge(done_scaled, n_scaled)
    nc.gpsimd.tensor_tensor(out, out, neg_half, ALU.pow).then_inc(done, 1)


def load_inputs(kit):
    nc, d = kit.nc, kit.dram
    sem = kit.sems("load", "x_in half_set")
    with nc.Block() as block:
        @block.sync
        def _(sp):
            sp.dma_start(kit.X[:], d.x.rearrange("(t p) d -> p t d", p=P)).then_inc(sem.x_in, 16)
            sp.dma_start(kit.ident[:], d.ident).then_inc(sem.x_in, 16)
            sp.wait_ge(sem.x_in, 32)

        @block.vector
        def _(dve):
            nc.vector.memset(kit.neg_half[:], -0.5).then_inc(sem.half_set, 1)
            dve.wait_ge(sem.half_set, 1)


def latent_queries(kit):
    nc, d = kit.nc, kit.dram
    X = kit.X
    with kit.stage() as st:
        m = kit.buffers(
            st, xl=([P, NT, D], F32), stats=([P, NT + 1, 6], F32), mv1=([P, NT, 2], F32), mv2=([P, NT, 2], F32),
            r1=([P, NT], F32), r2=([P, NT], F32), g_l=([P, D], F32), b_l=([P, D], F32), g_x=([B, D], F32), b_x=([B, D], F32),
            wq=([P, FC, INNER], F32), wk=([P, FC, INNER], F32), cent=([P, 2, D], F32), ln=([P, 2, D], F32),
            lnT=([P, 2, FC, P], F32), ksq=([P, INNER], F32), qsq=([P, INNER], F32), q=([P, 2, INNER], F32),
            ssk=([P, NT, H], F32), ssq=([P, 2, H], F32), rq=([P, 2, H], F32), qh=([P, 2, INNER], F32),
            qT=([P, 2, NP_, P], F32), last=([B, D], F32), mvl=([B, 1, 2], F32), rl=([B, 1], F32),
            lastn=([B, D], F32), lastT=([P, FC, B], F32), ssl=([B, H], F32), rkl=([B, H], F32), rk=([P, NT, H], F32))
        s = kit.sems("lat", "w_in last_in stats aggr1 aggr2 eps r1 r2 xl cent ln_ready lnT_ps lnT k_ps k_sq kss "
                     "q_ps q_sq q_copied qss rq_scaled rq qh qT_ps qT last_cent passed lastn lastT_ps lastT kl_ps kl_sq "
                     "kl_ss rkl rk_lat tail_ps tail_sb")
        tail = kit.tail_rk
        ln_stored, qT_stored = kit.pair("lat", "ln_stored"), kit.pair("lat", "qT_stored")

        with nc.Block() as block:
            @block.sync
            def _(sp):
                for sb, src in ((m.g_l, d.ln_l_g), (m.b_l, d.ln_l_b)):
                    sp.dma_start(sb[:], src.partition_broadcast(P)).then_inc(s.w_in, 16)
                for sb, src in ((m.g_x, d.ln_x_g), (m.b_x, d.ln_x_b)):
                    sp.dma_start(sb[:], src.partition_broadcast(B)).then_inc(s.w_in, 16)
                sp.dma_start(m.wq[:], d.Wq.rearrange("(f p) n -> p f n", p=P)).then_inc(s.w_in, 16)
                sp.dma_start(m.wk[:], d.Wkv[:, 0:INNER].rearrange("(f p) n -> p f n", p=P)).then_inc(s.w_in, 16)
                sp.dma_start(m.last[:], d.ctx[:, CTX - 1, :]).then_inc(s.last_in, 16)
                with sp.Fori(0, NT // 2) as u:
                    for k in range(2):
                        n = u * 2 + k
                        sp.wait_ge(s.ln_ready, n + 1)
                        sp.dma_start(d.tail_lat[n], m.ln[:, k, :]).then_inc(ln_stored[k], 16)
                        sp.wait_ge(s.qT, n + 1)
                        sp.dma_start(d.qT[:, :, bass.ts(n, P)], m.qT[:, k]).then_inc(qT_stored[k], 16)
                sp.wait_ge(s.lastn, 1)
                sp.dma_start(d.tail_last, m.lastn[:]).then_inc(s.last_in, 16)
                sp.wait_ge(s.last_in, 32)
                for k in range(2):
                    sp.wait_ge(ln_stored[k], 16 * (NT // 2 + 1))
                    sp.wait_ge(qT_stored[k], 16 * (NT // 2 + 1))

            @block.vector
            def _(dve):
                row_stats(nc, dve, [X[:, t, :] for t in range(NT)], m.stats, m.mv1, s.stats, s.aggr1)
                dve.wait_ge(s.r1, 1)
                for t in range(NT):
                    nc.vector.tensor_scalar(m.xl[:, t, :], X[:, t, :], m.mv1[:, t, 0:1], m.r1[:, t:t + 1],
                                            ALU.subtract, ALU.mult).then_inc(s.xl, 1)
                dve.wait_ge(s.xl, NT)
                row_stats(nc, dve, [m.xl[:, t, :] for t in range(NT)], m.stats, m.mv2, s.stats, s.aggr2, NT)
                dve.wait_ge(s.last_in, 16)
                row_stats(nc, dve, [m.last[:]], m.stats[0:B, NT:NT + 1, :], m.mvl, s.stats, s.aggr2, 2 * NT)
                dve.wait_ge(s.r2, 2)
                dve.wait_ge(s.w_in, 96)
                nc.vector.scalar_tensor_tensor(m.lastn[:], m.last[:], m.mvl[:, 0, 0:1], m.g_x[:], ALU.subtract, ALU.mult).then_inc(s.last_cent, 1)
                dve.wait_ge(s.last_cent, 1)
                nc.vector.scalar_tensor_tensor(m.lastn[:], m.lastn[:], m.rl[:, 0:1], m.b_x[:], ALU.mult, ALU.add).then_inc(s.lastn, 1)
                for k in range(2):
                    dve.sem_inc(ln_stored[k], 16)
                    dve.sem_inc(qT_stored[k], 16)
                with dve.Fori(0, NT // 2) as u:
                    for k in range(2):
                        n = u * 2 + k
                        nc.vector.scalar_tensor_tensor(m.cent[:, k, :], m.xl[:, n, :], m.mv2[:, n, 0:1], m.g_l[:],
                                                       ALU.subtract, ALU.mult).then_inc(s.cent, 1)
                        dve.wait_ge(s.cent, n + 1)
                        dve.wait_ge(ln_stored[k], u * 16 + 16)
                        nc.vector.scalar_tensor_tensor(m.ln[:, k, :], m.cent[:, k, :], m.r2[:, bass.ds(n, 1)], m.b_l[:],
                                                       ALU.mult, ALU.add).then_inc(s.ln_ready, 1)
                        dve.wait_ge(s.q_sq, n + 1)
                        nc.vector.tensor_reduce(m.ssq[:, k, :], m.qsq[:].rearrange("p (h e) -> p h e", h=H), AX.X, ALU.add).then_inc(s.qss, 1)
                        dve.wait_ge(s.rq, n + 1)
                        dve.wait_ge(s.q_copied, n + 1)
                        nc.vector.tensor_tensor(m.qh[:, k, :].rearrange("p (h e) -> p h e", h=H), m.q[:, k, :].rearrange("p (h e) -> p h e", h=H),
                                                m.rq[:, k, :].unsqueeze(2).to_broadcast([P, H, DH]), ALU.mult).then_inc(s.qh, 1)
                        dve.wait_ge(s.k_sq, n + 1)
                        nc.vector.tensor_reduce(m.ssk[:, n, :], m.ksq[:].rearrange("p (h e) -> p h e", h=H), AX.X, ALU.add).then_inc(s.kss, 1)
                        dve.wait_ge(s.qT_ps, n + 1)
                        dve.wait_ge(qT_stored[k], u * 16 + 16)
                        nc.vector.tensor_copy(m.qT[:, k].rearrange("p a t -> p (a t)"), kit.bank[3][:].rearrange("p a t -> p (a t)")).then_inc(s.qT, 1)
                dve.wait_ge(s.kl_sq, 1)
                nc.vector.tensor_reduce(m.ssl[:], m.ksq[0:B, :].rearrange("p (h e) -> p h e", h=H), AX.X, ALU.add).then_inc(s.kl_ss, 1)
                for t in range(NT):
                    dve.wait_ge(s.tail_ps, t // 4 + 1)
                    nc.vector.tensor_copy(tail[:, t * BT:(t + 1) * BT, 0:S],
                                          kit.psum(t // 4)[0:H, (t % 4) * P:(t % 4 + 1) * P].rearrange("h (b k) -> h b k", b=BT)).then_inc(s.tail_sb, 1)
                dve.wait_ge(s.tail_ps, 5)
                nc.vector.tensor_copy(tail[:, :, S:S + 1], kit.psum(4)[0:H, 0:B].unsqueeze(2)).then_inc(s.tail_sb, 1)

            @block.gpsimd
            def _(pool):
                pool.wait_ge(s.aggr1, NT)
                inv_root(nc, pool, kit.neg_half[:, 0:NT], m.r1[:], m.mv1[:, :, 1], 1.0, LN_EPS, ALU.add, s.eps, 1, s.r1)
                pool.wait_ge(s.aggr2, NT + 1)
                inv_root(nc, pool, kit.neg_half[:, 0:NT], m.r2[:], m.mv2[:, :, 1], 1.0, LN_EPS, ALU.add, s.eps, 2, s.r2)
                inv_root(nc, pool, kit.neg_half[0:B, 0:1], m.rl[:], m.mvl[:, :, 1], 1.0, LN_EPS, ALU.add, s.eps, 3, s.r2)
                with pool.Fori(0, NT // 2) as u:
                    for k in range(2):
                        n = u * 2 + k
                        hold(pool, s.qss, n + 1, s.passed)
                        inv_root(nc, pool, kit.neg_half[:, 0:H], m.rq[:, k, :], m.ssq[:, k, :], 1.0 / DH, 1e-16, ALU.max, s.rq_scaled, n + 1, s.rq)
                pool.wait_ge(s.kss, NT)
                inv_root(nc, pool, kit.neg_half[:], m.rk[:].rearrange("p t h -> p (t h)"), m.ssk[:].rearrange("p t h -> p (t h)"),
                         1.0 / DH, 1e-16, ALU.max, s.eps, 4, s.rk_lat)
                pool.wait_ge(s.kl_ss, 1)
                inv_root(nc, pool, kit.neg_half[0:B, 0:H], m.rkl[:], m.ssl[:], 1.0 / DH, 1e-16, ALU.max, s.eps, 5, s.rkl)

            @block.scalar
            def _(act):
                with act.Fori(0, NT // 2) as u:
                    for k in range(2):
                        n = u * 2 + k
                        act.wait_ge(s.lnT_ps, n + 1)
                        nc.scalar.copy(m.lnT[:, k].rearrange("p f t -> p (f t)"), kit.psum(0)[:, 0:FC * P]).then_inc(s.lnT, 1)
                        act.wait_ge(s.q_ps, n + 1)
                        nc.scalar.activation(m.qsq[:], kit.bank[2][:].rearrange("p a t -> p (a t)"), ACT.Square).then_inc(s.q_sq, 1)
                        nc.scalar.copy(m.q[:, k, :], kit.bank[2][:].rearrange("p a t -> p (a t)")).then_inc(s.q_copied, 1)
                        act.wait_ge(s.k_ps, n + 1)
                        nc.scalar.activation(m.ksq[:], kit.bank[1][:].rearrange("p a t -> p (a t)"), ACT.Square).then_inc(s.k_sq, 1)
                act.wait_ge(s.lastT_ps, 1)
                nc.scalar.copy(m.lastT[:], kit.psum(0)[:, 0:FC * B].rearrange("p (f t) -> p f t", f=FC)).then_inc(s.lastT, 1)
                act.wait_ge(s.kl_ps, 1)
                act.wait_ge(s.kss, NT)
                nc.scalar.activation(m.ksq[0:B, :], kit.bank[1][0:B].rearrange("p a t -> p (a t)"), ACT.Square).then_inc(s.kl_sq, 1)

            @block.tensor
            def _(pe):
                pe.wait_ge(s.w_in, 96)
                with pe.Fori(0, NT // 2) as u:
                    for k in range(2):
                        n = u * 2 + k
                        pe.wait_ge(s.ln_ready, n + 1)
                        for f in range(FC):
                            mm = nc.tensor.transpose(kit.psum(0)[:, f * P:(f + 1) * P], m.ln[:, k, f * P:(f + 1) * P], kit.ident[:])
                        mm.then_inc(s.lnT_ps, 1)
                        pe.wait_ge(s.lnT, n + 1)
                        for bank, w, done, freed in ((4, m.wq, s.q_ps, s.q_copied), (2, m.wk, s.k_ps, s.k_sq)):
                            pe.wait_ge(freed, n)
                            for half in range(2):
                                for f in range(FC):
                                    mm = nc.tensor.matmul(kit.psum(bank + half), m.lnT[:, k, f, :], w[:, f, half * 512:(half + 1) * 512],
                                                          start=(f == 0), stop=(f == FC - 1))
                            mm.then_inc(done, 1)
                        pe.wait_ge(s.qh, n + 1)
                        pe.wait_ge(s.qT, n)
                        for pr in range(NP_):
                            mm = nc.tensor.transpose(kit.psum(6 + pr // 4)[:, (pr % 4) * P:(pr % 4 + 1) * P], m.qh[:, k, pr * P:(pr + 1) * P], kit.ident[:])
                        mm.then_inc(s.qT_ps, 1)
                pe.wait_ge(s.lastn, 1)
                for f in range(FC):
                    mm = nc.tensor.transpose(kit.psum(0)[:, f * B:(f + 1) * B], m.lastn[:, f * P:(f + 1) * P], kit.ident[0:B, 0:B])
                mm.then_inc(s.lastT_ps, 1)
                pe.wait_ge(s.lastT, 1)
                pe.wait_ge(s.k_sq, NT)
                for half in range(2):
                    for f in range(FC):
                        mm = nc.tensor.matmul(kit.psum(2 + half)[0:B, :], m.lastT[:, f, :], m.wk[:, f, half * 512:(half + 1) * 512],
                                              start=(f == 0), stop=(f == FC - 1))
                mm.then_inc(s.kl_ps, 1)
                pe.wait_ge(s.kl_sq, 1)
                pe.wait_ge(s.rk_lat, 1)
                for t in range(NT):
                    mm = nc.tensor.transpose(kit.psum(t // 4)[0:H, (t % 4) * P:(t % 4 + 1) * P], m.rk[:, t, :], kit.ident[:])
                    if t % 4 == 3:
                        mm.then_inc(s.tail_ps, 1)
                pe.wait_ge(s.rkl, 1)
                nc.tensor.transpose(kit.psum(4)[0:H, 0:B], m.rkl[:], kit.ident[0:B, 0:B]).then_inc(s.tail_ps, 1)


def cross_attention(kit, stage, keyed, wk_t, w_v, w_out, bias, gains):
    nc, d = kit.nc, kit.dram
    X = kit.X
    TAIL = LEFT + (S if keyed else 0)
    NK = KF * P + TAIL
    TILES = [(0, P), (P, P), (KF * P, TAIL)]
    with kit.stage() as st:
        m = kit.buffers(
            st, wkT=([P, NP_, D], F32), wv=([P, FC, INNER], F32), wo=([P, NP_, D], F32), bo=([P, D], F32), gain=([P, 4], F32),
            qT=([P, NP_, GT], F32), qk=([P, FC, GB, H, S], F32), mix=([P, FC, H, GT], F32), oT=([P, NP_, GT], F32),
            rows=([P, 2, KF + 1, D], F32), rowsT=([P, 2, FC, NK], F32),
            prob=([P, HC, NK], F32), probT=([P, 3, 512], F32), top=([P, 2, HC], F32), ntop=([P, 2, HC], F32),
            mass=([P, 2, HC], F32), rmass=([P, 2, HC], F32))
        if keyed:
            mk = kit.buffers(
                st, wk=([P, FC, INNER], F32), raw=([P, 2, KF, D], F32), cent=([P, KF, D], F32), g_x=([P, D], F32), b_x=([P, D], F32),
                stats=([P, KF, 6], F32), mv=([P, 2, KF, 2], F32), rstd=([P, 2, KF], F32), ksq=([P, KF, INNER], F32),
                ss=([P, KF * H], F32), rk=([P, 2, KF * H], F32), rkT=([H, NK], F32), rkb=([P, HC, NK], F32), score=([P, HC, NK], F32), sel=([H, HC, P], F32),
                valid=([1, 2, CTX], U8), mask=([1, 2, NK], BF16), one=([1, P], BF16))
        s = kit.sems(stage, "w_in set mask gain wkT raw_free rows_free stats aggr eps rstd cent rows rT_ps rT k_ps k_sq ss rk_scaled rk "
                     "rkT_ps rkT rkT_tail rkb_ps rkb s_ps score ntop p mass normed pT_ps pT pT1 mix_ps mix0 mix1 o_ps o_act o_dve x_ps x_add "
                     "q_in qk_ps qk_act qk_dve qk_free passed_dve passed_pool")
        raw_in, rows_in = kit.pair(stage, "raw_in"), kit.pair(stage, "rows_in")
        sel_bank = [7, 6, 7, 6]

        row_loads = 48 if keyed else 32

        def pairs(g, j):
            return g * (GB // 2) + (j // 2 + 1)

        score_bank = [4, 5, 4, 5] if keyed else [4, 5, 6, 7]

        with nc.Block() as block:
            @block.sync
            def _(sp):
                sp.dma_start(m.wkT[:], wk_t.rearrange("(a p) n -> p a n", p=P)).then_inc(s.w_in, 16)
                sp.dma_start(m.wv[:], w_v.rearrange("(f p) n -> p f n", p=P)).then_inc(s.w_in, 16)
                sp.dma_start(m.wo[:], w_out.rearrange("(a p) n -> p a n", p=P)).then_inc(s.w_in, 16)
                sp.dma_start(m.bo[:], bias.partition_broadcast(P)).then_inc(s.w_in, 16)
                n_w = 4
                if keyed:
                    sp.dma_start(mk.wk[:], d.Wkv[:, 0:INNER].rearrange("(f p) n -> p f n", p=P)).then_inc(s.w_in, 16)
                    sp.dma_start(mk.g_x[:], d.ln_x_g.partition_broadcast(P)).then_inc(s.w_in, 16)
                    sp.dma_start(mk.b_x[:], d.ln_x_b.partition_broadcast(P)).then_inc(s.w_in, 16)
                    sp.dma_start(mk.sel[:], d.sel).then_inc(s.w_in, 16)
                    for half in range(2):
                        for i, g in enumerate(gains):
                            sp.dma_start(m.gain[half * DH:(half + 1) * DH, i:i + 1], g.unsqueeze(1)).then_inc(s.w_in, 16)

                def group(g):
                    sp.wait_ge(s.qk_free, g + 1)
                    sp.dma_start(m.qT[:], d.qT[:, :, bass.ts(g, GT)]).then_inc(s.q_in, 16)
                    for j in range(GB):
                        n, k = g * GB + j, j % 2
                        if keyed:
                            sp.wait_ge(s.raw_free, n + 1)
                            sp.dma_start(mk.raw[:, k], d.ctx[n, 0:KF * P, :].rearrange("(c p) d -> p c d", p=P)).then_inc(raw_in[k], 16)
                        sp.wait_ge(s.rows_free, n + 1)
                        if keyed:
                            sp.dma_start(m.rows[0:S, k, KF, :], d.tail_lat_b[n]).then_inc(rows_in[k], 16)
                            sp.dma_start(m.rows[S:S + 1, k, KF, :], d.tail_last[bass.ds(n, 1), :]).then_inc(rows_in[k], 16)
                            sp.dma_start(mk.valid[:, k, :], d.mask[bass.ds(n, 1), :]).then_inc(rows_in[k], 16)
                        else:
                            sp.dma_start(m.rows[:, k, 0:KF, :], d.ctx[n, 0:KF * P, :].rearrange("(c p) d -> p c d", p=P)).then_inc(rows_in[k], 16)
                            sp.dma_start(m.rows[0:LEFT, k, KF, :], d.ctx[n, KF * P:CTX, :]).then_inc(rows_in[k], 16)

                with sp.Fori(0, NG) as g:
                    group(g)

            n_weights = 16 * (4 + (8 if keyed else 0))

            @block.vector
            def _(dve):
                dve.sem_inc(s.qk_free, 1)
                dve.sem_inc(s.raw_free, 2)
                dve.sem_inc(s.rows_free, 2)
                if keyed:
                    nc.vector.memset(mk.mask[:], 0.0).then_inc(s.set, 1)
                    nc.vector.memset(mk.one[:], 1.0).then_inc(s.set, 1)
                dve.wait_ge(s.w_in, n_weights)
                if keyed:
                    nc.vector.scalar_tensor_tensor(m.gain[:, 2:3], m.gain[:, 0:1], DH ** -0.5, m.gain[:, 1:2], ALU.mult, ALU.mult).then_inc(s.gain, 1)
                    dve.wait_ge(s.gain, 1)
                    nc.vector.tensor_scalar(m.wkT[:], m.wkT[:], m.gain[:, 2:3], None, ALU.mult).then_inc(s.wkT, 1)
                else:
                    nc.vector.tensor_scalar(m.wkT[:], m.wkT[:], DH ** -0.5, None, ALU.mult).then_inc(s.wkT, 1)
                nc.vector.tensor_tensor(X[:], X[:], m.bo[:].unsqueeze(1).to_broadcast([P, NT, D]), ALU.add).then_inc(s.x_add, 1)

                def norm_stats(n, k, loads):
                    dve.wait_ge(raw_in[k], loads * 16)
                    for c in range(KF):
                        nc.vector.bn_stats(mk.stats[:, c, :], mk.raw[:, k, c, :]).then_inc(s.stats, 1)
                    hold(dve, s.stats, (n + 1) * KF, s.passed_dve)
                    for c in range(KF):
                        nc.vector.bn_aggr(mk.mv[:, k, c, :], mk.stats[:, c, :]).then_inc(s.aggr, 1)

                def norm_rows(n, k):
                    dve.wait_ge(s.rstd, n + 1)
                    for c in range(KF):
                        nc.vector.scalar_tensor_tensor(mk.cent[:, c, :], mk.raw[:, k, c, :], mk.mv[:, k, c, 0:1], mk.g_x[:],
                                                       ALU.subtract, ALU.mult).then_inc(s.cent, 1)
                    dve.wait_ge(s.cent, (n + 1) * KF)
                    dve.sem_inc(s.raw_free, 1)
                    dve.wait_ge(s.rows_free, n + 1)
                    for c in range(KF):
                        nc.vector.scalar_tensor_tensor(m.rows[:, k, c, :], mk.cent[:, c, :], mk.rstd[:, k, c:c + 1], mk.b_x[:],
                                                       ALU.mult, ALU.add).then_inc(s.rows, 1)

                def key_sums(n, k):
                    for c in range(KF):
                        dve.wait_ge(s.k_sq, n * 4 + (2 * c + 2))
                        nc.vector.tensor_reduce(mk.ss[:, c * H:(c + 1) * H], mk.ksq[:, c, :].rearrange("p (h e) -> p h e", h=H), AX.X, ALU.add).then_inc(s.ss, 1)

                def scores(n, k):
                    for c in range(HC):
                        if keyed:
                            hold(dve, s.s_ps, n * HC + (c + 1), s.passed_dve)
                            hold(dve, s.rkb, n * HC + (c + 1), s.passed_dve)
                            nc.vector.tensor_tensor_reduce(mk.score[:, c, :], kit.psum(score_bank[c])[:, 0:NK], mk.rkb[:, c, :], 1.0, -3.0e38,
                                                           ALU.mult, ALU.max, m.top[:, k, c:c + 1]).then_inc(s.score, 1)
                        else:
                            dve.wait_ge(s.s_ps, n * HC + (c + 1))
                            nc.vector.reduce_max(m.top[:, k, c:c + 1], kit.psum(score_bank[c])[:, 0:NK], AX.X).then_inc(s.score, 1)
                    dve.wait_ge(s.score, (n + 1) * HC)
                    nc.vector.tensor_scalar(m.ntop[:, k, :], m.top[:, k, :], -1.0, None, ALU.mult).then_inc(s.ntop, 1)

                def mass(n, k):
                    dve.wait_ge(s.p, n + 1)
                    nc.vector.reciprocal(m.rmass[:, k, :], m.mass[:, k, :]).then_inc(s.mass, 1)

                def copies(n, j):
                    for c, size in ((0, P), (2, TAIL)):
                        dve.wait_ge(s.pT_ps, n * 3 + (c + 1))
                        nc.vector.tensor_copy(m.probT[0:size, c, :], kit.psum(4 + c)[0:size, :]).then_inc(s.pT, 1)
                    dve.wait_ge(s.mix_ps, n * FC + FC)
                    dve.sem_inc(s.rows_free, 1)
                    nc.vector.tensor_copy(m.mix[:, 1, :, j * S:(j + 1) * S], kit.psum(5).rearrange("p (h q) -> p h q", h=H)).then_inc(s.mix1, 1)

                def group(g, more):
                    for i in range(1, H, 2):
                        dve.wait_ge(s.qk_ps, g * H + (i + 1))
                        nc.vector.tensor_copy(m.qk[:, :, :, i, :], kit.psum(3).rearrange("p (f b q) -> p f b q", f=FC, b=GB)).then_inc(s.qk_dve, 1)
                    for j in range(GB):
                        n, k = g * GB + j, j % 2
                        ahead = more or j + 1 < GB
                        if keyed and ahead:
                            norm_rows(n + 1, 1 - k)
                        scores(n, k)
                        if keyed and (more or j + 2 < GB):
                            norm_stats(n + 2, k, pairs(g, j + 2))
                        mass(n, k)
                        if keyed and ahead:
                            key_sums(n + 1, 1 - k)
                        copies(n, j)
                    for i in range(1, NP_ // 2, 2):
                        dve.wait_ge(s.o_ps, g * (NP_ // 2) + (i + 1))
                        nc.vector.tensor_copy(m.oT[:, 2 * i:2 * i + 2, :], kit.psum(2 + i % 2).rearrange("p (a t) -> p a t", a=2)).then_inc(s.o_dve, 1)
                    for i in range(GT // P):
                        dve.wait_ge(s.x_ps, g * (GT // P) + (i + 1))
                        if i == 0:
                            dve.wait_ge(s.x_add, 1)
                        nc.vector.tensor_tensor(X[:, g * (GT // P) + i, :], X[:, g * (GT // P) + i, :], kit.psum(i)[:, 0:D], ALU.add).then_inc(s.x_add, 1)

                if keyed:
                    norm_stats(0, 0, 1)
                    norm_rows(0, 0)
                    norm_stats(1, 1, 1)
                    key_sums(0, 0)
                with dve.Fori(0, NG - 1) as g:
                    group(g, True)
                group(NG - 1, False)

            @block.gpsimd
            def _(pool):
                def rstd(n, k):
                    hold(pool, s.aggr, (n + 1) * KF, s.passed_pool)
                    inv_root(nc, pool, kit.neg_half[:, 0:KF], mk.rstd[:, k, :], mk.mv[:, k, :, 1], 1.0, LN_EPS, ALU.add, s.eps, n + 1, s.rstd)

                def key_norms(n, k):
                    hold(pool, s.ss, (n + 1) * KF, s.passed_pool)
                    inv_root(nc, pool, kit.neg_half[:, 0:KF * H], mk.rk[:, k, :], mk.ss[:], 1.0 / DH, 1e-16, ALU.max, s.rk_scaled, n + 1, s.rk)

                def rk_tail(n):
                    pool.wait_ge(s.rkb_ps, n * HC)
                    nc.gpsimd.tensor_copy(mk.rkT[:, KF * P:NK], kit.tail_rk[:, n, :]).then_inc(s.rkT_tail, 1)

                def mask(n, k, loads):
                    hold(pool, rows_in[k], loads * row_loads, s.passed_pool)
                    for at, rows in ((0, slice(0, KF * P)), (NK - LEFT, slice(KF * P, CTX))):
                        nc.gpsimd.tensor_scalar(mk.mask[:, k, at:at + rows.stop - rows.start], mk.valid[:, k, rows], 1.0, MASKED, ALU.subtract, ALU.mult).then_inc(s.mask, 1)

                def normed(n, k):
                    pool.wait_ge(s.mass, n + 1)
                    nc.gpsimd.tensor_tensor(m.prob[:], m.prob[:], m.rmass[:, k, :].unsqueeze(2).to_broadcast([P, HC, NK]), ALU.mult).then_inc(s.normed, 1)

                def group(g, more):
                    for j in range(GB):
                        n, k = g * GB + j, j % 2
                        if keyed:
                            rk_tail(n)
                            mask(n, k, pairs(g, j))
                            if more or j + 2 < GB:
                                rstd(n + 2, k)
                        normed(n, k)
                        if keyed and (more or j + 1 < GB):
                            key_norms(n + 1, 1 - k)

                if keyed:
                    pool.wait_ge(s.set, 2)
                    rstd(0, 0)
                    rstd(1, 1)
                    key_norms(0, 0)
                with pool.Fori(0, NG - 1) as g:
                    group(g, True)
                group(NG - 1, False)

            @block.scalar
            def _(act):
                def rows_T(n, k):
                    act.wait_ge(s.rT_ps, n + 1)
                    nc.scalar.copy(m.rowsT[:, k], kit.bank[0][:, :, 0:NK]).then_inc(s.rT, 1)

                def key_squares(n, k):
                    for i in range(4):
                        act.wait_ge(s.k_ps, n * 4 + (i + 1))
                        nc.scalar.activation(mk.ksq[:, i // 2, (i % 2) * 512:(i % 2 + 1) * 512], kit.psum(2 + i % 2), ACT.Square).then_inc(s.k_sq, 1)

                def spread_norms(n, k):
                    act.wait_ge(s.rkT_ps, n + 1)
                    nc.scalar.copy(mk.rkT[:, 0:KF * P], kit.psum(6)[0:H, 0:KF * P]).then_inc(s.rkT, 1)
                    for c in range(HC):
                        act.wait_ge(s.rkb_ps, n * HC + (c + 1))
                        nc.scalar.copy(mk.rkb[:, c, :], kit.psum(sel_bank[c])[:, 0:NK]).then_inc(s.rkb, 1)

                def exps(n, k):
                    act.wait_ge(s.ntop, n + 1)
                    act.wait_ge(s.pT_ps, n * 3)
                    for c in range(HC):
                        src = mk.score[:, c, :] if keyed else kit.psum(score_bank[c])[:, 0:NK]
                        e = nc.scalar.activation(m.prob[:, c, :], src, ACT.Exp, bias=m.ntop[:, k, c:c + 1], accum_out=m.mass[:, k, c:c + 1])
                    e.then_inc(s.p, 1)

                def copies(n, j):
                    act.wait_ge(s.pT_ps, n * 3 + 2)
                    nc.scalar.copy(m.probT[:, 1, :], kit.psum(5)).then_inc(s.pT1, 1)
                    act.wait_ge(s.mix_ps, n * FC + 1)
                    nc.scalar.copy(m.mix[:, 0, :, j * S:(j + 1) * S], kit.psum(7).rearrange("p (h q) -> p h q", h=H)).then_inc(s.mix0, 1)

                def group(g, more):
                    for i in range(0, H, 2):
                        act.wait_ge(s.qk_ps, g * H + (i + 1))
                        nc.scalar.copy(m.qk[:, :, :, i, :], kit.psum(2).rearrange("p (f b q) -> p f b q", f=FC, b=GB)).then_inc(s.qk_act, 1)
                    for j in range(GB):
                        n, k = g * GB + j, j % 2
                        ahead = more or j + 1 < GB
                        if keyed:
                            spread_norms(n, k)
                        if ahead:
                            rows_T(n + 1, 1 - k)
                        exps(n, k)
                        if keyed and ahead:
                            key_squares(n + 1, 1 - k)
                        copies(n, j)
                    for i in range(0, NP_ // 2, 2):
                        act.wait_ge(s.o_ps, g * (NP_ // 2) + (i + 1))
                        nc.scalar.copy(m.oT[:, 2 * i:2 * i + 2, :], kit.psum(2 + i % 2).rearrange("p (a t) -> p a t", a=2)).then_inc(s.o_act, 1)

                rows_T(0, 0)
                if keyed:
                    key_squares(0, 0)
                with act.Fori(0, NG - 1) as g:
                    group(g, True)
                group(NG - 1, False)

            @block.tensor
            def _(pe):
                def front(n, k, loads):
                    if keyed:
                        pe.wait_ge(s.rows, (n + 1) * KF)
                    pe.wait_ge(rows_in[k], loads * row_loads)
                    pe.wait_ge(s.rT, n)
                    for f in range(FC):
                        for c, (a, size) in enumerate(TILES):
                            mm = nc.tensor.transpose(kit.psum(f)[:, a:a + size], m.rows[0:size, k, c, f * P:(f + 1) * P], kit.ident[0:size, 0:size])
                    mm.then_inc(s.rT_ps, 1)
                    if keyed:
                        pe.wait_ge(s.rT, n + 1)
                        for i in range(4):
                            c, half = i // 2, i % 2
                            if i >= 2:
                                pe.wait_ge(s.k_sq, n * 4 + (i - 1))
                            for f in range(FC):
                                mm = nc.tensor.matmul(kit.psum(2 + half), m.rowsT[:, k, f, c * P:(c + 1) * P], mk.wk[:, f, half * 512:(half + 1) * 512],
                                                      start=(f == 0), stop=(f == FC - 1))
                            mm.then_inc(s.k_ps, 1)

                def score(n, k, j):
                    if keyed:
                        pe.wait_ge(s.rk, n + 1)
                        for c in range(KF):
                            mm = nc.tensor.transpose(kit.psum(6)[0:H, c * P:(c + 1) * P], mk.rk[:, k, c * H:(c + 1) * H], kit.ident[:])
                        mm.then_inc(s.rkT_ps, 1)
                    else:
                        pe.wait_ge(s.rT, n + 1)
                    for c in range(HC):
                        if keyed:
                            if c == 0:
                                pe.wait_ge(s.rkT, n + 1)
                                pe.wait_ge(s.rkT_tail, n + 1)
                                pe.wait_ge(s.mask, (n + 1) * 2)
                                pe.wait_ge(s.mix0, n)
                            if c >= 2:
                                pe.wait_ge(s.rkb, n * HC + (c - 1))
                            nc.tensor.matmul(kit.psum(sel_bank[c])[:, 0:NK], mk.sel[:, c, :], mk.rkT[:], start=True, stop=True).then_inc(s.rkb_ps, 1)
                            if c >= 2:
                                pe.wait_ge(s.score, n * HC + (c - 1))
                        if c == 0 and not keyed:
                            pe.wait_ge(s.mix0, n)
                        if c == 1:
                            pe.wait_ge(s.mix1, n)
                        for f in range(FC):
                            mm = nc.tensor.matmul(kit.psum(score_bank[c])[:, 0:NK], m.qk[:, f, j, c * BT:(c + 1) * BT, :].rearrange("p h q -> p (h q)"),
                                                  m.rowsT[:, k, f, :], start=(f == 0), stop=(f == FC - 1 and not keyed))
                        if keyed:
                            mm = nc.tensor.matmul(kit.psum(score_bank[c])[:, 0:NK], mk.one[:], mk.mask[:, k, :], start=False, stop=True)
                        mm.then_inc(s.s_ps, 1)

                def mix(n, k):
                    pe.wait_ge(s.normed, n + 1)
                    for t, (a, size) in enumerate(TILES):
                        for c in range(HC):
                            mm = nc.tensor.transpose(kit.psum(4 + t)[0:size, c * P:(c + 1) * P], m.prob[:, c, a:a + size], kit.ident[:])
                        mm.then_inc(s.pT_ps, 1)
                    pe.wait_ge(s.pT, (n + 1) * 2)
                    pe.wait_ge(s.pT1, n + 1)
                    for f in range(FC):
                        for t, (a, size) in enumerate(TILES):
                            mm = nc.tensor.matmul(kit.psum(7 if f == 0 else 5), m.rows[0:size, k, t, f * P:(f + 1) * P], m.probT[0:size, t, :],
                                                  start=(t == 0), stop=(t == len(TILES) - 1))
                        mm.then_inc(s.mix_ps, 1)

                def queries(g):
                    pe.wait_ge(s.q_in, (g + 1) * 16)
                    if keyed:
                        pe.wait_ge(s.k_sq, g * GB * 4 + 4)
                    for i in range(H):
                        if i >= 2:
                            pe.wait_ge(s.qk_dve if i % 2 else s.qk_act, g * (H // 2) + i // 2)
                        pr, half = i // 2, i % 2
                        for f in range(FC):
                            mm = nc.tensor.matmul(kit.psum(2 + i % 2)[:, f * GT:(f + 1) * GT], m.wkT[half * DH:(half + 1) * DH, pr, f * P:(f + 1) * P],
                                                  m.qT[half * DH:(half + 1) * DH, pr, :], start=True, stop=True)
                        mm.then_inc(s.qk_ps, 1)
                    mm = None

                def project(g, more):
                    if keyed:
                        pe.wait_ge(s.k_sq, g * GB * 4 + (GB * 4 + (4 if more else 0)))
                    pe.wait_ge(s.mix0, (g + 1) * GB)
                    pe.wait_ge(s.mix1, (g + 1) * GB)
                    for i in range(NP_ // 2):
                        if i >= 2:
                            pe.wait_ge(s.o_dve if i % 2 else s.o_act, g * (NP_ // 4) + i // 2)
                        for pr in (2 * i, 2 * i + 1):
                            for half in range(2):
                                h = 2 * pr + half
                                for f in range(FC):
                                    mm = nc.tensor.matmul(kit.psum(2 + i % 2)[half * DH:(half + 1) * DH, (pr % 2) * GT:(pr % 2 + 1) * GT],
                                                          m.wv[:, f, h * DH:(h + 1) * DH], m.mix[:, f, h, :], start=(f == 0), stop=(f == FC - 1),
                                                          skip_group_check=True)
                        mm.then_inc(s.o_ps, 1)
                    pe.wait_ge(s.o_act, (g + 1) * (NP_ // 4))
                    pe.wait_ge(s.o_dve, (g + 1) * (NP_ // 4))
                    for i in range(GT // P):
                        for pr in range(NP_):
                            mm = nc.tensor.matmul(kit.psum(i)[:, 0:D], m.oT[:, pr, i * P:(i + 1) * P], m.wo[:, pr, :], start=(pr == 0), stop=(pr == NP_ - 1))
                        mm.then_inc(s.x_ps, 1)

                def group(g, more):
                    queries(g)
                    pe.wait_ge(s.qk_act, (g + 1) * (H // 2))
                    pe.wait_ge(s.qk_dve, (g + 1) * (H // 2))
                    pe.sem_inc(s.qk_free, 1)
                    for j in range(GB):
                        n, k = g * GB + j, j % 2
                        score(n, k, j)
                        if j == 0:
                            pe.wait_ge(s.x_add, g * (GT // P) + 1)
                        if more or j + 1 < GB:
                            front(n + 1, 1 - k, pairs(g, j + 1))
                        mix(n, k)
                    project(g, more)

                pe.wait_ge(s.w_in, n_weights)
                pe.wait_ge(s.wkT, 1)
                if keyed:
                    pe.wait_ge(s.set, 2)
                front(0, 0, 1)
                with pe.Fori(0, NG - 1) as g:
                    group(g, True)
                group(NG - 1, False)


class Norm:

    def __init__(self, kit, stage, stack):
        self.kit, self.nc = kit, kit.nc
        self.m = kit.buffers(stack, stats=([P, NT, 6], F32), mv=([P, NT, 2], F32), rstd=([P, NT], F32))
        self.s = kit.sems(f"{stage}_norm", "stats aggr eps rstd")

    def vector_part(self, dve):
        row_stats(self.nc, dve, [self.kit.X[:, t, :] for t in range(NT)], self.m.stats, self.m.mv, self.s.stats, self.s.aggr)
        dve.wait_ge(self.s.rstd, 1)

    def pool_part(self, pool):
        pool.wait_ge(self.s.aggr, NT)
        inv_root(self.nc, pool, self.kit.neg_half[:, 0:NT], self.m.rstd[:], self.m.mv[:, :, 1], 1.0, LN_EPS, ALU.add, self.s.eps, 1, self.s.rstd)

    def rows(self, out, n):
        return self.nc.vector.tensor_scalar(out, self.kit.X[:, n, :], self.m.mv[:, n, 0:1], self.m.rstd[:, bass.ds(n, 1)], ALU.subtract, ALU.mult)


def plain_queries(kit, stage, w_q):
    nc, d = kit.nc, kit.dram
    GQ = 512
    with kit.stage() as st:
        norm = Norm(kit, stage, st)
        m = kit.buffers(st, wq=([P, FC, INNER], F32), xl=([P, 2, D], F32), xlT=([P, FC, B * S], F32), qT=([P, 2, NP_, GQ], F32))
        s = kit.sems(stage, "w_in xl xlT_ps xlT q_ps q_act q_dve")
        stored = kit.pair(stage, "stored")
        with nc.Block() as block:
            @block.sync
            def _(sp):
                sp.dma_start(m.wq[:], w_q.rearrange("(f p) n -> p f n", p=P)).then_inc(s.w_in, 16)
                with sp.Fori(0, B * S // GQ // 2) as u:
                    for k in range(2):
                        g = u * 2 + k
                        sp.wait_ge(s.q_act, g * 4 + 4)
                        sp.wait_ge(s.q_dve, g * 4 + 4)
                        sp.dma_start(d.qT[:, :, bass.ts(g, GQ)], m.qT[:, k]).then_inc(stored[k], 16)
                for k in range(2):
                    sp.wait_ge(stored[k], 16 * (B * S // GQ // 2 + 1))

            @block.vector
            def _(dve):
                for k in range(2):
                    dve.sem_inc(stored[k], 16)
                norm.vector_part(dve)
                with dve.Fori(0, NT // 2) as u:
                    for k in range(2):
                        n = u * 2 + k
                        dve.wait_ge(s.xlT_ps, u * 2 + max(k - 1, 0))
                        norm.rows(m.xl[:, k, :], n).then_inc(s.xl, 1)
                with dve.Fori(0, B * S // GQ // 2) as u:
                    for k in range(2):
                        g = u * 2 + k
                        dve.wait_ge(stored[k], u * 16 + 16)
                        for i in range(1, NP_, 2):
                            dve.wait_ge(s.q_ps, g * NP_ + (i + 1))
                            nc.vector.tensor_copy(m.qT[:, k, i, :], kit.psum(i)).then_inc(s.q_dve, 1)

            @block.gpsimd
            def _(pool):
                norm.pool_part(pool)

            @block.scalar
            def _(act):
                with act.Fori(0, NT // 2) as u:
                    for k in range(2):
                        n = u * 2 + k
                        act.wait_ge(s.xlT_ps, n + 1)
                        nc.scalar.copy(m.xlT[:, :, bass.ts(n, P)], kit.psum(k)[:, 0:D].rearrange("p (f t) -> p f t", f=FC)).then_inc(s.xlT, 1)
                with act.Fori(0, B * S // GQ // 2) as u:
                    for k in range(2):
                        g = u * 2 + k
                        act.wait_ge(stored[k], u * 16 + 16)
                        for i in range(0, NP_, 2):
                            act.wait_ge(s.q_ps, g * NP_ + (i + 1))
                            nc.scalar.copy(m.qT[:, k, i, :], kit.psum(i)).then_inc(s.q_act, 1)

            @block.tensor
            def _(pe):
                with pe.Fori(0, NT // 2) as u:
                    for k in range(2):
                        n = u * 2 + k
                        pe.wait_ge(s.xl, n + 1)
                        pe.wait_ge(s.xlT, u * 2 + max(k - 1, 0))
                        for f in range(FC):
                            mm = nc.tensor.transpose(kit.psum(k)[:, f * P:(f + 1) * P], m.xl[:, k, f * P:(f + 1) * P], kit.ident[:])
                        mm.then_inc(s.xlT_ps, 1)
                pe.wait_ge(s.xlT, NT)
                pe.wait_ge(s.w_in, 16)
                with pe.Fori(0, B * S // GQ) as g:
                    for i in range(NP_):
                        pe.wait_ge(s.q_dve if i % 2 else s.q_act, g * 4)
                        for f in range(FC):
                            mm = nc.tensor.matmul(kit.psum(i), m.wq[:, f, i * P:(i + 1) * P], m.xlT[:, f, bass.ts(g, GQ)], start=(f == 0), stop=(f == FC - 1))
                        mm.then_inc(s.q_ps, 1)


def rotary_weights(kit, m, w, wo, stage):
    nc, d = kit.nc, kit.dram
    with kit.stage() as st:
        t = kit.buffers(
            st, cw=([P, 6, D], F32), cb=([P, 6], F32), cbb=([P, 6, P], F32), bd=([P, 2, 8, 32], F32), bdv=([P, P], F32), blk=([P, P], F32),
            kvr=([32, 8, 16], F32), lor=([32, 8, 16], F32), kvb=([32, 1], F32), kvbb=([32, P], F32), qlb=([P, 32], F32), klb=([P, 32], F32), lob=([P, 16], F32))
        s = kit.sems(stage + "w", "zero w_in m2_ps bdv cbb out_ps out ready")
        with nc.Block() as block:
            n_in = 0

            @block.sync
            def _(sp):
                sp.wait_ge(s.zero, 2)
                for src, dst in ((d.cw.rearrange("(c p) n -> p c n", p=P), t.cw[:]), (d.cb, t.cb[:]),
                                 (d.blk, t.blk[:]), (d.kvb.unsqueeze(1), t.kvb[:]),
                                 (d.kv2l.unsqueeze(1).to_broadcast([32, 8, 16]), t.kvr[:]), (d.l2oT.unsqueeze(1).to_broadcast([32, 8, 16]), t.lor[:]),
                                 (d.q2lb.partition_broadcast(P), t.qlb[:]), (d.kvb.partition_broadcast(P), t.klb[:]), (d.l2ob.partition_broadcast(P), t.lob[:]),
                                 (d.cprojT.rearrange("(f p) n -> p f n", p=P), wo[:]), (d.cprojb.partition_broadcast(P), m.bo[:]),
                                 (d.cos, m.cos[:]), (d.sin, m.sin[:]), (d.causal, m.causal[:])):
                    sp.dma_start(dst, src).then_inc(s.w_in, 16)
                for j in range(8):
                    sp.dma_start(t.bd[16 * j:16 * j + 16, 0, j, :], d.q2lT).then_inc(s.w_in, 16)
                    sp.dma_start(t.bd[16 * j:16 * j + 16, 1, j, :], d.kv2lT).then_inc(s.w_in, 16)
                for j in range(4):
                    sp.dma_start(m.wqk[32 * j:32 * j + 32, 32 * j:32 * j + 32], d.wqkT).then_inc(s.w_in, 16)
                    sp.dma_start(m.wqkb[32 * j:32 * j + 32, :], d.wqkb.unsqueeze(1)).then_inc(s.w_in, 16)
            n_in = 16 * (14 + 16 + 8)

            @block.vector
            def _(dve):
                nc.vector.memset(t.bd[:], 0.0).then_inc(s.zero, 1)
                nc.vector.memset(m.wqk[:], 0.0).then_inc(s.zero, 1)
                dve.wait_ge(s.w_in, n_in)
                nc.vector.tensor_copy(t.cbb[:], t.cb[:].unsqueeze(2).to_broadcast([P, 6, P])).then_inc(s.cbb, 1)
                nc.vector.tensor_copy(t.kvbb[:], t.kvb[:].to_broadcast([32, P])).then_inc(s.cbb, 1)
                dve.wait_ge(s.m2_ps, 1)
                nc.vector.tensor_tensor(t.bdv[:], kit.psum(0)[:, 0:P], t.blk[:], ALU.mult).then_inc(s.bdv, 1)
                for f in range(FC):
                    dve.wait_ge(s.out_ps, f + 1)
                    nc.vector.tensor_copy(w[:, f, 0:512], kit.psum(3 * f + 1)).then_inc(s.out, 1)
                    nc.vector.tensor_copy(w[:, f, 512:1024], kit.psum(3 * f + 2)).then_inc(s.out, 1)
                    nc.vector.tensor_copy(w[:, f, 1024:1280], kit.psum(3 * f + 3)[:, 0:256]).then_inc(s.out, 1)
                dve.wait_ge(s.out_ps, FC + 1)
                nc.vector.tensor_tensor(m.b[:, 0:512].rearrange("p (h l) -> p h l", l=32), kit.psum(1).rearrange("p (h l) -> p h l", l=32),
                                        t.qlb[:].unsqueeze(1).to_broadcast([P, 16, 32]), ALU.add).then_inc(s.ready, 1)
                nc.vector.tensor_tensor(m.b[:, 512:1024].rearrange("p (h l) -> p h l", l=32), kit.psum(2).rearrange("p (h l) -> p h l", l=32),
                                        t.klb[:].unsqueeze(1).to_broadcast([P, 16, 32]), ALU.add).then_inc(s.ready, 1)
                nc.vector.tensor_tensor(m.b[:, 1024:1280].rearrange("p (h l) -> p h l", l=16), kit.psum(3)[:, 0:256].rearrange("p (h l) -> p h l", l=16),
                                        t.lob[:].unsqueeze(1).to_broadcast([P, 16, 16]), ALU.add).then_inc(s.ready, 1)
                dve.wait_ge(s.ready, 3)

            @block.tensor
            def _(pe):
                pe.wait_ge(s.w_in, n_in)
                nc.tensor.matmul(kit.psum(0)[:, 0:P], t.kvr[:].rearrange("p a b -> p (a b)"), t.lor[:].rearrange("p a b -> p (a b)"),
                                 start=True, stop=True).then_inc(s.m2_ps, 1)
                pe.wait_ge(s.bdv, 1)

                def rows(c):
                    return t.bdv[:] if c >= 4 else t.bd[:, c // 2].rearrange("p a b -> p (a b)")

                for f in range(FC):
                    for c in range(6):
                        wide = P if c >= 4 else 256
                        mm = nc.tensor.matmul(kit.psum(3 * f + 1 + c // 2)[:, (c % 2) * wide:(c % 2 + 1) * wide], t.cw[:, c, f * P:(f + 1) * P], rows(c),
                                              start=True, stop=True)
                    mm.then_inc(s.out_ps, 1)
                pe.wait_ge(s.out, 3)
                pe.wait_ge(s.cbb, 2)
                for c in range(6):
                    wide = P if c >= 4 else 256
                    out = kit.psum(1 + c // 2)[:, (c % 2) * wide:(c % 2 + 1) * wide]
                    mm = nc.tensor.matmul(out, t.cbb[:, c, :], rows(c), start=True, stop=(c < 4))
                    if c >= 4:
                        mm = nc.tensor.matmul(out, t.kvbb[:], t.lor[:].rearrange("p a b -> p (a b)"), start=False, stop=True)
                mm.then_inc(s.out_ps, 1)


def self_attention(kit, stage, rotary):
    nc, d = kit.nc, kit.dram
    X = kit.X
    WIDE = 1280 if rotary else 768
    with kit.stage() as st:
        m = kit.buffers(
            st, w=([P, FC, WIDE], F32), wo=([P, FC, D], F32), xl=([P, 2, D], F32), xlT=([P, 2, FC, P], F32),
            qk=([P, 2, 32, 32], F32), v=([P, 2, D], F32), qT=([P, 512], F32), kT=([P, 512], F32), score=([P, H, S], F32), top=([P, H], F32),
            prob=([P, H, S], F32), mass=([P, H], F32), rmass=([P, H], F32), spread=([P, H, P], F32), y=([P, D], F32), yT=([P, FC, P], F32))
        if rotary:
            r = kit.buffers(st, b=([P, WIDE], F32), bo=([P, D], F32), cos=([P, 16], F32), sin=([P, 2, 16], F32), causal=([P, S], F32), wqk=([P, P], F32),
                            wqkb=([P, 1], F32), lat=([P, 32, 32], F32), turn=([P, 32, 32], F32), qrT=([P, 512], F32))
            rotary_weights(kit, r, m.w, m.wo, stage)
        else:
            r = kit.buffers(st, raw=([P, 512], F32), sq=([P, 512], F32), ss=([P, 32], F32), rss=([P, 2, 32], F32), gq=([P, 2, 16], F32), gain=([P, 16], F32))
        norm = Norm(kit, stage, st)
        s = kit.sems(stage, "w_in zero zero_qk gain xl xlT_ps xlT qk_ps raw raw_q sq v ss scaled rss qk_n qk lat turned cosed qT_ps qT kT qrT_ps qrT s_ps cut_act cut_dve masked "
                     "top shift p mass rmass prob spread y_ps y yT_ps yT o_ps x_add passed")
        heads = lambda ap: ap.rearrange("p (h e) -> p h e", h=H)

        with nc.Block() as block:
            @block.sync
            def _(sp):
                if not rotary:
                    for i, w in enumerate((d.WqT, d.WkT0, d.WvT)):
                        sp.dma_start(m.w[:, :, i * D:(i + 1) * D], w.rearrange("(f p) n -> p f n", p=P)).then_inc(s.w_in, 16)
                    sp.dma_start(m.wo[:], d.WoT.rearrange("(f p) n -> p f n", p=P)).then_inc(s.w_in, 16)
                    sp.dma_start(r.gq[:, 0, :], d.qn_w.partition_broadcast(P)).then_inc(s.w_in, 16)
                    sp.dma_start(r.gq[:, 1, :], d.kn_w.partition_broadcast(P)).then_inc(s.w_in, 16)
            n_w = 0 if rotary else 96

            @block.vector
            def _(dve):
                nc.vector.memset(m.spread[:], 0.0).then_inc(s.zero, 1)
                if not rotary:
                    nc.vector.memset(m.qk[:], 0.0).then_inc(s.zero_qk, 1)
                    dve.wait_ge(s.w_in, n_w)
                    nc.vector.scalar_tensor_tensor(r.gain[:], r.gq[:, 0, :], 16 ** -0.5, r.gq[:, 1, :], ALU.mult, ALU.mult).then_inc(s.gain, 1)
                    dve.wait_ge(s.gain, 1)
                    dve.wait_ge(s.zero_qk, 1)
                dve.wait_ge(s.zero, 1)
                norm.vector_part(dve)

                def front(n, k):
                    norm.rows(m.xl[:, k, :], n).then_inc(s.xl, 1)
                    if rotary:
                        dve.wait_ge(s.qk_ps, n + 1)
                        nc.vector.tensor_tensor(r.lat[:].rearrange("p h l -> p (h l)"), kit.bank[1][:].rearrange("p a t -> p (a t)"), r.b[:, 0:1024], ALU.add).then_inc(s.lat, 1)
                        nc.vector.tensor_tensor(m.v[:, k, :], kit.psum(1)[:, 0:D], r.b[:, 1024:1280], ALU.add).then_inc(s.v, 1)
                        dve.wait_ge(s.lat, n + 1)
                        nc.vector.tensor_tensor(m.qk[:, k].rearrange("p h (i e) -> p h i e", e=2), r.lat[:].rearrange("p h (i e) -> p h i e", e=2),
                                                r.cos[:].unsqueeze(1).unsqueeze(3).to_broadcast([P, 32, 16, 2]), ALU.mult).then_inc(s.cosed, 1)
                        dve.wait_ge(s.cosed, n + 1)
                        dve.wait_ge(s.turned, n * 2 + 2)
                        nc.vector.tensor_tensor(m.qk[:, k], m.qk[:, k], r.turn[:], ALU.add).then_inc(s.qk, 1)
                    else:
                        dve.wait_ge(s.sq, n + 1)
                        nc.vector.tensor_reduce(r.ss[:], r.sq[:].rearrange("p (h e) -> p h e", e=16), AX.X, ALU.add).then_inc(s.ss, 1)
                        dve.wait_ge(s.raw_q, n + 1)
                        dve.wait_ge(s.rss, n + 1)
                        nc.vector.tensor_tensor(m.qk[:, k, :, 0:16], r.raw[:].rearrange("p (h e) -> p h e", e=16),
                                                r.rss[:, k, :].unsqueeze(2).to_broadcast([P, 32, 16]), ALU.mult).then_inc(s.qk_n, 1)
                        dve.wait_ge(s.qk_n, n + 1)
                        nc.vector.tensor_tensor(m.qk[:, k, 0:H, 0:16], m.qk[:, k, 0:H, 0:16], r.gain[:].unsqueeze(1).to_broadcast([P, H, 16]), ALU.mult).then_inc(s.qk, 1)

                def back(n, k):
                    dve.wait_ge(s.qT_ps, n * 2 + 2)
                    nc.vector.tensor_copy(m.kT[:], kit.psum(3)).then_inc(s.kT, 1)
                    if rotary:
                        dve.wait_ge(s.qrT_ps, n + 1)
                        nc.vector.tensor_scalar(m.qT[:], kit.psum(2), r.wqkb[:], 32 ** -0.5, ALU.add, ALU.mult).then_inc(s.qT, 1)
                    dve.wait_ge(s.s_ps, n + 1)
                    for j in range(2, BT):
                        rows = slice(j * S, (j + 1) * S)
                        for i in range(2):
                            nc.vector.tensor_copy(m.score[rows].rearrange("p (c r) k -> p r c k", r=4)[:, 2 * i:2 * i + 2],
                                                  kit.bank[2 + i][rows].rearrange("p r (c k) -> p r c k", c=4)[:, :, :, rows]).then_inc(s.cut_dve, 1)
                    if rotary:
                        dve.wait_ge(s.masked, n + 1)
                    else:
                        dve.wait_ge(s.cut_act, (n + 1) * 4)
                        dve.wait_ge(s.cut_dve, (n + 1) * 4)
                    nc.vector.tensor_reduce(m.top[:], m.score[:], AX.X, ALU.max).then_inc(s.top, 1)
                    dve.wait_ge(s.top, n + 1)
                    nc.vector.tensor_tensor(m.score[:], m.score[:], m.top[:].unsqueeze(2).to_broadcast([P, H, S]), ALU.subtract).then_inc(s.shift, 1)
                    dve.wait_ge(s.p, n + 1)
                    nc.vector.tensor_reduce(m.mass[:], m.prob[:], AX.X, ALU.add).then_inc(s.mass, 1)
                    dve.wait_ge(s.mass, n + 1)
                    nc.vector.reciprocal(m.rmass[:], m.mass[:]).then_inc(s.rmass, 1)
                    dve.wait_ge(s.rmass, n + 1)
                    nc.vector.tensor_tensor(m.prob[:], m.prob[:], m.rmass[:].unsqueeze(2).to_broadcast([P, H, S]), ALU.mult).then_inc(s.prob, 1)
                    dve.wait_ge(s.prob, n + 1)
                    dve.wait_ge(s.y_ps, n)
                    for j in range(BT):
                        rows = slice(j * S, (j + 1) * S)
                        nc.vector.transpose(m.spread[rows, :, rows], m.prob[rows]).then_inc(s.spread, 1)
                    dve.wait_ge(s.o_ps, n + 1)
                    nc.vector.tensor_tensor(X[:, n, :], X[:, n, :], kit.psum(0)[:, D:2 * D], ALU.add).then_inc(s.x_add, 1)

                front(0, 0)
                with dve.Fori(0, NT // 2 - 1) as u:
                    for k in range(2):
                        front(u * 2 + (k + 1), 1 - k)
                        back(u * 2 + k, k)
                front(NT - 1, 1)
                back(NT - 2, 0)
                back(NT - 1, 1)
                if rotary:
                    dve.wait_ge(s.x_add, NT)
                    nc.vector.tensor_tensor(X[:], X[:], r.bo[:].unsqueeze(1).to_broadcast([P, NT, D]), ALU.add).then_inc(s.x_add, 1)
                    dve.wait_ge(s.x_add, NT + 1)

            @block.gpsimd
            def _(pool):
                norm.pool_part(pool)

                def front(n, k):
                    if rotary:
                        pool.wait_ge(s.lat, n + 1)
                        pool.wait_ge(s.qk, n)
                        lat, turn = (x[:].rearrange("p h (i e) -> p h i e", e=2) for x in (r.lat, r.turn))
                        for e in range(2):
                            nc.gpsimd.tensor_tensor(turn[:, :, :, e], lat[:, :, :, 1 - e], r.sin[:, e, :].unsqueeze(1).to_broadcast([P, 32, 16]), ALU.mult).then_inc(s.turned, 1)
                    else:
                        hold(pool, s.ss, n + 1, s.passed)
                        inv_root(nc, pool, kit.neg_half[:, 0:32], r.rss[:, k, :], r.ss[:], 1.0 / 16, float(np.finfo(np.float32).eps), ALU.add, s.scaled, n + 1, s.rss)

                def back(n, k):
                    if rotary:
                        pool.wait_ge(s.cut_act, (n + 1) * 4)
                        pool.wait_ge(s.cut_dve, (n + 1) * 4)
                        nc.gpsimd.tensor_tensor(m.score[:], m.score[:], r.causal[:].unsqueeze(1).to_broadcast([P, H, S]), ALU.add).then_inc(s.masked, 1)

                front(0, 0)
                with pool.Fori(0, NT // 2 - 1) as u:
                    for k in range(2):
                        front(u * 2 + (k + 1), 1 - k)
                        back(u * 2 + k, k)
                front(NT - 1, 1)
                back(NT - 2, 0)
                back(NT - 1, 1)

            @block.scalar
            def _(act):
                def front(n, k):
                    act.wait_ge(s.xlT_ps, n + 1)
                    nc.scalar.copy(m.xlT[:, k].rearrange("p f t -> p (f t)"), kit.psum(0)[:, 0:D]).then_inc(s.xlT, 1)
                    if not rotary:
                        act.wait_ge(s.qk_ps, n + 1)
                        act.wait_ge(s.qk, n)
                        nc.scalar.activation(r.sq[:], kit.psum(2), ACT.Square).then_inc(s.sq, 1)
                        nc.scalar.copy(r.raw[:], kit.psum(2)).then_inc(s.raw_q, 1)
                        nc.scalar.copy(m.v[:, k, :], kit.psum(1)[:, 0:D]).then_inc(s.v, 1)

                def back(n, k):
                    act.wait_ge(s.qT_ps, n * 2 + 1)
                    if rotary:
                        nc.scalar.copy(r.qrT[:], kit.psum(2)).then_inc(s.qrT, 1)
                    else:
                        nc.scalar.copy(m.qT[:], kit.psum(2)).then_inc(s.qT, 1)
                    act.wait_ge(s.s_ps, n + 1)
                    for j in range(2):
                        rows = slice(j * S, (j + 1) * S)
                        for i in range(2):
                            nc.scalar.copy(m.score[rows].rearrange("p (c r) k -> p r c k", r=4)[:, 2 * i:2 * i + 2],
                                           kit.bank[2 + i][rows].rearrange("p r (c k) -> p r c k", c=4)[:, :, :, rows]).then_inc(s.cut_act, 1)
                    act.wait_ge(s.shift, n + 1)
                    nc.scalar.activation(m.prob[:].rearrange("p h k -> p (h k)"), m.score[:].rearrange("p h k -> p (h k)"), ACT.Exp).then_inc(s.p, 1)
                    act.wait_ge(s.y_ps, n + 1)
                    nc.scalar.copy(m.y[:], kit.psum(1)[:, D:2 * D]).then_inc(s.y, 1)
                    act.wait_ge(s.yT_ps, n + 1)
                    nc.scalar.copy(m.yT[:].rearrange("p f t -> p (f t)"), kit.psum(0)[:, 0:D]).then_inc(s.yT, 1)

                front(0, 0)
                with act.Fori(0, NT // 2 - 1) as u:
                    for k in range(2):
                        front(u * 2 + (k + 1), 1 - k)
                        back(u * 2 + k, k)
                front(NT - 1, 1)
                back(NT - 2, 0)
                back(NT - 1, 1)

            @block.tensor
            def _(pe):
                if not rotary:
                    pe.wait_ge(s.w_in, n_w)

                def front(n, k):
                    pe.wait_ge(s.xl, n + 1)
                    pe.wait_ge(s.x_add, prev(n))
                    for f in range(FC):
                        mm = nc.tensor.transpose(kit.psum(0)[:, f * P:(f + 1) * P], m.xl[:, k, f * P:(f + 1) * P], kit.ident[:])
                    mm.then_inc(s.xlT_ps, 1)
                    pe.wait_ge(s.xlT, n + 1)
                    pe.wait_ge(s.y, prev(n))
                    parts = ((2, 0, 512), (3, 512, 512), (1, 1024, 256)) if rotary else ((2, 0, 512), (1, 512, 256))
                    for bank, at, wide in parts:
                        for f in range(FC):
                            mm = nc.tensor.matmul(kit.psum(bank)[:, 0:wide], m.xlT[:, k, f, :], m.w[:, f, at:at + wide], start=(f == 0), stop=(f == FC - 1))
                    mm.then_inc(s.qk_ps, 1)

                def back(n, k):
                    pe.wait_ge(s.qk, n + 1)
                    pe.wait_ge(s.v, ahead(n))
                    for i in range(2):
                        for c in range(HC):
                            mm = nc.tensor.transpose(kit.psum(2 + i)[:, c * P:(c + 1) * P], m.qk[:, k, (i * HC + c) * BT:(i * HC + c + 1) * BT, :].rearrange("p h l -> p (h l)"), kit.ident[:])
                        mm.then_inc(s.qT_ps, 1)
                    if rotary:
                        pe.wait_ge(s.qrT, n + 1)
                        nc.tensor.matmul(kit.psum(2), r.wqk[:], r.qrT[:], start=True, stop=True).then_inc(s.qrT_ps, 1)
                    pe.wait_ge(s.qT, n + 1)
                    pe.wait_ge(s.kT, n + 1)
                    for c in range(HC):
                        for j in range(BT):
                            mm = nc.tensor.matmul(kit.psum(4 + j)[:, c * P:(c + 1) * P], m.qT[32 * j:32 * j + 32, c * P:(c + 1) * P],
                                                  m.kT[32 * j:32 * j + 32, c * P:(c + 1) * P], start=True, stop=True)
                    mm.then_inc(s.s_ps, 1)
                    pe.wait_ge(s.spread, (n + 1) * BT)
                    for h in range(H):
                        mm = nc.tensor.matmul(kit.psum(1)[:, D + h * 16:D + (h + 1) * 16], m.spread[:, h, :], m.v[:, k, h * 16:(h + 1) * 16], start=True, stop=True)
                    mm.then_inc(s.y_ps, 1)
                    pe.wait_ge(s.y, n + 1)
                    for f in range(FC):
                        mm = nc.tensor.transpose(kit.psum(0)[:, f * P:(f + 1) * P], m.y[:, f * P:(f + 1) * P], kit.ident[:])
                    mm.then_inc(s.yT_ps, 1)
                    pe.wait_ge(s.yT, n + 1)
                    for f in range(FC):
                        mm = nc.tensor.matmul(kit.psum(0)[:, D:2 * D], m.yT[:, f, :], m.wo[:, f, :], start=(f == 0), stop=(f == FC - 1))
                    mm.then_inc(s.o_ps, 1)

                def prev(n):
                    return 0 if isinstance(n, int) and n == 0 else n + (-1)

                def ahead(n):
                    return NT if isinstance(n, int) and n == NT - 1 else n + 2

                front(0, 0)
                with pe.Fori(0, NT // 2 - 1) as u:
                    for k in range(2):
                        front(u * 2 + (k + 1), 1 - k)
                        back(u * 2 + k, k)
                front(NT - 1, 1)
                back(NT - 2, 0)
                back(NT - 1, 1)


def tanh_map(kit):
    nc, d = kit.nc, kit.dram
    X = kit.X
    with kit.stage() as st:
        norm = Norm(kit, "map", st)
        m = kit.buffers(st, wT=([P, FC, D], F32), a1T=([P, FC, D], F32), a2=([P, FC, D], F32), a12=([P, FC, D], F32), w=([P, FC, D], F32), b=([P, D], F32),
                        xl=([P, 2, D], F32), xlT=([P, 2, FC, P], F32), h=([P, 2, D], F32), y=([P, 2, D], F32), out=([P, 2, D], F32))
        s = kit.sems("map", "w_in a12_ps a12 w_ps w xl xlT_ps xlT h_ps h y out")
        stored = kit.pair("map", "stored")
        with nc.Block() as block:
            @block.sync
            def _(sp):
                for sb, src in ((m.wT, d.weightT), (m.a1T, d.aux1T), (m.a2, d.aux2)):
                    sp.dma_start(sb[:], src.rearrange("(f p) n -> p f n", p=P)).then_inc(s.w_in, 16)
                sp.dma_start(m.b[:], d.map_b.partition_broadcast(P)).then_inc(s.w_in, 16)
                with sp.Fori(0, NT // 2) as u:
                    for k in range(2):
                        n = u * 2 + k
                        sp.wait_ge(s.out, n + 1)
                        sp.dma_start(d.out_tiles[n], m.out[:, k, :]).then_inc(stored[k], 16)
                for k in range(2):
                    sp.wait_ge(stored[k], 16 * (NT // 2 + 1))

            @block.vector
            def _(dve):
                for k in range(2):
                    dve.sem_inc(stored[k], 16)
                dve.wait_ge(s.a12_ps, 1)
                nc.vector.tensor_copy(m.a12[:], kit.psum(0).rearrange("p (f n) -> p f n", f=FC)).then_inc(s.a12, 1)
                dve.wait_ge(s.w_ps, 1)
                nc.vector.tensor_copy(m.w[:], kit.psum(1).rearrange("p (f n) -> p f n", f=FC)).then_inc(s.w, 1)
                norm.vector_part(dve)
                dve.wait_ge(s.w_in, 64)
                norm.rows(m.xl[:, 0, :], 0).then_inc(s.xl, 1)

                def tile(n, k, more):
                    if more:
                        dve.wait_ge(s.xlT_ps, n)
                        norm.rows(m.xl[:, 1 - k, :], n + 1).then_inc(s.xl, 1)
                    dve.wait_ge(s.h_ps, n + 1)
                    nc.vector.tensor_tensor(m.h[:, k, :], kit.psum(4 + k)[:, 0:D], m.b[:], ALU.add).then_inc(s.h, 1)
                    dve.wait_ge(s.y, n + 1)
                    dve.wait_ge(stored[k], stores(n, k))
                    nc.vector.tensor_tensor(m.out[:, k, :], X[:, n, :], m.y[:, k, :], ALU.add).then_inc(s.out, 1)

                def stores(n, k):
                    return (n + (2 - k)) * 8

                with dve.Fori(0, NT // 2 - 1) as u:
                    for k in range(2):
                        tile(u * 2 + k, k, True)
                tile(NT - 2, 0, True)
                tile(NT - 1, 1, False)

            @block.gpsimd
            def _(pool):
                norm.pool_part(pool)

            @block.scalar
            def _(act):
                with act.Fori(0, NT // 2) as u:
                    for k in range(2):
                        n = u * 2 + k
                        act.wait_ge(s.xlT_ps, n + 1)
                        nc.scalar.copy(m.xlT[:, k].rearrange("p f t -> p (f t)"), kit.psum(2 + k)[:, 0:D]).then_inc(s.xlT, 1)
                        act.wait_ge(s.h, n + 1)
                        nc.scalar.activation(m.y[:, k, :], m.h[:, k, :], ACT.Tanh).then_inc(s.y, 1)

            @block.tensor
            def _(pe):
                pe.wait_ge(s.w_in, 64)
                for lhsT, rhs, bank, done, ready in ((m.a1T, m.a2, 0, s.a12_ps, None), (m.wT, m.a12, 1, s.w_ps, s.a12)):
                    if ready is not None:
                        pe.wait_ge(ready, 1)
                    for i in range(FC):
                        for f in range(FC):
                            mm = nc.tensor.matmul(kit.psum(bank)[:, i * D:(i + 1) * D], lhsT[:, f, i * P:(i + 1) * P], rhs[:, f, :], start=(f == 0), stop=(f == FC - 1))
                    mm.then_inc(done, 1)
                pe.wait_ge(s.w, 1)
                with pe.Fori(0, NT // 2) as u:
                    for k in range(2):
                        n = u * 2 + k
                        pe.wait_ge(s.xl, n + 1)
                        for f in range(FC):
                            mm = nc.tensor.transpose(kit.psum(2 + k)[:, f * P:(f + 1) * P], m.xl[:, k, f * P:(f + 1) * P], kit.ident[:])
                        mm.then_inc(s.xlT_ps, 1)
                        pe.wait_ge(s.xlT, n + 1)
                        for f in range(FC):
                            mm = nc.tensor.matmul(kit.psum(4 + k)[:, 0:D], m.xlT[:, k, f, :], m.w[:, f, :], start=(f == 0), stop=(f == FC - 1))
                        mm.then_inc(s.h_ps, 1)


E_, TOPK, CAP = 64, 8, 128
I_, IS = 128, 512
ROUTED = D + E_
GS = 512


def mixture(kit):
    nc, d = kit.nc, kit.dram
    X = kit.X
    with kit.stage() as st:
        kept = kit.buffers(st, token=([CAP, E_], U32), address=([P, NT, TOPK], U32))
        route(kit, kept)
        experts(kit, kept)


def route(kit, kept):
    nc, d = kit.nc, kit.dram
    X = kit.X
    with kit.stage() as st:
        norm = Norm(kit, "moe", st)
        m = kit.buffers(
            st, wg=([P, FC, E_ + 1], F32), sgu=([P, FC, 2 * IS], F32), sd=([P, IS // P, D], F32), before=([P, P], F32), ones=([P, P], F32),
            rank=([P, NT], F32), first=([P, E_], F32), routed=([P, 2, ROUTED], F32), xlT=([P, 2, FC, P], F32), xlT_all=([P, FC, B * S], F32),
            logit=([P, E_ + 1], F32), best=([P, TOPK], F32), nbest=([P, 1], F32), rest=([P, E_], F32), chosen=([P, 2, E_], F32), count=([P, 2, E_], F32),
            gate=([P, E_], F32), mass=([P, 1], F32), rmass=([P, 1], F32), keep=([P, E_], F32), place=([P, E_], F32), key=([P, E_], F32), spot=([P, TOPK], F32),
            keyT=([E_, B * S], F32), order=([E_, CAP], F32), token=([CAP, E_], F32), sgate=([P, NT], F32), up=([P, 2, GS], F32), hid=([P, 2, IS // P, GS], F32))
        s = kit.sems("moe", "w_in c_set xl xlT_ps xlT xlT_kept lg_ps logit best nbest rest chosen e mass rmass w place_ps keep placed place spot address key keyT_ps keyT "
                     "count sgate_e sgate1 sgate order struck order_ps tok1 tok su_ps silu hid so_ps x_add passed passed_pe")
        stored = kit.pair("moe", "stored")
        with nc.Block() as block:
            @block.sync
            def _(sp):
                for sb, src in ((m.wg[:], d.gates_w), (m.sgu[:], d.shared_gu), (m.sd[:], d.shared_down)):
                    sp.dma_start(sb, src.rearrange("(f p) n -> p f n", p=P)).then_inc(s.w_in, 16)
                for sb, src in ((m.before, d.before), (m.rank, d.rank), (m.first, d.first)):
                    sp.dma_start(sb[:], src).then_inc(s.w_in, 16)
                with sp.Fori(0, NT // 2) as u:
                    for k in range(2):
                        n = u * 2 + k
                        sp.wait_ge(s.w, n + 1)
                        sp.dma_start(d.routed_tiles[n], m.routed[:, k, :]).then_inc(stored[k], 16)
                for k in range(2):
                    sp.wait_ge(stored[k], 16 * (NT // 2 + 1))

            @block.vector
            def _(dve):
                for k in range(2):
                    dve.sem_inc(stored[k], 16)
                nc.vector.memset(m.ones[:], 1.0).then_inc(s.c_set, 1)
                nc.vector.memset(m.count[:], 0.0).then_inc(s.c_set, 1)
                norm.vector_part(dve)
                dve.wait_ge(s.w_in, 96)
                dve.wait_ge(s.c_set, 2)

                def tile(n, u, k):
                    dve.wait_ge(stored[k], u * 16 + 16)
                    norm.rows(m.routed[:, k, 0:D], n).then_inc(s.xl, 1)
                    dve.wait_ge(s.lg_ps, n + 1)
                    nc.vector.tensor_copy(m.logit[:], kit.psum(1)[:, 0:E_ + 1]).then_inc(s.logit, 1)
                    hold(dve, s.logit, n + 1, s.passed)
                    nc.vector.max(m.best[:], m.logit[:, 0:E_]).then_inc(s.best, 1)
                    hold(dve, s.best, n + 1, s.passed)
                    nc.vector.match_replace(m.rest[:], m.best[:], m.logit[:, 0:E_], -3.0e38).then_inc(s.rest, 1)
                    nc.vector.tensor_scalar(m.nbest[:], m.best[:, 0:1], -1.0, None, ALU.mult).then_inc(s.nbest, 1)
                    dve.wait_ge(s.rest, n + 1)
                    nc.vector.tensor_tensor(m.chosen[:, k, :], m.rest[:], m.logit[:, 0:E_], ALU.not_equal).then_inc(s.chosen, 1)
                    dve.wait_ge(s.e, n + 1)
                    dve.wait_ge(s.chosen, n + 1)
                    nc.vector.scalar_tensor_tensor(m.gate[:], m.gate[:], 1.0, m.chosen[:, k, :], ALU.mult, ALU.mult, accum_out=m.mass[:]).then_inc(s.mass, 1)
                    dve.wait_ge(s.mass, n + 1)
                    nc.vector.reciprocal(m.rmass[:], m.mass[:]).then_inc(s.rmass, 1)
                    dve.wait_ge(s.rmass, n + 1)
                    nc.vector.tensor_scalar(m.routed[:, k, D:ROUTED], m.gate[:], m.rmass[:], None, ALU.mult).then_inc(s.w, 1)
                    dve.wait_ge(s.place_ps, n + 1)
                    nc.vector.scalar_tensor_tensor(m.keep[:], kit.psum(2)[:, 0:E_], float(CAP), m.chosen[:, k, :], ALU.is_lt, ALU.mult).then_inc(s.keep, 1)
                    nc.vector.tensor_tensor(m.place[:], kit.psum(2)[:, 0:E_], m.first[:], ALU.add).then_inc(s.placed, 1)
                    nc.vector.tensor_tensor(m.count[:, 1 - k, :], m.count[:, k, :], m.chosen[:, k, :], ALU.add).then_inc(s.count, 1)
                    dve.wait_ge(s.keep, n + 1)
                    dve.wait_ge(s.placed, n + 1)
                    nc.vector.tensor_tensor(m.place[:], m.place[:], m.keep[:], ALU.mult).then_inc(s.place, 1)
                    dve.wait_ge(s.keyT_ps, n)
                    nc.vector.tensor_scalar(m.key[:], m.keep[:], m.rank[:, bass.ds(n, 1)], None, ALU.mult).then_inc(s.key, 1)
                    hold(dve, s.place, n + 1, s.passed)
                    nc.vector.max(m.spot[:], m.place[:]).then_inc(s.spot, 1)
                    dve.wait_ge(s.spot, n + 1)
                    nc.vector.tensor_copy(kept.address[:, n, :], m.spot[:]).then_inc(s.address, 1)

                with dve.Fori(0, NT // 2) as u:
                    for k in range(2):
                        tile(u * 2 + k, u, k)
                dve.wait_ge(s.sgate_e, NT)
                nc.vector.tensor_scalar(m.sgate[:], m.sgate[:], 1.0, None, ALU.add).then_inc(s.sgate1, 1)
                dve.wait_ge(s.sgate1, 1)
                nc.vector.reciprocal(m.sgate[:], m.sgate[:]).then_inc(s.sgate, 1)
                dve.wait_ge(s.keyT, NT)
                rounds = CAP // 8
                groups = B * S // GS
                for g in range(groups):
                    for i in range(IS // P):
                        r = g * (rounds // groups) + i
                        if r > 0:
                            dve.wait_ge(s.struck, r)
                        nc.vector.max(m.order[:, 8 * r:8 * r + 8], m.keyT[:]).then_inc(s.order, 1)
                        n = g * (IS // P) + i
                        dve.wait_ge(s.silu, n + 1)
                        dve.wait_ge(s.su_ps, 2 * n + 2)
                        if g >= 2:
                            dve.wait_ge(s.so_ps, 4 * (g - 1))
                        nc.vector.tensor_tensor(m.hid[:, g % 2, i, :], m.up[:, n % 2, :], kit.psum(4 + n % 2), ALU.mult).then_inc(s.hid, 1)
                        dve.wait_ge(s.order, r + 1)
                        nc.vector.match_replace(m.keyT[:], m.order[:, 8 * r:8 * r + 8], m.keyT[:], 0.0).then_inc(s.struck, 1)
                    if g == 0:
                        dve.wait_ge(s.sgate, 1)
                    for i in range(GS // P):
                        n = g * (GS // P) + i
                        dve.wait_ge(s.so_ps, n + 1)
                        nc.vector.scalar_tensor_tensor(X[:, n, :], kit.psum(6 + n % 2)[:, 0:D], m.sgate[:, n:n + 1], X[:, n, :], ALU.mult, ALU.add).then_inc(s.x_add, 1)
                dve.wait_ge(s.order_ps, 1)
                nc.vector.tensor_scalar(m.token[:], kit.psum(0)[:, 0:E_], -1.0, float(B * S), ALU.mult, ALU.add).then_inc(s.tok1, 1)
                dve.wait_ge(s.tok1, 1)
                nc.vector.tensor_scalar(kept.token[:], m.token[:], float(B * S - 1), None, ALU.min).then_inc(s.tok, 1)
                dve.wait_ge(s.tok, 1)
                dve.wait_ge(s.address, NT)
                dve.wait_ge(s.x_add, NT)

            @block.gpsimd
            def _(pool):
                norm.pool_part(pool)
                with pool.Fori(0, NT // 2) as u:
                    for k in range(2):
                        n = u * 2 + k
                        pool.wait_ge(s.xlT, n + 1)
                        nc.gpsimd.tensor_copy(m.xlT_all[:, :, bass.ts(n, P)], m.xlT[:, k]).then_inc(s.xlT_kept, 1)

            @block.scalar
            def _(act):
                with act.Fori(0, NT // 2) as u:
                    for k in range(2):
                        n = u * 2 + k
                        act.wait_ge(s.xlT_ps, n + 1)
                        act.wait_ge(s.xlT_kept, u * 2)
                        nc.scalar.copy(m.xlT[:, k].rearrange("p f t -> p (f t)"), kit.psum(0)[:, 0:D]).then_inc(s.xlT, 1)
                        act.wait_ge(s.logit, n + 1)
                        nc.scalar.activation(m.sgate[:, bass.ds(n, 1)], m.logit[:, E_:E_ + 1], ACT.Exp, scale=-1.0).then_inc(s.sgate_e, 1)
                        act.wait_ge(s.nbest, n + 1)
                        nc.scalar.activation(m.gate[:], m.logit[:, 0:E_], ACT.Exp, bias=m.nbest[:]).then_inc(s.e, 1)
                        act.wait_ge(s.keyT_ps, n + 1)
                        nc.scalar.copy(m.keyT[:, bass.ts(n, P)], kit.psum(3)[0:E_, 0:P]).then_inc(s.keyT, 1)
                with act.Fori(0, B * S // GS * (IS // P) // 2) as u:
                    for k in range(2):
                        n = u * 2 + k
                        act.wait_ge(s.su_ps, n * 2 + 1)
                        act.wait_ge(s.hid, u * 2)
                        nc.scalar.activation(m.up[:, k, :], kit.psum(2 + k), ACT.Silu).then_inc(s.silu, 1)

            @block.tensor
            def _(pe):
                pe.wait_ge(s.w_in, 96)
                pe.wait_ge(s.c_set, 2)
                with pe.Fori(0, NT // 2) as u:
                    for k in range(2):
                        n = u * 2 + k
                        pe.wait_ge(s.xl, n + 1)
                        for f in range(FC):
                            mm = nc.tensor.transpose(kit.psum(0)[:, f * P:(f + 1) * P], m.routed[:, k, f * P:(f + 1) * P], kit.ident[:])
                        mm.then_inc(s.xlT_ps, 1)
                        pe.wait_ge(s.xlT, n + 1)
                        pe.wait_ge(s.logit, n)
                        for f in range(FC):
                            mm = nc.tensor.matmul(kit.psum(1)[:, 0:E_ + 1], m.xlT[:, k, f, :], m.wg[:, f, :], start=(f == 0), stop=(f == FC - 1))
                        mm.then_inc(s.lg_ps, 1)
                        pe.wait_ge(s.chosen, n + 1)
                        pe.wait_ge(s.count, n)
                        nc.tensor.matmul(kit.psum(2)[:, 0:E_], m.before[:], m.chosen[:, k, :], start=True, stop=False)
                        nc.tensor.matmul(kit.psum(2)[:, 0:E_], m.ones[:], m.count[:, k, :], start=False, stop=True).then_inc(s.place_ps, 1)
                        pe.wait_ge(s.keyT, n)
                        hold(pe, s.key, n + 1, s.passed_pe)
                        nc.tensor.transpose(kit.psum(3)[0:E_, 0:P], m.key[:], kit.ident[:]).then_inc(s.keyT_ps, 1)
                pe.wait_ge(s.keyT, NT)
                pe.wait_ge(s.xlT_kept, NT)
                with pe.Fori(0, B * S // GS // 2) as u:
                    for k in range(2):
                        g = u * 2 + k
                        for i in range(IS // P):
                            n = g * (IS // P) + i
                            pe.wait_ge(s.hid, g * (IS // P) + max(i - 1, 0))
                            for part, bank in ((0, 2 + i % 2), (1, 4 + i % 2)):
                                for f in range(FC):
                                    mm = nc.tensor.matmul(kit.psum(bank), m.sgu[:, f, part * IS + i * P:part * IS + (i + 1) * P], m.xlT_all[:, f, bass.ts(g, GS)],
                                                          start=(f == 0), stop=(f == FC - 1))
                                mm.then_inc(s.su_ps, 1)
                        pe.wait_ge(s.hid, g * (IS // P) + (IS // P))
                        for i in range(GS // P):
                            pe.wait_ge(s.x_add, g * (GS // P) + max(i - 1, 0))
                            for c in range(IS // P):
                                mm = nc.tensor.matmul(kit.psum(6 + i % 2)[:, 0:D], m.hid[:, k, c, i * P:(i + 1) * P], m.sd[:, c, :], start=(c == 0), stop=(c == IS // P - 1))
                            mm.then_inc(s.so_ps, 1)
                pe.wait_ge(s.order, CAP // 8)
                nc.tensor.transpose(kit.psum(0)[:, 0:E_], m.order[:], kit.ident[0:E_, 0:E_]).then_inc(s.order_ps, 1)


def experts(kit, kept):
    nc, d = kit.nc, kit.dram
    X = kit.X
    with kit.stage() as st:
        m = kit.buffers(
            st, index=([CAP, 2, 1], U32), rows=([CAP, 2, ROUTED], F32), rowsT=([P, 2, FC, CAP], F32), wgu=([P, 2, FC, 2 * I_], F32), wd=([I_, 2, D], F32),
            silu=([I_, 2, CAP], F32), hid=([I_, 2, CAP], F32), out=([CAP, 2, D], F32), zero=([2, D], F32),
            where=([P, 2, TOPK], U32), parts=([P, 2, TOPK, D], F32), total=([P, 2, D], F32))
        s = kit.sems("exp", "zero zero_out index where w_free rT_ps rT gu_ps silu hid y_ps out total x_add passed")
        w_in, rows_in, stored, parts_in = (kit.pair("exp", n) for n in ("w_in", "rows_in", "stored", "parts_in"))
        with nc.Block() as block:
            @block.sync
            def _(sp):
                sp.wait_ge(s.zero, 1)
                sp.dma_start(d.expert_rows[0:1, :], m.zero[0:1, :]).then_inc(s.zero_out, 16)
                with sp.Fori(0, E_ // 2) as u:
                    for k in range(2):
                        e = u * 2 + k
                        sp.wait_ge(s.w_free, e + 1)
                        sp.dma_start(m.wgu[:, k], d.expert_gu[e].rearrange("(f p) n -> p f n", p=P)).then_inc(w_in[k], 16)
                        sp.dma_start(m.wd[:, k, :], d.expert_down[e]).then_inc(w_in[k], 16)

            @block.gpsimd
            def _(pool):
                with pool.Fori(0, E_ // 2) as u:
                    for k in range(2):
                        e = u * 2 + k
                        pool.wait_ge(s.out, e)
                        nc.gpsimd.tensor_copy(m.index[:, k, :], kept.token[:, bass.ds(e, 1)]).then_inc(s.index, 1)
                        hold(pool, s.index, e + 1, s.passed)
                        nc.gpsimd.indirect_dma_start(m.rows[:, k, :], None, d.routed, bass.IndirectOffsetOnAxis(m.index[:, k, :], 0)).then_inc(rows_in[k], 16)
                for k in range(2):
                    pool.wait_ge(stored[k], 16 * (E_ // 2 + 1))
                pool.wait_ge(s.zero_out, 16)
                with pool.Fori(0, NT // 2) as u:
                    for k in range(2):
                        n = u * 2 + k
                        pool.wait_ge(s.total, n)
                        nc.gpsimd.tensor_copy(m.where[:, k, :], kept.address[:, n, :]).then_inc(s.where, 1)
                        hold(pool, s.where, n + 1, s.passed)
                        for c in range(TOPK):
                            nc.gpsimd.indirect_dma_start(m.parts[:, k, c, :], None, d.expert_rows, bass.IndirectOffsetOnAxis(m.where[:, k, c:c + 1], 0)).then_inc(parts_in[k], 16)

            @block.vector
            def _(dve):
                nc.vector.memset(m.zero[:], 0.0).then_inc(s.zero, 1)
                for k in range(2):
                    dve.sem_inc(stored[k], 16)
                dve.sem_inc(s.w_free, 2)
                dve.sem_inc(s.out, 1)
                dve.sem_inc(s.total, 1)

                def gated(e, k):
                    dve.wait_ge(s.silu, e + 1)
                    nc.vector.tensor_tensor(m.hid[:, k, :], m.silu[:, k, :], kit.psum(2 + k)[:, CAP:2 * CAP], ALU.mult).then_inc(s.hid, 1)

                def weighted(e, k, u):
                    dve.wait_ge(s.y_ps, e + 1)
                    dve.sem_inc(s.w_free, 1)
                    dve.wait_ge(stored[k], u * 16 + 16)
                    nc.vector.tensor_scalar(m.out[:, k, :], kit.psum(4 + k)[:, 0:D], m.rows[:, k, bass.ds(e + D, 1)], None, ALU.mult).then_inc(s.out, 1)

                gated(0, 0)
                with dve.Fori(0, E_ // 2 - 1) as u:
                    for k in range(2):
                        gated(u * 2 + (k + 1), 1 - k)
                        weighted(u * 2 + k, k, u)
                gated(E_ - 1, 1)
                weighted(E_ - 2, 0, E_ // 2 - 1)
                weighted(E_ - 1, 1, E_ // 2 - 1)
                with dve.Fori(0, NT // 2) as u:
                    for k in range(2):
                        n = u * 2 + k
                        dve.wait_ge(parts_in[k], u * 128 + 128)
                        nc.vector.tensor_reduce(m.total[:, k, :], m.parts[:, k].rearrange("p c d -> p d c"), AX.X, ALU.add).then_inc(s.total, 1)
                        dve.wait_ge(s.total, n + 2)
                        nc.vector.tensor_tensor(X[:, n, :], X[:, n, :], m.total[:, k, :], ALU.add).then_inc(s.x_add, 1)
                dve.wait_ge(s.x_add, NT)

            @block.scalar
            def _(act):
                def front(e, k):
                    act.wait_ge(s.rT_ps, e + 1)
                    nc.scalar.copy(m.rowsT[:, k].rearrange("p f t -> p (f t)"), kit.psum(k)[:, 0:FC * CAP]).then_inc(s.rT, 1)
                    act.wait_ge(s.gu_ps, e + 1)
                    nc.scalar.activation(m.silu[:, k, :], kit.psum(2 + k)[:, 0:CAP], ACT.Silu).then_inc(s.silu, 1)

                def store(e, k):
                    act.wait_ge(s.out, e + 2)
                    act.dma_start(d.expert_tiles[e], m.out[:, k, :]).then_inc(stored[k], 16)

                front(0, 0)
                with act.Fori(0, E_ // 2 - 1) as u:
                    for k in range(2):
                        front(u * 2 + (k + 1), 1 - k)
                        store(u * 2 + k, k)
                front(E_ - 1, 1)
                store(E_ - 2, 0)
                store(E_ - 1, 1)

            @block.tensor
            def _(pe):
                def front(e, k, u):
                    pe.wait_ge(rows_in[k], u * 16 + 16)
                    for f in range(FC):
                        mm = nc.tensor.transpose(kit.psum(k)[:, f * CAP:(f + 1) * CAP], m.rows[:, k, f * P:(f + 1) * P], kit.ident[:])
                    mm.then_inc(s.rT_ps, 1)
                    pe.wait_ge(w_in[k], u * 32 + 32)
                    pe.wait_ge(s.rT, e + 1)
                    for part in range(2):
                        for f in range(FC):
                            mm = nc.tensor.matmul(kit.psum(2 + k)[:, part * CAP:(part + 1) * CAP], m.wgu[:, k, f, part * I_:(part + 1) * I_], m.rowsT[:, k, f, :],
                                                  start=(f == 0), stop=(f == FC - 1))
                    mm.then_inc(s.gu_ps, 1)

                def back(e, k):
                    pe.wait_ge(s.hid, e + 1)
                    nc.tensor.matmul(kit.psum(4 + k)[:, 0:D], m.hid[:, k, :], m.wd[:, k, :], start=True, stop=True).then_inc(s.y_ps, 1)

                front(0, 0, 0)
                with pe.Fori(0, E_ // 2 - 1) as u:
                    for k in range(2):
                        front(u * 2 + (k + 1), 1 - k, u + k)
                        pe.wait_ge(s.out, u * 2 + k)
                        back(u * 2 + k, k)
                front(E_ - 1, 1, E_ // 2 - 1)
                pe.wait_ge(s.out, E_ - 2)
                back(E_ - 2, 0)
                back(E_ - 1, 1)



def build(nc, dram):
    d = dram
    with ExitStack() as ctx:
        kit = Kit(nc, ctx, dram)
        load_inputs(kit)
        with kit.stage() as st:
            kit.tail_rk = st.enter_context(nc.sbuf_tensor("tail_rk", [H, B, S + LEFT], F32))
            latent_queries(kit)
            cross_attention(kit, "xa0", True, d.WkT, d.Wkv[:, INNER:2 * INNER], d.Wout, d.bout, (d.qn_g, d.kn_g))
        self_attention(kit, "sa0", False)
        mixture(kit)
        plain_queries(kit, "lq1", d.wq1)
        cross_attention(kit, "xa1", False, d.wkT1, d.wv1, d.wo1, d.bo1, ())
        self_attention(kit, "sa1", True)
        tanh_map(kit)


def kernel(**inputs):
    import concourse.bacc as bacc
    from concourse.bass_utils import run_bass_kernel_spmd

    a = {k: np.asarray(v) for k, v in inputs.items()}
    x0, s0, f0, x1, s1, f1 = (f"L{i}_{n}_" for i in range(2) for n in ("xattn", "attn", "ffn"))
    head, row = np.arange(H), np.arange(P)
    freq = np.outer(row % S, 1.0 / 10000.0 ** (np.arange(0, 32, 2, dtype=np.float32) / np.float32(32))).astype(np.float32)
    constants = {
        "ident": np.eye(P), "sel": head[:, None, None] == BT * np.arange(HC)[None, :, None] + row[None, None, :] // S,
        "cos": np.cos(freq), "sin": np.stack([-np.sin(freq), np.sin(freq)], 1),
        "causal": np.where(np.arange(S)[None, :] <= (row % S)[:, None], 0.0, -3.0e38), "blk": row[:, None] // 16 == row[None, :] // 16,
        "before": row[:, None] < row[None, :], "rank": B * S - (np.arange(NT)[None, :] * P + row[:, None]),
        "first": np.broadcast_to(1.0 + CAP * np.arange(E_), (P, E_)),
    }
    arrays = {k: v.astype(np.float32) for k, v in constants.items()}
    arrays |= {
        "x": a["x"].reshape(B * S, D), "ctx": a["ctx_1024"], "mask": a["mask_BxS2_bf1"].view(np.uint8),
        "ln_x_g": a[x0 + "ln_x_g"], "ln_x_b": a[x0 + "ln_x_b"], "ln_l_g": a[x0 + "ln_l_g"], "ln_l_b": a[x0 + "ln_l_b"],
        "qn_g": a[x0 + "qn_g"], "kn_g": a[x0 + "kn_g"], "Wq": a[x0 + "Wq"], "Wkv": a[x0 + "Wkv"],
        "WkT": a[x0 + "Wkv"][:, :INNER].T, "Wout": a[x0 + "Wout"], "bout": a[x0 + "bout"],
        "WqT": a[s0 + "Wq"].T, "WkT0": a[s0 + "Wk"].T, "WvT": a[s0 + "Wv"].T, "WoT": a[s0 + "Wo"].T, "qn_w": a[s0 + "qn_w"], "kn_w": a[s0 + "kn_w"],
        "gates_w": np.concatenate([a[f0 + "gate_w"], a[f0 + "shared_gate_w"]], 1), "shared_gu": a[f0 + "shared_gate_up_w"], "shared_down": a[f0 + "shared_down_w"],
        "expert_gu": a[f0 + "expert_gate_up_w"], "expert_down": a[f0 + "expert_down_w"],
        "wq1": a[x1 + "wq"].reshape(D, INNER), "wkT1": a[x1 + "wk"].reshape(D, INNER).T, "wv1": a[x1 + "wv"].reshape(D, INNER),
        "wo1": a[x1 + "wo"].reshape(INNER, D), "bo1": a[x1 + "bo"],
        "cw": a[s1 + "c_attn_w"], "cb": a[s1 + "c_attn_b"].reshape(6, P).T, "q2lT": a[s1 + "q2l_w"].T, "q2lb": a[s1 + "q2l_b"], "kv2l": a[s1 + "kv2l_w"], "kv2lT": a[s1 + "kv2l_w"].T,
        "kvb": a[s1 + "kv2l_b"], "l2oT": a[s1 + "l2o_w"].T, "l2ob": a[s1 + "l2o_b"], "wqkT": a[s1 + "wqk_w"].T, "wqkb": a[s1 + "wqk_b"],
        "cprojT": a[s1 + "cproj_w"].T, "cprojb": a[s1 + "cproj_b"],
        "weightT": a[f1 + "weight"].T, "aux1T": a[f1 + "aux_weight1"].T, "aux2": a[f1 + "aux_weight2"], "map_b": a[f1 + "bias"],
    }
    arrays = {k: np.ascontiguousarray(v) for k, v in arrays.items()}
    nc = bacc.Bacc("TRN2", target_bir_lowering=False, num_devices=1)
    handles = {k: nc.dram_tensor(f"in_{k}", v.shape, mybir.dt.from_np(v.dtype), kind="ExternalInput").ap() for k, v in arrays.items()}
    out = nc.dram_tensor("out_x", (B * S, D), F32, kind="ExternalOutput").ap()
    handles["out"] = out
    handles["out_tiles"] = out.rearrange("(t p) d -> t p d", p=P)
    handles["qT"] = nc.dram_tensor("scratch_qT", (P, NP_, B * S), F32, kind="Internal").ap()
    lat = nc.dram_tensor("scratch_lat", (B * S, D), F32, kind="Internal").ap()
    handles["tail_lat"] = lat.rearrange("(t p) d -> t p d", p=P)
    handles["tail_lat_b"] = lat.rearrange("(b s) d -> b s d", s=S)
    handles["tail_last"] = nc.dram_tensor("scratch_last", (B, D), F32, kind="Internal").ap()
    handles["routed"] = nc.dram_tensor("scratch_routed", (B * S, ROUTED), F32, kind="Internal").ap()
    handles["routed_tiles"] = handles["routed"].rearrange("(t p) d -> t p d", p=P)
    handles["expert_rows"] = nc.dram_tensor("scratch_expert", (1 + E_ * CAP, D), F32, kind="Internal").ap()
    handles["expert_tiles"] = handles["expert_rows"][1:1 + E_ * CAP, :].rearrange("(e c) d -> e c d", c=CAP)
    build(nc, named(handles))
    res = run_bass_kernel_spmd(nc, [{f"in_{k}": v for k, v in arrays.items()}], core_ids=[0])
    return res.results[0]["out_x"].reshape(B, S, D)
```

```python
from collections import namedtuple
from contextlib import ExitStack, contextmanager

import numpy as np
import concourse.bass as bass
from concourse import mybir

F32 = mybir.dt.float32
BF16 = mybir.dt.bfloat16
U32 = mybir.dt.uint32
U8 = mybir.dt.uint8
ALU = mybir.AluOpType
ACT = mybir.ActivationFunctionType
AX = mybir.AxisListType

P = 128
B, S, D = 64, 32, 256
NT = B * S // P
BT = P // S
FC = D // P
H, DH = 16, 64
INNER = H * DH
NP_ = INNER // P
CTX = 257
KF = 2
LEFT = CTX - KF * P
GB = 8
NG = B // GB
GT = GB * S
HC = H // BT
LN_EPS = 1e-5
MASKED = 1e30


def named(things):
    return namedtuple("Named", list(things))(**things)


class Kit:

    def __init__(self, nc, ctx, dram):
        self.nc, self.dram, self.used = nc, dram, []
        self.bank = [ctx.enter_context(nc.psum_tensor(f"bank{i}", [P, 2, 512], F32)) for i in range(4)]
        self.X = ctx.enter_context(nc.sbuf_tensor("residual", [P, NT, D], F32))
        self.ident = ctx.enter_context(nc.sbuf_tensor("ident", [P, P], F32))
        self.neg_half = ctx.enter_context(nc.sbuf_tensor("neg_half", [P, 256], F32))

    @contextmanager
    def stage(self):
        outer, self.used = self.used, []
        with ExitStack() as stack:
            yield stack
            self.nc.clear_and_free_semaphores(self.used)
            self.nc.all_engine_barrier()
        self.used = outer

    def semaphore(self, name):
        self.used.append(self.nc.alloc_semaphore(name=name))
        return self.used[-1]

    def psum(self, i):
        return self.bank[i // 2][:, i % 2, :]

    def buffers(self, stack, **shapes):
        made = {}
        for name, (shape, dtype) in shapes.items():
            made[name] = stack.enter_context(self.nc.sbuf_tensor(f"{name}_{self.nc.next_id()}", shape, dtype))
        return named(made)

    def sems(self, stage, names):
        return named({n: self.semaphore(f"{stage}_{n}") for n in names.split()})

    def several(self, stage, name, count):
        return [self.semaphore(f"{stage}_{name}{i}") for i in range(count)]

    def pair(self, stage, name):
        return self.several(stage, name, 2)


def hold(engine, sem, value, passed):
    engine.wait_ge(sem, value)
    engine.sem_inc(passed, 1)


def row_stats(nc, dve, rows, stats, mean_var, stats_done, aggr_done, base=0):
    for t, r in enumerate(rows):
        nc.vector.bn_stats(stats[:, t, :], r).then_inc(stats_done, 1)
    for t in range(len(rows)):
        dve.wait_ge(stats_done, base + t + 1)
        nc.vector.bn_aggr(mean_var[:, t, :], stats[:, t, :]).then_inc(aggr_done, 1)


def inv_root(nc, pool, neg_half, out, value, scale, shift, op, done_scaled, n_scaled, done):
    nc.gpsimd.tensor_scalar(out, value, scale, shift, ALU.mult, op).then_inc(done_scaled, 1)
    pool.wait_ge(done_scaled, n_scaled)
    nc.gpsimd.tensor_tensor(out, out, neg_half, ALU.pow).then_inc(done, 1)


def load_inputs(kit):
    nc, d = kit.nc, kit.dram
    sem = kit.sems("load", "x_in half_set")
    with nc.Block() as block:
        @block.sync
        def _(sp):
            sp.dma_start(kit.X[:], d.x.rearrange("(t p) d -> p t d", p=P)).then_inc(sem.x_in, 16)
            sp.dma_start(kit.ident[:], d.ident).then_inc(sem.x_in, 16)
            sp.wait_ge(sem.x_in, 32)

        @block.vector
        def _(dve):
            nc.vector.memset(kit.neg_half[:], -0.5).then_inc(sem.half_set, 1)
            dve.wait_ge(sem.half_set, 1)


def latent_queries(kit):
    nc, d = kit.nc, kit.dram
    X = kit.X
    with kit.stage() as st:
        m = kit.buffers(
            st, xl=([P, NT, D], F32), stats=([P, NT + 1, 6], F32), mv1=([P, NT, 2], F32), mv2=([P, NT, 2], F32),
            r1=([P, NT], F32), r2=([P, NT], F32), g_l=([P, D], F32), b_l=([P, D], F32), g_x=([B, D], F32), b_x=([B, D], F32),
            wq=([P, FC, INNER], F32), wk=([P, FC, INNER], F32), cent=([P, 2, D], F32), ln=([P, 2, D], F32),
            lnT=([P, 2, FC, P], F32), ksq=([P, INNER], F32), qsq=([P, INNER], F32), q=([P, 2, INNER], F32),
            ssk=([P, NT, H], F32), ssq=([P, 2, H], F32), rq=([P, 2, H], F32), qh=([P, 2, INNER], F32),
            qT=([P, 2, NP_, P], F32), last=([B, D], F32), mvl=([B, 1, 2], F32), rl=([B, 1], F32),
            lastn=([B, D], F32), lastT=([P, FC, B], F32), ssl=([B, H], F32), rkl=([B, H], F32), rk=([P, NT, H], F32))
        s = kit.sems("lat", "w_in last_in stats aggr1 aggr2 eps r1 r2 xl cent ln_ready lnT_ps lnT k_ps k_sq kss "
                     "q_ps q_sq q_copied qss rq_scaled rq qh qT_ps qT last_cent passed lastn lastT_ps lastT kl_ps kl_sq "
                     "kl_ss rkl rk_lat tail_ps tail_sb")
        tail = kit.tail_rk
        ln_stored, qT_stored = kit.pair("lat", "ln_stored"), kit.pair("lat", "qT_stored")

        with nc.Block() as block:
            @block.sync
            def _(sp):
                for sb, src in ((m.g_l, d.ln_l_g), (m.b_l, d.ln_l_b)):
                    sp.dma_start(sb[:], src.partition_broadcast(P)).then_inc(s.w_in, 16)
                for sb, src in ((m.g_x, d.ln_x_g), (m.b_x, d.ln_x_b)):
                    sp.dma_start(sb[:], src.partition_broadcast(B)).then_inc(s.w_in, 16)
                sp.dma_start(m.wq[:], d.Wq.rearrange("(f p) n -> p f n", p=P)).then_inc(s.w_in, 16)
                sp.dma_start(m.wk[:], d.Wkv[:, 0:INNER].rearrange("(f p) n -> p f n", p=P)).then_inc(s.w_in, 16)
                sp.dma_start(m.last[:], d.ctx[:, CTX - 1, :]).then_inc(s.last_in, 16)
                with sp.Fori(0, NT // 2) as u:
                    for k in range(2):
                        n = u * 2 + k
                        sp.wait_ge(s.ln_ready, n + 1)
                        sp.dma_start(d.tail_lat[n], m.ln[:, k, :]).then_inc(ln_stored[k], 16)
                        sp.wait_ge(s.qT, n + 1)
                        sp.dma_start(d.qT[:, :, bass.ts(n, P)], m.qT[:, k]).then_inc(qT_stored[k], 16)
                sp.wait_ge(s.lastn, 1)
                sp.dma_start(d.tail_last, m.lastn[:]).then_inc(s.last_in, 16)
                sp.wait_ge(s.last_in, 32)
                for k in range(2):
                    sp.wait_ge(ln_stored[k], 16 * (NT // 2 + 1))
                    sp.wait_ge(qT_stored[k], 16 * (NT // 2 + 1))

            @block.vector
            def _(dve):
                row_stats(nc, dve, [X[:, t, :] for t in range(NT)], m.stats, m.mv1, s.stats, s.aggr1)
                dve.wait_ge(s.r1, 1)
                for t in range(NT):
                    nc.vector.tensor_scalar(m.xl[:, t, :], X[:, t, :], m.mv1[:, t, 0:1], m.r1[:, t:t + 1],
                                            ALU.subtract, ALU.mult).then_inc(s.xl, 1)
                dve.wait_ge(s.xl, NT)
                row_stats(nc, dve, [m.xl[:, t, :] for t in range(NT)], m.stats, m.mv2, s.stats, s.aggr2, NT)
                dve.wait_ge(s.last_in, 16)
                row_stats(nc, dve, [m.last[:]], m.stats[0:B, NT:NT + 1, :], m.mvl, s.stats, s.aggr2, 2 * NT)
                dve.wait_ge(s.r2, 2)
                dve.wait_ge(s.w_in, 96)
                nc.vector.scalar_tensor_tensor(m.lastn[:], m.last[:], m.mvl[:, 0, 0:1], m.g_x[:], ALU.subtract, ALU.mult).then_inc(s.last_cent, 1)
                dve.wait_ge(s.last_cent, 1)
                nc.vector.scalar_tensor_tensor(m.lastn[:], m.lastn[:], m.rl[:, 0:1], m.b_x[:], ALU.mult, ALU.add).then_inc(s.lastn, 1)
                for k in range(2):
                    dve.sem_inc(ln_stored[k], 16)
                    dve.sem_inc(qT_stored[k], 16)
                with dve.Fori(0, NT // 2) as u:
                    for k in range(2):
                        n = u * 2 + k
                        nc.vector.scalar_tensor_tensor(m.cent[:, k, :], m.xl[:, n, :], m.mv2[:, n, 0:1], m.g_l[:],
                                                       ALU.subtract, ALU.mult).then_inc(s.cent, 1)
                        dve.wait_ge(s.cent, n + 1)
                        dve.wait_ge(ln_stored[k], u * 16 + 16)
                        nc.vector.scalar_tensor_tensor(m.ln[:, k, :], m.cent[:, k, :], m.r2[:, bass.ds(n, 1)], m.b_l[:],
                                                       ALU.mult, ALU.add).then_inc(s.ln_ready, 1)
                        dve.wait_ge(s.q_sq, n + 1)
                        nc.vector.tensor_reduce(m.ssq[:, k, :], m.qsq[:].rearrange("p (h e) -> p h e", h=H), AX.X, ALU.add).then_inc(s.qss, 1)
                        dve.wait_ge(s.rq, n + 1)
                        dve.wait_ge(s.q_copied, n + 1)
                        nc.vector.tensor_tensor(m.qh[:, k, :].rearrange("p (h e) -> p h e", h=H), m.q[:, k, :].rearrange("p (h e) -> p h e", h=H),
                                                m.rq[:, k, :].unsqueeze(2).to_broadcast([P, H, DH]), ALU.mult).then_inc(s.qh, 1)
                        dve.wait_ge(s.k_sq, n + 1)
                        nc.vector.tensor_reduce(m.ssk[:, n, :], m.ksq[:].rearrange("p (h e) -> p h e", h=H), AX.X, ALU.add).then_inc(s.kss, 1)
                        dve.wait_ge(s.qT_ps, n + 1)
                        dve.wait_ge(qT_stored[k], u * 16 + 16)
                        nc.vector.tensor_copy(m.qT[:, k].rearrange("p a t -> p (a t)"), kit.bank[3][:].rearrange("p a t -> p (a t)")).then_inc(s.qT, 1)
                dve.wait_ge(s.kl_sq, 1)
                nc.vector.tensor_reduce(m.ssl[:], m.ksq[0:B, :].rearrange("p (h e) -> p h e", h=H), AX.X, ALU.add).then_inc(s.kl_ss, 1)
                for t in range(NT):
                    dve.wait_ge(s.tail_ps, t // 4 + 1)
                    nc.vector.tensor_copy(tail[:, t * BT:(t + 1) * BT, 0:S],
                                          kit.psum(t // 4)[0:H, (t % 4) * P:(t % 4 + 1) * P].rearrange("h (b k) -> h b k", b=BT)).then_inc(s.tail_sb, 1)
                dve.wait_ge(s.tail_ps, 5)
                nc.vector.tensor_copy(tail[:, :, S:S + 1], kit.psum(4)[0:H, 0:B].unsqueeze(2)).then_inc(s.tail_sb, 1)

            @block.gpsimd
            def _(pool):
                pool.wait_ge(s.aggr1, NT)
                inv_root(nc, pool, kit.neg_half[:, 0:NT], m.r1[:], m.mv1[:, :, 1], 1.0, LN_EPS, ALU.add, s.eps, 1, s.r1)
                pool.wait_ge(s.aggr2, NT + 1)
                inv_root(nc, pool, kit.neg_half[:, 0:NT], m.r2[:], m.mv2[:, :, 1], 1.0, LN_EPS, ALU.add, s.eps, 2, s.r2)
                inv_root(nc, pool, kit.neg_half[0:B, 0:1], m.rl[:], m.mvl[:, :, 1], 1.0, LN_EPS, ALU.add, s.eps, 3, s.r2)
                with pool.Fori(0, NT // 2) as u:
                    for k in range(2):
                        n = u * 2 + k
                        hold(pool, s.qss, n + 1, s.passed)
                        inv_root(nc, pool, kit.neg_half[:, 0:H], m.rq[:, k, :], m.ssq[:, k, :], 1.0 / DH, 1e-16, ALU.max, s.rq_scaled, n + 1, s.rq)
                pool.wait_ge(s.kss, NT)
                inv_root(nc, pool, kit.neg_half[:], m.rk[:].rearrange("p t h -> p (t h)"), m.ssk[:].rearrange("p t h -> p (t h)"),
                         1.0 / DH, 1e-16, ALU.max, s.eps, 4, s.rk_lat)
                pool.wait_ge(s.kl_ss, 1)
                inv_root(nc, pool, kit.neg_half[0:B, 0:H], m.rkl[:], m.ssl[:], 1.0 / DH, 1e-16, ALU.max, s.eps, 5, s.rkl)

            @block.scalar
            def _(act):
                with act.Fori(0, NT // 2) as u:
                    for k in range(2):
                        n = u * 2 + k
                        act.wait_ge(s.lnT_ps, n + 1)
                        nc.scalar.copy(m.lnT[:, k].rearrange("p f t -> p (f t)"), kit.psum(0)[:, 0:FC * P]).then_inc(s.lnT, 1)
                        act.wait_ge(s.q_ps, n + 1)
                        nc.scalar.activation(m.qsq[:], kit.bank[2][:].rearrange("p a t -> p (a t)"), ACT.Square).then_inc(s.q_sq, 1)
                        nc.scalar.copy(m.q[:, k, :], kit.bank[2][:].rearrange("p a t -> p (a t)")).then_inc(s.q_copied, 1)
                        act.wait_ge(s.k_ps, n + 1)
                        nc.scalar.activation(m.ksq[:], kit.bank[1][:].rearrange("p a t -> p (a t)"), ACT.Square).then_inc(s.k_sq, 1)
                act.wait_ge(s.lastT_ps, 1)
                nc.scalar.copy(m.lastT[:], kit.psum(0)[:, 0:FC * B].rearrange("p (f t) -> p f t", f=FC)).then_inc(s.lastT, 1)
                act.wait_ge(s.kl_ps, 1)
                act.wait_ge(s.kss, NT)
                nc.scalar.activation(m.ksq[0:B, :], kit.bank[1][0:B].rearrange("p a t -> p (a t)"), ACT.Square).then_inc(s.kl_sq, 1)

            @block.tensor
            def _(pe):
                pe.wait_ge(s.w_in, 96)
                with pe.Fori(0, NT // 2) as u:
                    for k in range(2):
                        n = u * 2 + k
                        pe.wait_ge(s.ln_ready, n + 1)
                        for f in range(FC):
                            mm = nc.tensor.transpose(kit.psum(0)[:, f * P:(f + 1) * P], m.ln[:, k, f * P:(f + 1) * P], kit.ident[:])
                        mm.then_inc(s.lnT_ps, 1)
                        pe.wait_ge(s.lnT, n + 1)
                        for bank, w, done, freed in ((4, m.wq, s.q_ps, s.q_copied), (2, m.wk, s.k_ps, s.k_sq)):
                            pe.wait_ge(freed, n)
                            for half in range(2):
                                for f in range(FC):
                                    mm = nc.tensor.matmul(kit.psum(bank + half), m.lnT[:, k, f, :], w[:, f, half * 512:(half + 1) * 512],
                                                          start=(f == 0), stop=(f == FC - 1))
                            mm.then_inc(done, 1)
                        pe.wait_ge(s.qh, n + 1)
                        pe.wait_ge(s.qT, n)
                        for pr in range(NP_):
                            mm = nc.tensor.transpose(kit.psum(6 + pr // 4)[:, (pr % 4) * P:(pr % 4 + 1) * P], m.qh[:, k, pr * P:(pr + 1) * P], kit.ident[:])
                        mm.then_inc(s.qT_ps, 1)
                pe.wait_ge(s.lastn, 1)
                for f in range(FC):
                    mm = nc.tensor.transpose(kit.psum(0)[:, f * B:(f + 1) * B], m.lastn[:, f * P:(f + 1) * P], kit.ident[0:B, 0:B])
                mm.then_inc(s.lastT_ps, 1)
                pe.wait_ge(s.lastT, 1)
                pe.wait_ge(s.k_sq, NT)
                for half in range(2):
                    for f in range(FC):
                        mm = nc.tensor.matmul(kit.psum(2 + half)[0:B, :], m.lastT[:, f, :], m.wk[:, f, half * 512:(half + 1) * 512],
                                              start=(f == 0), stop=(f == FC - 1))
                mm.then_inc(s.kl_ps, 1)
                pe.wait_ge(s.kl_sq, 1)
                pe.wait_ge(s.rk_lat, 1)
                for t in range(NT):
                    mm = nc.tensor.transpose(kit.psum(t // 4)[0:H, (t % 4) * P:(t % 4 + 1) * P], m.rk[:, t, :], kit.ident[:])
                    if t % 4 == 3:
                        mm.then_inc(s.tail_ps, 1)
                pe.wait_ge(s.rkl, 1)
                nc.tensor.transpose(kit.psum(4)[0:H, 0:B], m.rkl[:], kit.ident[0:B, 0:B]).then_inc(s.tail_ps, 1)


def cross_attention(kit, stage, keyed, wk_t, w_v, w_out, bias, gains):
    nc, d = kit.nc, kit.dram
    X = kit.X
    TAIL = LEFT + (S if keyed else 0)
    NK = KF * P + TAIL
    TILES = [(0, P), (P, P), (KF * P, TAIL)]
    RB = 4
    PB = 1 if keyed else 2
    score_bank, spread_bank = [4, 5, 4, 5], [7, 6, 7, 6]
    prob_bank, mix_bank = ([4, 5, 6], [7, 5]) if keyed else ([2, 3, 6], [7, 6])
    with kit.stage() as st:
        m = kit.buffers(
            st, wkT=([P, NP_, D], F32), wv=([P, FC, INNER], F32), wo=([P, NP_, D], F32), bo=([P, D], F32), gain=([P, 4], F32),
            qT=([P, NP_, GT], F32), qk=([P, FC, GB, H, S], F32), mix=([P, FC, H, GT], F32), oT=([P, NP_, GT], F32),
            rows=([P, RB, KF + 1, D], F32), rowsT=([P, 2, FC, NK], F32),
            prob=([P, PB, HC, NK], F32), probT=([P, 3, 512], F32), top=([P, 2, HC], F32), ntop=([P, 2, HC], F32),
            mass=([P, 2, HC], F32), rmass=([P, 2, HC], F32))
        if keyed:
            mk = kit.buffers(
                st, wk=([P, FC, INNER], F32), raw=([P, 2, KF, D], F32), cent=([P, KF, D], F32), g_x=([P, D], F32), b_x=([P, D], F32),
                stats=([P, KF, 6], F32), mv=([P, 2, KF, 2], F32), rstd=([P, 2, KF], F32), ksq=([P, KF, INNER], F32),
                ss=([P, KF * H], F32), rk=([P, 2, KF * H], F32), rkT=([H, NK], F32), rkb=([P, HC, NK], F32), score=([P, HC, NK], F32), sel=([H, HC, P], F32),
                valid=([1, RB, CTX], U8), mask=([1, 2, NK], BF16), one=([1, P], BF16))
        s = kit.sems(stage, "w_in set mask gain wkT raw_free rows_free stats aggr eps rstd cent rows rT_ps rT k_ps k_sq ss rk_scaled rk "
                     "rkT_ps rkT rkT_tail rkb_ps rkb s_ps score ntop p mass normed pT_ps pT pT1 mix_ps mix0 mix1 o_ps o_act o_dve x_ps x_add "
                     "q_in qk_ps qk_act qk_dve qk_free passed_dve passed_pool")
        raw_in = kit.several(stage, "raw_in", 2)
        rows_in = kit.several(stage, "rows_in", RB)
        row_loads = 48 if keyed else 32

        def uses(g, j, buffers):
            return g * (GB // buffers) + (j // buffers + 1)

        def past(engine, sem, value):
            if not isinstance(value, int) or value > 0:
                engine.wait_ge(sem, value)

        def groups(engine, group):
            with engine.Fori(0, NG - 1) as g:
                group(g, lambda j: True)
            group(NG - 1, lambda j: j < GB)

        with nc.Block() as block:
            @block.sync
            def _(sp):
                sp.dma_start(m.wkT[:], wk_t.rearrange("(a p) n -> p a n", p=P)).then_inc(s.w_in, 16)
                sp.dma_start(m.wv[:], w_v.rearrange("(f p) n -> p f n", p=P)).then_inc(s.w_in, 16)
                sp.dma_start(m.wo[:], w_out.rearrange("(a p) n -> p a n", p=P)).then_inc(s.w_in, 16)
                sp.dma_start(m.bo[:], bias.partition_broadcast(P)).then_inc(s.w_in, 16)
                if keyed:
                    sp.dma_start(mk.wk[:], d.Wkv[:, 0:INNER].rearrange("(f p) n -> p f n", p=P)).then_inc(s.w_in, 16)
                    sp.dma_start(mk.g_x[:], d.ln_x_g.partition_broadcast(P)).then_inc(s.w_in, 16)
                    sp.dma_start(mk.b_x[:], d.ln_x_b.partition_broadcast(P)).then_inc(s.w_in, 16)
                    sp.dma_start(mk.sel[:], d.sel).then_inc(s.w_in, 16)
                    for half in range(2):
                        for i, g in enumerate(gains):
                            sp.dma_start(m.gain[half * DH:(half + 1) * DH, i:i + 1], g.unsqueeze(1)).then_inc(s.w_in, 16)

                def group(g):
                    sp.wait_ge(s.qk_free, g + 1)
                    sp.dma_start(m.qT[:], d.qT[:, :, bass.ts(g, GT)]).then_inc(s.q_in, 16)
                    for j in range(GB):
                        n, k, b = g * GB + j, j % 2, j % RB
                        if keyed:
                            sp.wait_ge(s.raw_free, n + 1)
                            sp.dma_start(mk.raw[:, k], d.ctx[n, 0:KF * P, :].rearrange("(c p) d -> p c d", p=P)).then_inc(raw_in[k], 16)
                        sp.wait_ge(s.rows_free, n + 1)
                        if keyed:
                            sp.dma_start(m.rows[0:S, b, KF, :], d.tail_lat_b[n]).then_inc(rows_in[b], 16)
                            sp.dma_start(m.rows[S:S + 1, b, KF, :], d.tail_last[bass.ds(n, 1), :]).then_inc(rows_in[b], 16)
                            sp.dma_start(mk.valid[:, b, :], d.mask[bass.ds(n, 1), :]).then_inc(rows_in[b], 16)
                        else:
                            sp.dma_start(m.rows[:, b, 0:KF, :], d.ctx[n, 0:KF * P, :].rearrange("(c p) d -> p c d", p=P)).then_inc(rows_in[b], 16)
                            sp.dma_start(m.rows[0:LEFT, b, KF, :], d.ctx[n, KF * P:CTX, :]).then_inc(rows_in[b], 16)

                with sp.Fori(0, NG) as g:
                    group(g)

            n_weights = 16 * (4 + (8 if keyed else 0))

            @block.vector
            def _(dve):
                dve.sem_inc(s.qk_free, 1)
                dve.sem_inc(s.raw_free, 2)
                dve.sem_inc(s.rows_free, RB)
                if keyed:
                    nc.vector.memset(mk.mask[:], 0.0).then_inc(s.set, 1)
                    nc.vector.memset(mk.one[:], 1.0).then_inc(s.set, 1)
                dve.wait_ge(s.w_in, n_weights)
                if keyed:
                    nc.vector.scalar_tensor_tensor(m.gain[:, 2:3], m.gain[:, 0:1], DH ** -0.5, m.gain[:, 1:2], ALU.mult, ALU.mult).then_inc(s.gain, 1)
                    dve.wait_ge(s.gain, 1)
                    nc.vector.tensor_scalar(m.wkT[:], m.wkT[:], m.gain[:, 2:3], None, ALU.mult).then_inc(s.wkT, 1)
                else:
                    nc.vector.tensor_scalar(m.wkT[:], m.wkT[:], DH ** -0.5, None, ALU.mult).then_inc(s.wkT, 1)
                nc.vector.tensor_tensor(X[:], X[:], m.bo[:].unsqueeze(1).to_broadcast([P, NT, D]), ALU.add).then_inc(s.x_add, 1)

                def norm_stats(n, k, loads):
                    dve.wait_ge(raw_in[k], loads * 16)
                    for c in range(KF):
                        nc.vector.bn_stats(mk.stats[:, c, :], mk.raw[:, k, c, :]).then_inc(s.stats, 1)
                    hold(dve, s.stats, (n + 1) * KF, s.passed_dve)
                    for c in range(KF):
                        nc.vector.bn_aggr(mk.mv[:, k, c, :], mk.stats[:, c, :]).then_inc(s.aggr, 1)

                def norm_rows(n, k, b):
                    dve.wait_ge(s.rstd, n + 1)
                    for c in range(KF):
                        nc.vector.scalar_tensor_tensor(mk.cent[:, c, :], mk.raw[:, k, c, :], mk.mv[:, k, c, 0:1], mk.g_x[:],
                                                       ALU.subtract, ALU.mult).then_inc(s.cent, 1)
                    dve.wait_ge(s.cent, (n + 1) * KF)
                    dve.sem_inc(s.raw_free, 1)
                    dve.wait_ge(s.rows_free, n + 1)
                    for c in range(KF):
                        nc.vector.scalar_tensor_tensor(m.rows[:, b, c, :], mk.cent[:, c, :], mk.rstd[:, k, c:c + 1], mk.b_x[:],
                                                       ALU.mult, ALU.add).then_inc(s.rows, 1)

                def key_sums(n):
                    past(dve, s.rk_scaled, n)
                    for c in range(KF):
                        dve.wait_ge(s.k_sq, n * 4 + (2 * c + 2))
                        nc.vector.tensor_reduce(mk.ss[:, c * H:(c + 1) * H], mk.ksq[:, c, :].rearrange("p (h e) -> p h e", h=H), AX.X, ALU.add).then_inc(s.ss, 1)

                def maxima(n, k):
                    for c in range(HC):
                        if keyed:
                            hold(dve, s.s_ps, n * HC + (c + 1), s.passed_dve)
                            hold(dve, s.rkb, n * HC + (c + 1), s.passed_dve)
                            nc.vector.tensor_tensor_reduce(mk.score[:, c, :], kit.psum(score_bank[c])[:, 0:NK], mk.rkb[:, c, :], 1.0, -3.0e38,
                                                           ALU.mult, ALU.max, m.top[:, k, c:c + 1]).then_inc(s.score, 1)
                        else:
                            dve.wait_ge(s.s_ps, n * HC + (c + 1))
                            nc.vector.reduce_max(m.top[:, k, c:c + 1], kit.psum(score_bank[c])[:, 0:NK], AX.X).then_inc(s.score, 1)
                        dve.wait_ge(s.score, n * HC + (c + 1))
                        nc.vector.tensor_scalar(m.ntop[:, k, c:c + 1], m.top[:, k, c:c + 1], -1.0, None, ALU.mult).then_inc(s.ntop, 1)

                def normed(n, k):
                    for c in range(HC):
                        dve.wait_ge(s.p, n * HC + (c + 1))
                        nc.vector.reciprocal(m.rmass[:, k, c:c + 1], m.mass[:, k, c:c + 1]).then_inc(s.mass, 1)
                    for c in range(HC):
                        dve.wait_ge(s.mass, n * HC + (c + 1))
                        nc.vector.tensor_scalar(m.prob[:, k % PB, c, :], m.prob[:, k % PB, c, :], m.rmass[:, k, c:c + 1], None, ALU.mult).then_inc(s.normed, 1)

                def probs_T(n):
                    for c, size in ((0, P), (2, TAIL)):
                        dve.wait_ge(s.pT_ps, n * 3 + (c + 1))
                        nc.vector.tensor_copy(m.probT[0:size, c, :], kit.psum(prob_bank[c])[0:size, :]).then_inc(s.pT, 1)

                def mixed(n, j):
                    dve.wait_ge(s.mix_ps, n * FC + FC)
                    dve.sem_inc(s.rows_free, 1)
                    nc.vector.tensor_copy(m.mix[:, 1, :, j * S:(j + 1) * S], kit.psum(mix_bank[1]).rearrange("p (h q) -> p h q", h=H)).then_inc(s.mix1, 1)

                def queries(g):
                    for i in range(1, H, 2):
                        dve.wait_ge(s.qk_ps, g * H + (i + 1))
                        nc.vector.tensor_copy(m.qk[:, :, :, i, :], kit.psum(3).rearrange("p (f b q) -> p f b q", f=FC, b=GB)).then_inc(s.qk_dve, 1)

                def group(g, is_in):
                    for j in range(GB):
                        n, k = g * GB + j, j % 2
                        if keyed:
                            maxima(n, k)
                            normed(n, k)
                            if is_in(j + 3):
                                norm_rows(n + 3, 1 - k, (j + 3) % RB)
                            probs_T(n)
                            if is_in(j + 2):
                                key_sums(n + 2)
                            if is_in(j + 4):
                                norm_stats(n + 4, k, uses(g, j + 4, 2))
                        else:
                            if j + 1 == GB and is_in(GB):
                                queries(g + 1)
                            if is_in(j + 1):
                                maxima(n + 1, 1 - k)
                            probs_T(n)
                            if is_in(j + 1):
                                normed(n + 1, 1 - k)
                        mixed(n, j)
                    if keyed and is_in(GB):
                        queries(g + 1)
                    for i in range(1, NP_ // 2, 2):
                        dve.wait_ge(s.o_ps, g * (NP_ // 2) + (i + 1))
                        nc.vector.tensor_copy(m.oT[:, 2 * i:2 * i + 2, :], kit.psum(2 + i % 2).rearrange("p (a t) -> p a t", a=2)).then_inc(s.o_dve, 1)
                    for i in range(GT // P):
                        dve.wait_ge(s.x_ps, g * (GT // P) + (i + 1))
                        if i == 0:
                            dve.wait_ge(s.x_add, 1)
                        nc.vector.tensor_tensor(X[:, g * (GT // P) + i, :], X[:, g * (GT // P) + i, :], kit.psum(i)[:, 0:D], ALU.add).then_inc(s.x_add, 1)

                if keyed:
                    for n in range(4):
                        norm_stats(n, n % 2, n // 2 + 1)
                        if n < 3:
                            norm_rows(n, n % 2, n)
                    key_sums(0)
                    key_sums(1)
                queries(0)
                if not keyed:
                    maxima(0, 0)
                    normed(0, 0)
                groups(dve, group)

            @block.gpsimd
            def _(pool):
                def rstd(n, k):
                    hold(pool, s.aggr, (n + 1) * KF, s.passed_pool)
                    inv_root(nc, pool, kit.neg_half[:, 0:KF], mk.rstd[:, k, :], mk.mv[:, k, :, 1], 1.0, LN_EPS, ALU.add, s.eps, n + 1, s.rstd)

                def key_norms(n, k):
                    hold(pool, s.ss, (n + 1) * KF, s.passed_pool)
                    inv_root(nc, pool, kit.neg_half[:, 0:KF * H], mk.rk[:, k, :], mk.ss[:], 1.0 / DH, 1e-16, ALU.max, s.rk_scaled, n + 1, s.rk)

                def tail(n):
                    past(pool, s.rkb_ps, n * HC)
                    nc.gpsimd.tensor_copy(mk.rkT[:, KF * P:NK], kit.tail_rk[:, n, :]).then_inc(s.rkT_tail, 1)

                def mask(n, k, b, loads):
                    hold(pool, rows_in[b], loads * row_loads, s.passed_pool)
                    for at, rows in ((0, slice(0, KF * P)), (NK - LEFT, slice(KF * P, CTX))):
                        nc.gpsimd.tensor_scalar(mk.mask[:, k, at:at + rows.stop - rows.start], mk.valid[:, b, rows], 1.0, MASKED, ALU.subtract, ALU.mult).then_inc(s.mask, 1)

                def group(g, is_in):
                    for j in range(GB):
                        n, k = g * GB + j, j % 2
                        if is_in(j + 1):
                            tail(n + 1)
                            mask(n + 1, 1 - k, (j + 1) % RB, uses(g, j + 1, RB))
                        if is_in(j + 2):
                            key_norms(n + 2, k)
                        if is_in(j + 4):
                            rstd(n + 4, k)

                if keyed:
                    pool.wait_ge(s.set, 2)
                    for n in range(4):
                        rstd(n, n % 2)
                    tail(0)
                    mask(0, 0, 0, 1)
                    key_norms(0, 0)
                    key_norms(1, 1)
                    groups(pool, group)

            @block.scalar
            def _(act):
                def rows_T(n, k):
                    act.wait_ge(s.rT_ps, n + 1)
                    nc.scalar.copy(m.rowsT[:, k], kit.bank[0][:, :, 0:NK]).then_inc(s.rT, 1)

                def key_squares(n, c):
                    past(act, s.ss, n * KF + (c - 1))
                    for i in range(2 * c, 2 * c + 2):
                        act.wait_ge(s.k_ps, n * 4 + (i + 1))
                        nc.scalar.activation(mk.ksq[:, c, (i % 2) * 512:(i % 2 + 1) * 512], kit.psum(2 + i % 2), ACT.Square).then_inc(s.k_sq, 1)

                def spread(n, c):
                    act.wait_ge(s.rkb_ps, n * HC + (c + 1))
                    nc.scalar.copy(mk.rkb[:, c, :], kit.psum(spread_bank[c])[:, 0:NK]).then_inc(s.rkb, 1)

                def exps(n, k, c):
                    act.wait_ge(s.ntop, n * HC + (c + 1))
                    src = mk.score[:, c, :] if keyed else kit.psum(score_bank[c])[:, 0:NK]
                    nc.scalar.activation(m.prob[:, k % PB, c, :], src, ACT.Exp, bias=m.ntop[:, k, c:c + 1], accum_out=m.mass[:, k, c:c + 1]).then_inc(s.p, 1)

                def probs_T(n):
                    act.wait_ge(s.pT_ps, n * 3 + 2)
                    nc.scalar.copy(m.probT[:, 1, :], kit.psum(prob_bank[1])).then_inc(s.pT1, 1)

                def mixed(n, j):
                    act.wait_ge(s.mix_ps, n * FC + 1)
                    nc.scalar.copy(m.mix[:, 0, :, j * S:(j + 1) * S], kit.psum(mix_bank[0]).rearrange("p (h q) -> p h q", h=H)).then_inc(s.mix0, 1)

                def queries(g):
                    for i in range(0, H, 2):
                        act.wait_ge(s.qk_ps, g * H + (i + 1))
                        nc.scalar.copy(m.qk[:, :, :, i, :], kit.psum(2).rearrange("p (f b q) -> p f b q", f=FC, b=GB)).then_inc(s.qk_act, 1)

                def group(g, is_in):
                    for j in range(GB):
                        n, k = g * GB + j, j % 2
                        if keyed:
                            act.wait_ge(s.rkT_ps, n + 1)
                            nc.scalar.copy(mk.rkT[:, 0:KF * P], kit.psum(6)[0:H, 0:KF * P]).then_inc(s.rkT, 1)
                            spread(n, 0)
                            spread(n, 1)
                            past(act, s.pT_ps, n * 3)
                            for c in range(HC):
                                exps(n, k, c)
                                if c + 2 < HC:
                                    spread(n, c + 2)
                            if is_in(j + 2):
                                rows_T(n + 2, k)
                                key_squares(n + 2, 0)
                            probs_T(n)
                            if is_in(j + 2):
                                key_squares(n + 2, 1)
                        else:
                            if j + 1 == GB and is_in(GB):
                                queries(g + 1)
                            if is_in(j + 1):
                                past(act, s.pT_ps, n * 3)
                                for c in range(HC):
                                    exps(n + 1, 1 - k, c)
                            probs_T(n)
                            if is_in(j + 2):
                                rows_T(n + 2, k)
                        mixed(n, j)
                    if keyed and is_in(GB):
                        queries(g + 1)
                    for i in range(0, NP_ // 2, 2):
                        act.wait_ge(s.o_ps, g * (NP_ // 2) + (i + 1))
                        nc.scalar.copy(m.oT[:, 2 * i:2 * i + 2, :], kit.psum(2 + i % 2).rearrange("p (a t) -> p a t", a=2)).then_inc(s.o_act, 1)

                for n in range(2):
                    rows_T(n, n)
                    if keyed:
                        key_squares(n, 0)
                        key_squares(n, 1)
                queries(0)
                if not keyed:
                    for c in range(HC):
                        exps(0, 0, c)
                groups(act, group)

            @block.tensor
            def _(pe):
                def rows_T(n, k, b, loads):
                    if keyed:
                        pe.wait_ge(s.rows, (n + 1) * KF)
                    pe.wait_ge(rows_in[b], loads * row_loads)
                    past(pe, s.rT, n)
                    for f in range(FC):
                        for c, (a, size) in enumerate(TILES):
                            mm = nc.tensor.transpose(kit.psum(f)[:, a:a + size], m.rows[0:size, b, c, f * P:(f + 1) * P], kit.ident[0:size, 0:size])
                    mm.then_inc(s.rT_ps, 1)

                def keys(n, k, c):
                    pe.wait_ge(s.rT, n + 1)
                    for half in range(2):
                        i = 2 * c + half
                        past(pe, s.k_sq, n * 4 + (i - 1))
                        for f in range(FC):
                            mm = nc.tensor.matmul(kit.psum(2 + half), m.rowsT[:, k, f, c * P:(c + 1) * P], mk.wk[:, f, half * 512:(half + 1) * 512],
                                                  start=(f == 0), stop=(f == FC - 1))
                        mm.then_inc(s.k_ps, 1)

                def scores(n, k, j):
                    if keyed:
                        pe.wait_ge(s.rk, n + 1)
                        for c in range(KF):
                            mm = nc.tensor.transpose(kit.psum(6)[0:H, c * P:(c + 1) * P], mk.rk[:, k, c * H:(c + 1) * H], kit.ident[:])
                        mm.then_inc(s.rkT_ps, 1)
                    else:
                        pe.wait_ge(s.rT, n + 1)
                    for c in range(HC):
                        if keyed:
                            if c == 0:
                                pe.wait_ge(s.rkT, n + 1)
                                pe.wait_ge(s.rkT_tail, n + 1)
                                pe.wait_ge(s.mask, (n + 1) * 2)
                                past(pe, s.mix0, n)
                            if c >= 2:
                                pe.wait_ge(s.rkb, n * HC + (c - 1))
                            nc.tensor.matmul(kit.psum(spread_bank[c])[:, 0:NK], mk.sel[:, c, :], mk.rkT[:], start=True, stop=True).then_inc(s.rkb_ps, 1)
                            if c >= 2:
                                pe.wait_ge(s.score, n * HC + (c - 1))
                            if c == 1:
                                past(pe, s.mix1, n)
                        else:
                            past(pe, s.p, n * HC + (c - 1))
                        for f in range(FC):
                            mm = nc.tensor.matmul(kit.psum(score_bank[c])[:, 0:NK], m.qk[:, f, j % GB, c * BT:(c + 1) * BT, :].rearrange("p h q -> p (h q)"),
                                                  m.rowsT[:, k, f, :], start=(f == 0), stop=(f == FC - 1 and not keyed))
                        if keyed:
                            mm = nc.tensor.matmul(kit.psum(score_bank[c])[:, 0:NK], mk.one[:], mk.mask[:, k, :], start=False, stop=True)
                        mm.then_inc(s.s_ps, 1)

                def probs_T(n, k):
                    pe.wait_ge(s.normed, (n + 1) * HC)
                    if not keyed:
                        past(pe, s.mix1, n)
                    for t, (a, size) in enumerate(TILES):
                        for c in range(HC):
                            mm = nc.tensor.transpose(kit.psum(prob_bank[t])[0:size, c * P:(c + 1) * P], m.prob[:, k % PB, c, a:a + size], kit.ident[:])
                        mm.then_inc(s.pT_ps, 1)

                def mix(n, b):
                    pe.wait_ge(s.pT, (n + 1) * 2)
                    pe.wait_ge(s.pT1, n + 1)
                    if not keyed:
                        past(pe, s.mix0, n)
                    for f in range(FC):
                        for t, (a, size) in enumerate(TILES):
                            mm = nc.tensor.matmul(kit.psum(mix_bank[f]), m.rows[0:size, b, t, f * P:(f + 1) * P], m.probT[0:size, t, :],
                                                  start=(t == 0), stop=(t == len(TILES) - 1))
                        mm.then_inc(s.mix_ps, 1)

                def queries(g):
                    pe.wait_ge(s.q_in, (g + 1) * 16)
                    if keyed:
                        pe.wait_ge(s.k_sq, g * (GB * 4) + 8)
                    for i in range(H):
                        if i >= 2:
                            pe.wait_ge(s.qk_dve if i % 2 else s.qk_act, g * (H // 2) + i // 2)
                        pr, half = i // 2, i % 2
                        for f in range(FC):
                            mm = nc.tensor.matmul(kit.psum(2 + i % 2)[:, f * GT:(f + 1) * GT], m.wkT[half * DH:(half + 1) * DH, pr, f * P:(f + 1) * P],
                                                  m.qT[half * DH:(half + 1) * DH, pr, :], start=True, stop=True)
                        mm.then_inc(s.qk_ps, 1)
                    pe.wait_ge(s.qk_act, (g + 1) * (H // 2))
                    pe.wait_ge(s.qk_dve, (g + 1) * (H // 2))
                    pe.sem_inc(s.qk_free, 1)

                def project(g, more):
                    pe.wait_ge(s.mix0, (g + 1) * GB)
                    pe.wait_ge(s.mix1, (g + 1) * GB)
                    for i in range(NP_ // 2):
                        if i >= 2:
                            pe.wait_ge(s.o_dve if i % 2 else s.o_act, g * (NP_ // 4) + i // 2)
                        for pr in (2 * i, 2 * i + 1):
                            for half in range(2):
                                h = 2 * pr + half
                                for f in range(FC):
                                    mm = nc.tensor.matmul(kit.psum(2 + i % 2)[half * DH:(half + 1) * DH, (pr % 2) * GT:(pr % 2 + 1) * GT],
                                                          m.wv[:, f, h * DH:(h + 1) * DH], m.mix[:, f, h, :], start=(f == 0), stop=(f == FC - 1),
                                                          skip_group_check=True)
                        mm.then_inc(s.o_ps, 1)
                    pe.wait_ge(s.o_act, (g + 1) * (NP_ // 4))
                    pe.wait_ge(s.o_dve, (g + 1) * (NP_ // 4))
                    pe.wait_ge(s.rT, (g + 1) * GB + (2 if more else 0))
                    for i in range(GT // P):
                        for pr in range(NP_):
                            mm = nc.tensor.matmul(kit.psum(i)[:, 0:D], m.oT[:, pr, i * P:(i + 1) * P], m.wo[:, pr, :], start=(pr == 0), stop=(pr == NP_ - 1))
                        mm.then_inc(s.x_ps, 1)

                def group(g, is_in):
                    for j in range(GB):
                        n, k, b = g * GB + j, j % 2, j % RB
                        if keyed:
                            scores(n, k, j)
                        else:
                            if j + 1 == GB and is_in(GB):
                                queries(g + 1)
                            if is_in(j + 1):
                                scores(n + 1, 1 - k, j + 1)
                            probs_T(n, k)
                        if j == 0:
                            pe.wait_ge(s.x_add, g * (GT // P) + 1)
                        if is_in(j + 2):
                            rows_T(n + 2, k, (j + 2) % RB, uses(g, j + 2, RB))
                        if keyed:
                            if is_in(j + 2):
                                keys(n + 2, k, 0)
                            probs_T(n, k)
                            if is_in(j + 2):
                                keys(n + 2, k, 1)
                        mix(n, b)
                    if keyed and is_in(GB):
                        queries(g + 1)
                    project(g, is_in(GB))

                pe.wait_ge(s.w_in, n_weights)
                pe.wait_ge(s.wkT, 1)
                if keyed:
                    pe.wait_ge(s.set, 2)
                for n in range(2):
                    rows_T(n, n, n, 1)
                    if keyed:
                        keys(n, n, 0)
                        keys(n, n, 1)
                queries(0)
                if not keyed:
                    scores(0, 0, 0)
                groups(pe, group)


class Norm:

    def __init__(self, kit, stage, stack):
        self.kit, self.nc = kit, kit.nc
        self.m = kit.buffers(stack, stats=([P, NT, 6], F32), mv=([P, NT, 2], F32), rstd=([P, NT], F32))
        self.s = kit.sems(f"{stage}_norm", "stats aggr eps rstd")

    def vector_part(self, dve):
        row_stats(self.nc, dve, [self.kit.X[:, t, :] for t in range(NT)], self.m.stats, self.m.mv, self.s.stats, self.s.aggr)
        dve.wait_ge(self.s.rstd, 1)

    def pool_part(self, pool):
        pool.wait_ge(self.s.aggr, NT)
        inv_root(self.nc, pool, self.kit.neg_half[:, 0:NT], self.m.rstd[:], self.m.mv[:, :, 1], 1.0, LN_EPS, ALU.add, self.s.eps, 1, self.s.rstd)

    def rows(self, out, n):
        return self.nc.vector.tensor_scalar(out, self.kit.X[:, n, :], self.m.mv[:, n, 0:1], self.m.rstd[:, bass.ds(n, 1)], ALU.subtract, ALU.mult)


def plain_queries(kit, stage, w_q):
    nc, d = kit.nc, kit.dram
    GQ = 512
    with kit.stage() as st:
        norm = Norm(kit, stage, st)
        m = kit.buffers(st, wq=([P, FC, INNER], F32), xl=([P, 2, D], F32), xlT=([P, FC, B * S], F32), qT=([P, 2, NP_, GQ], F32))
        s = kit.sems(stage, "w_in xl xlT_ps xlT q_ps q_act q_dve")
        stored = kit.pair(stage, "stored")
        with nc.Block() as block:
            @block.sync
            def _(sp):
                sp.dma_start(m.wq[:], w_q.rearrange("(f p) n -> p f n", p=P)).then_inc(s.w_in, 16)
                with sp.Fori(0, B * S // GQ // 2) as u:
                    for k in range(2):
                        g = u * 2 + k
                        sp.wait_ge(s.q_act, g * 4 + 4)
                        sp.wait_ge(s.q_dve, g * 4 + 4)
                        sp.dma_start(d.qT[:, :, bass.ts(g, GQ)], m.qT[:, k]).then_inc(stored[k], 16)
                for k in range(2):
                    sp.wait_ge(stored[k], 16 * (B * S // GQ // 2 + 1))

            @block.vector
            def _(dve):
                for k in range(2):
                    dve.sem_inc(stored[k], 16)
                norm.vector_part(dve)
                with dve.Fori(0, NT // 2) as u:
                    for k in range(2):
                        n = u * 2 + k
                        dve.wait_ge(s.xlT_ps, u * 2 + max(k - 1, 0))
                        norm.rows(m.xl[:, k, :], n).then_inc(s.xl, 1)
                with dve.Fori(0, B * S // GQ // 2) as u:
                    for k in range(2):
                        g = u * 2 + k
                        dve.wait_ge(stored[k], u * 16 + 16)
                        for i in range(1, NP_, 2):
                            dve.wait_ge(s.q_ps, g * NP_ + (i + 1))
                            nc.vector.tensor_copy(m.qT[:, k, i, :], kit.psum(i)).then_inc(s.q_dve, 1)

            @block.gpsimd
            def _(pool):
                norm.pool_part(pool)

            @block.scalar
            def _(act):
                with act.Fori(0, NT // 2) as u:
                    for k in range(2):
                        n = u * 2 + k
                        act.wait_ge(s.xlT_ps, n + 1)
                        nc.scalar.copy(m.xlT[:, :, bass.ts(n, P)], kit.psum(k)[:, 0:D].rearrange("p (f t) -> p f t", f=FC)).then_inc(s.xlT, 1)
                with act.Fori(0, B * S // GQ // 2) as u:
                    for k in range(2):
                        g = u * 2 + k
                        act.wait_ge(stored[k], u * 16 + 16)
                        for i in range(0, NP_, 2):
                            act.wait_ge(s.q_ps, g * NP_ + (i + 1))
                            nc.scalar.copy(m.qT[:, k, i, :], kit.psum(i)).then_inc(s.q_act, 1)

            @block.tensor
            def _(pe):
                with pe.Fori(0, NT // 2) as u:
                    for k in range(2):
                        n = u * 2 + k
                        pe.wait_ge(s.xl, n + 1)
                        pe.wait_ge(s.xlT, u * 2 + max(k - 1, 0))
                        for f in range(FC):
                            mm = nc.tensor.transpose(kit.psum(k)[:, f * P:(f + 1) * P], m.xl[:, k, f * P:(f + 1) * P], kit.ident[:])
                        mm.then_inc(s.xlT_ps, 1)
                pe.wait_ge(s.xlT, NT)
                pe.wait_ge(s.w_in, 16)
                with pe.Fori(0, B * S // GQ) as g:
                    for i in range(NP_):
                        pe.wait_ge(s.q_dve if i % 2 else s.q_act, g * 4)
                        for f in range(FC):
                            mm = nc.tensor.matmul(kit.psum(i), m.wq[:, f, i * P:(i + 1) * P], m.xlT[:, f, bass.ts(g, GQ)], start=(f == 0), stop=(f == FC - 1))
                        mm.then_inc(s.q_ps, 1)


def rotary_weights(kit, m, w, wo, stage):
    nc, d = kit.nc, kit.dram
    with kit.stage() as st:
        t = kit.buffers(
            st, cw=([P, 6, D], F32), cb=([P, 6], F32), cbb=([P, 6, P], F32), bd=([P, 2, 8, 32], F32), bdv=([P, P], F32), blk=([P, P], F32),
            kvr=([32, 8, 16], F32), lor=([32, 8, 16], F32), kvb=([32, 1], F32), kvbb=([32, P], F32), qlb=([P, 32], F32), klb=([P, 32], F32), lob=([P, 16], F32))
        s = kit.sems(stage + "w", "zero w_in m2_ps bdv cbb out_ps out ready")
        with nc.Block() as block:
            n_in = 0

            @block.sync
            def _(sp):
                sp.wait_ge(s.zero, 2)
                for src, dst in ((d.cw.rearrange("(c p) n -> p c n", p=P), t.cw[:]), (d.cb, t.cb[:]),
                                 (d.blk, t.blk[:]), (d.kvb.unsqueeze(1), t.kvb[:]),
                                 (d.kv2l.unsqueeze(1).to_broadcast([32, 8, 16]), t.kvr[:]), (d.l2oT.unsqueeze(1).to_broadcast([32, 8, 16]), t.lor[:]),
                                 (d.q2lb.partition_broadcast(P), t.qlb[:]), (d.kvb.partition_broadcast(P), t.klb[:]), (d.l2ob.partition_broadcast(P), t.lob[:]),
                                 (d.cprojT.rearrange("(f p) n -> p f n", p=P), wo[:]), (d.cprojb.partition_broadcast(P), m.bo[:]),
                                 (d.cos, m.cos[:]), (d.sin, m.sin[:]), (d.causal, m.causal[:])):
                    sp.dma_start(dst, src).then_inc(s.w_in, 16)
                for j in range(8):
                    sp.dma_start(t.bd[16 * j:16 * j + 16, 0, j, :], d.q2lT).then_inc(s.w_in, 16)
                    sp.dma_start(t.bd[16 * j:16 * j + 16, 1, j, :], d.kv2lT).then_inc(s.w_in, 16)
                for j in range(4):
                    sp.dma_start(m.wqk[32 * j:32 * j + 32, 32 * j:32 * j + 32], d.wqkT).then_inc(s.w_in, 16)
                    sp.dma_start(m.wqkb[32 * j:32 * j + 32, :], d.wqkb.unsqueeze(1)).then_inc(s.w_in, 16)
            n_in = 16 * (14 + 16 + 8)

            @block.vector
            def _(dve):
                nc.vector.memset(t.bd[:], 0.0).then_inc(s.zero, 1)
                nc.vector.memset(m.wqk[:], 0.0).then_inc(s.zero, 1)
                dve.wait_ge(s.w_in, n_in)
                nc.vector.tensor_copy(t.cbb[:], t.cb[:].unsqueeze(2).to_broadcast([P, 6, P])).then_inc(s.cbb, 1)
                nc.vector.tensor_copy(t.kvbb[:], t.kvb[:].to_broadcast([32, P])).then_inc(s.cbb, 1)
                dve.wait_ge(s.m2_ps, 1)
                nc.vector.tensor_tensor(t.bdv[:], kit.psum(0)[:, 0:P], t.blk[:], ALU.mult).then_inc(s.bdv, 1)
                for f in range(FC):
                    dve.wait_ge(s.out_ps, f + 1)
                    nc.vector.tensor_copy(w[:, f, 0:512], kit.psum(3 * f + 1)).then_inc(s.out, 1)
                    nc.vector.tensor_copy(w[:, f, 512:1024], kit.psum(3 * f + 2)).then_inc(s.out, 1)
                    nc.vector.tensor_copy(w[:, f, 1024:1280], kit.psum(3 * f + 3)[:, 0:256]).then_inc(s.out, 1)
                dve.wait_ge(s.out_ps, FC + 1)
                nc.vector.tensor_tensor(m.b[:, 0:512].rearrange("p (h l) -> p h l", l=32), kit.psum(1).rearrange("p (h l) -> p h l", l=32),
                                        t.qlb[:].unsqueeze(1).to_broadcast([P, 16, 32]), ALU.add).then_inc(s.ready, 1)
                nc.vector.tensor_tensor(m.b[:, 512:1024].rearrange("p (h l) -> p h l", l=32), kit.psum(2).rearrange("p (h l) -> p h l", l=32),
                                        t.klb[:].unsqueeze(1).to_broadcast([P, 16, 32]), ALU.add).then_inc(s.ready, 1)
                nc.vector.tensor_tensor(m.b[:, 1024:1280].rearrange("p (h l) -> p h l", l=16), kit.psum(3)[:, 0:256].rearrange("p (h l) -> p h l", l=16),
                                        t.lob[:].unsqueeze(1).to_broadcast([P, 16, 16]), ALU.add).then_inc(s.ready, 1)
                dve.wait_ge(s.ready, 3)

            @block.tensor
            def _(pe):
                pe.wait_ge(s.w_in, n_in)
                nc.tensor.matmul(kit.psum(0)[:, 0:P], t.kvr[:].rearrange("p a b -> p (a b)"), t.lor[:].rearrange("p a b -> p (a b)"),
                                 start=True, stop=True).then_inc(s.m2_ps, 1)
                pe.wait_ge(s.bdv, 1)

                def rows(c):
                    return t.bdv[:] if c >= 4 else t.bd[:, c // 2].rearrange("p a b -> p (a b)")

                for f in range(FC):
                    for c in range(6):
                        wide = P if c >= 4 else 256
                        mm = nc.tensor.matmul(kit.psum(3 * f + 1 + c // 2)[:, (c % 2) * wide:(c % 2 + 1) * wide], t.cw[:, c, f * P:(f + 1) * P], rows(c),
                                              start=True, stop=True)
                    mm.then_inc(s.out_ps, 1)
                pe.wait_ge(s.out, 3)
                pe.wait_ge(s.cbb, 2)
                for c in range(6):
                    wide = P if c >= 4 else 256
                    out = kit.psum(1 + c // 2)[:, (c % 2) * wide:(c % 2 + 1) * wide]
                    mm = nc.tensor.matmul(out, t.cbb[:, c, :], rows(c), start=True, stop=(c < 4))
                    if c >= 4:
                        mm = nc.tensor.matmul(out, t.kvbb[:], t.lor[:].rearrange("p a b -> p (a b)"), start=False, stop=True)
                mm.then_inc(s.out_ps, 1)


def self_attention(kit, stage, rotary):
    nc, d = kit.nc, kit.dram
    X = kit.X
    WIDE = 1280 if rotary else 768
    HF = H // FC
    EV = D // H
    with kit.stage() as st:
        m = kit.buffers(
            st, w=([P, FC, WIDE], F32), wo=([P, FC, D], F32), xl=([P, 2, D], F32), xlT=([P, 2, FC, P], F32),
            qk=([P, 2, 2 * H, S], F32), v=([P, 2, FC, HF * (P + EV)], F32), qT=([P, 512], F32), kT=([P, HC, BT, P], F32), score=([P, H, S], F32), top=([P, H], F32),
            prob=([P, H, S], F32), mass=([P, H], F32), rmass=([P, H], F32), spread=([P, H, P], F32), yT=([P, FC, P], F32))
        if rotary:
            r = kit.buffers(st, b=([P, WIDE], F32), bo=([P, D], F32), cos=([P, 16], F32), sin=([P, 2, 16], F32), causal=([P, S], F32), wqk=([P, P], F32),
                            wqkb=([P, 1], F32), lat=([P, 2 * H, S], F32), turn=([P, 2 * H, S], F32), qrT=([P, 512], F32))
            rotary_weights(kit, r, m.w, m.wo, stage)
        else:
            r = kit.buffers(st, raw=([P, 512], F32), sq=([P, 512], F32), ss=([P, 2 * H], F32), rss=([P, 2, 2 * H], F32), gq=([P, 2, 16], F32), gain=([P, 16], F32))
        norm = Norm(kit, stage, st)
        s = kit.sems(stage, "w_in zero gain xl xlT_ps xlT qk_ps raw_q sq v ss scaled rss qk_n qk lat turned cosed qT_ps qT kT_act kT_dve qrT_ps qrT s_ps cut_act cut_dve masked "
                     "top shift p mass rmass prob spread y_ps yT o_ps x_add passed")

        def own(v, f):
            return v[:, f, :].rearrange("p (h c) -> p h c", h=HF)[:, :, 0:EV]

        def values(buffer, f):
            return buffer[:, f * HF * EV:(f + 1) * HF * EV].rearrange("p (h e) -> p h e", h=HF)

        def steps(engine, step):
            with engine.Fori(0, NT // 2 - 2) as u:
                for k in range(2):
                    step(u * 2 + k, k, 3)
            for n in range(NT - 4, NT):
                step(n, n % 2, NT - 1 - n)

        def past(engine, sem, value):
            if not isinstance(value, int) or value > 0:
                engine.wait_ge(sem, value)

        with nc.Block() as block:
            @block.sync
            def _(sp):
                if not rotary:
                    for i, w in enumerate((d.WqT, d.WkT0, d.WvT)):
                        sp.dma_start(m.w[:, :, i * D:(i + 1) * D], w.rearrange("(f p) n -> p f n", p=P)).then_inc(s.w_in, 16)
                    sp.dma_start(m.wo[:], d.WoT.rearrange("(f p) n -> p f n", p=P)).then_inc(s.w_in, 16)
                    sp.dma_start(r.gq[:, 0, :], d.qn_w.partition_broadcast(P)).then_inc(s.w_in, 16)
                    sp.dma_start(r.gq[:, 1, :], d.kn_w.partition_broadcast(P)).then_inc(s.w_in, 16)
            n_w = 0 if rotary else 96

            @block.vector
            def _(dve):
                nc.vector.memset(m.spread[:], 0.0).then_inc(s.zero, 1)
                nc.vector.memset(m.v[:], 0.0).then_inc(s.zero, 1)
                nc.vector.memset(m.kT[:], 0.0).then_inc(s.zero, 1)
                n_zero = 3
                if not rotary:
                    nc.vector.memset(m.qk[:], 0.0).then_inc(s.zero, 1)
                    n_zero = 4
                    dve.wait_ge(s.w_in, n_w)
                    nc.vector.scalar_tensor_tensor(r.gain[:], r.gq[:, 0, :], 16 ** -0.5, r.gq[:, 1, :], ALU.mult, ALU.mult).then_inc(s.gain, 1)
                    dve.wait_ge(s.gain, 1)
                dve.wait_ge(s.zero, n_zero)
                norm.vector_part(dve)

                def rows(n, k):
                    past(dve, s.xlT_ps, n + (-1) if not isinstance(n, int) else n - 1)
                    norm.rows(m.xl[:, k, :], n).then_inc(s.xl, 1)

                def inner(n, k):
                    if rotary:
                        dve.wait_ge(s.qk_ps, n + 1)
                        nc.vector.tensor_tensor(r.lat[:].rearrange("p h l -> p (h l)"), kit.bank[2][:].rearrange("p a t -> p (a t)"), r.b[:, 0:1024], ALU.add).then_inc(s.lat, 1)
                        dve.wait_ge(s.lat, n + 1)
                        nc.vector.tensor_tensor(m.qk[:, k].rearrange("p h (i e) -> p h i e", e=2), r.lat[:].rearrange("p h (i e) -> p h i e", e=2),
                                                r.cos[:].unsqueeze(1).unsqueeze(3).to_broadcast([P, 32, 16, 2]), ALU.mult).then_inc(s.cosed, 1)
                    else:
                        dve.wait_ge(s.sq, n + 1)
                        nc.vector.tensor_reduce(r.ss[:], r.sq[:].rearrange("p (h e) -> p h e", e=16), AX.X, ALU.add).then_inc(s.ss, 1)

                def value_rows(n, k):
                    if rotary:
                        dve.wait_ge(s.qk_ps, n + 1)
                        past(dve, s.y_ps, n + (-1) if not isinstance(n, int) else n - 1)
                        for f in range(FC):
                            nc.vector.tensor_tensor(own(m.v[:, k], f), values(kit.psum(7), f), values(r.b[:, 1024:1280], f), ALU.add).then_inc(s.v, 1)

                def queries_keys(n, k):
                    if rotary:
                        dve.wait_ge(s.cosed, n + 1)
                        dve.wait_ge(s.turned, n * 2 + 2)
                        nc.vector.tensor_tensor(m.qk[:, k], m.qk[:, k], r.turn[:], ALU.add).then_inc(s.qk, 1)
                    else:
                        dve.wait_ge(s.raw_q, n + 1)
                        dve.wait_ge(s.rss, n + 1)
                        nc.vector.tensor_tensor(m.qk[:, k, :, 0:16], r.raw[:].rearrange("p (h e) -> p h e", e=16),
                                                r.rss[:, k, :].unsqueeze(2).to_broadcast([P, 32, 16]), ALU.mult).then_inc(s.qk_n, 1)
                        dve.wait_ge(s.qk_n, n + 1)
                        nc.vector.tensor_tensor(m.qk[:, k, 0:H, 0:16], m.qk[:, k, 0:H, 0:16], r.gain[:].unsqueeze(1).to_broadcast([P, H, 16]), ALU.mult).then_inc(s.qk, 1)

                def keys_T(n):
                    dve.wait_ge(s.qT_ps, n * 2 + 2)
                    past(dve, s.s_ps, n)
                    for j in range(2, BT):
                        rows = slice(j * S, (j + 1) * S)
                        nc.vector.tensor_copy(m.kT[rows, :, j, :], kit.psum(3)[rows].rearrange("p (c t) -> p c t", c=HC)).then_inc(s.kT_dve, 1)

                def queries_T(n):
                    if rotary:
                        dve.wait_ge(s.qrT_ps, n + 1)
                        nc.vector.tensor_scalar(m.qT[:], kit.psum(2), r.wqkb[:], 32 ** -0.5, ALU.add, ALU.mult).then_inc(s.qT, 1)

                def cut(n):
                    dve.wait_ge(s.s_ps, n + 1)
                    for j in range(2, BT):
                        rows = slice(j * S, (j + 1) * S)
                        for i in range(2):
                            nc.vector.tensor_copy(m.score[rows, i * 8:i * 8 + 8, :].rearrange("p (c r) k -> p c r k", c=2),
                                                  kit.bank[2 + i][rows].rearrange("p c (r k) -> p c r k", r=BT)[:, :, :, rows]).then_inc(s.cut_dve, 1)

                def softmax(n):
                    if rotary:
                        dve.wait_ge(s.masked, n + 1)
                    else:
                        dve.wait_ge(s.cut_act, (n + 1) * 4)
                        dve.wait_ge(s.cut_dve, (n + 1) * 4)
                    nc.vector.tensor_reduce(m.top[:], m.score[:], AX.X, ALU.max).then_inc(s.top, 1)
                    dve.wait_ge(s.top, n + 1)
                    nc.vector.tensor_tensor(m.score[:], m.score[:], m.top[:].unsqueeze(2).to_broadcast([P, H, S]), ALU.subtract).then_inc(s.shift, 1)
                    dve.wait_ge(s.p, n + 1)
                    nc.vector.tensor_reduce(m.mass[:], m.prob[:], AX.X, ALU.add).then_inc(s.mass, 1)
                    dve.wait_ge(s.mass, n + 1)
                    nc.vector.reciprocal(m.rmass[:], m.mass[:]).then_inc(s.rmass, 1)
                    dve.wait_ge(s.rmass, n + 1)
                    nc.vector.tensor_tensor(m.prob[:], m.prob[:], m.rmass[:].unsqueeze(2).to_broadcast([P, H, S]), ALU.mult).then_inc(s.prob, 1)
                    dve.wait_ge(s.prob, n + 1)
                    past(dve, s.y_ps, n)
                    for j in range(BT):
                        rows = slice(j * S, (j + 1) * S)
                        nc.vector.transpose(m.spread[rows, :, rows], m.prob[rows]).then_inc(s.spread, 1)

                def add(n):
                    dve.wait_ge(s.o_ps, n + 1)
                    nc.vector.tensor_tensor(X[:, n, :], X[:, n, :], kit.psum(0)[:, D:2 * D], ALU.add).then_inc(s.x_add, 1)

                def step(n, k, ahead):
                    softmax(n)
                    if ahead >= 1:
                        queries_T(n + 1)
                    if ahead >= 2:
                        inner(n + 2, k)
                        value_rows(n + 2, k)
                    if ahead >= 3:
                        rows(n + 3, 1 - k)
                    if ahead >= 1:
                        cut(n + 1)
                    if ahead >= 2:
                        queries_keys(n + 2, k)
                        keys_T(n + 2)
                    add(n)

                rows(0, 0)
                rows(1, 1)
                inner(0, 0)
                value_rows(0, 0)
                queries_keys(0, 0)
                rows(2, 0)
                keys_T(0)
                inner(1, 1)
                value_rows(1, 1)
                queries_T(0)
                cut(0)
                queries_keys(1, 1)
                keys_T(1)
                steps(dve, step)
                if rotary:
                    dve.wait_ge(s.x_add, NT)
                    nc.vector.tensor_tensor(X[:], X[:], r.bo[:].unsqueeze(1).to_broadcast([P, NT, D]), ALU.add).then_inc(s.x_add, 1)
                    dve.wait_ge(s.x_add, NT + 1)

            @block.gpsimd
            def _(pool):
                norm.pool_part(pool)

                def inner(n, k):
                    if rotary:
                        pool.wait_ge(s.lat, n + 1)
                        past(pool, s.qk, n)
                        lat, turn = (x[:].rearrange("p h (i e) -> p h i e", e=2) for x in (r.lat, r.turn))
                        for e in range(2):
                            nc.gpsimd.tensor_tensor(turn[:, :, :, e], lat[:, :, :, 1 - e], r.sin[:, e, :].unsqueeze(1).to_broadcast([P, 32, 16]), ALU.mult).then_inc(s.turned, 1)
                    else:
                        hold(pool, s.ss, n + 1, s.passed)
                        inv_root(nc, pool, kit.neg_half[:, 0:32], r.rss[:, k, :], r.ss[:], 1.0 / 16, float(np.finfo(np.float32).eps), ALU.add, s.scaled, n + 1, s.rss)

                def mask(n):
                    if rotary:
                        pool.wait_ge(s.cut_act, (n + 1) * 4)
                        pool.wait_ge(s.cut_dve, (n + 1) * 4)
                        nc.gpsimd.tensor_tensor(m.score[:], m.score[:], r.causal[:].unsqueeze(1).to_broadcast([P, H, S]), ALU.add).then_inc(s.masked, 1)

                def step(n, k, ahead):
                    if ahead >= 2:
                        inner(n + 2, k)
                    if ahead >= 1:
                        mask(n + 1)

                inner(0, 0)
                inner(1, 1)
                mask(0)
                steps(pool, step)

            @block.scalar
            def _(act):
                def norm_T(n, k):
                    act.wait_ge(s.xlT_ps, n + 1)
                    nc.scalar.copy(m.xlT[:, k].rearrange("p f t -> p (f t)"), kit.psum(0)[:, 0:D]).then_inc(s.xlT, 1)

                def inner(n, k):
                    if not rotary:
                        act.wait_ge(s.qk_ps, n + 1)
                        past(act, s.qk, n)
                        nc.scalar.activation(r.sq[:], kit.psum(4), ACT.Square).then_inc(s.sq, 1)
                        nc.scalar.copy(r.raw[:], kit.psum(4)).then_inc(s.raw_q, 1)

                def value_rows(n, k):
                    if not rotary:
                        if isinstance(n, int) and n < 2:
                            act.wait_ge(s.zero, 4)
                        past(act, s.y_ps, n + (-1) if not isinstance(n, int) else n - 1)
                        for f in range(FC):
                            nc.scalar.copy(own(m.v[:, k], f), values(kit.psum(7), f)).then_inc(s.v, 1)

                def queries_keys_T(n):
                    act.wait_ge(s.qT_ps, n * 2 + 1)
                    past(act, s.s_ps, n)
                    if rotary:
                        nc.scalar.copy(r.qrT[:], kit.psum(2)).then_inc(s.qrT, 1)
                    else:
                        nc.scalar.copy(m.qT[:], kit.psum(2)).then_inc(s.qT, 1)
                    act.wait_ge(s.qT_ps, n * 2 + 2)
                    for j in range(2):
                        rows = slice(j * S, (j + 1) * S)
                        nc.scalar.copy(m.kT[rows, :, j, :], kit.psum(3)[rows].rearrange("p (c t) -> p c t", c=HC)).then_inc(s.kT_act, 1)

                def cut(n):
                    act.wait_ge(s.s_ps, n + 1)
                    past(act, s.p, n)
                    for j in range(2):
                        rows = slice(j * S, (j + 1) * S)
                        for i in range(2):
                            nc.scalar.copy(m.score[rows, i * 8:i * 8 + 8, :].rearrange("p (c r) k -> p c r k", c=2),
                                           kit.bank[2 + i][rows].rearrange("p c (r k) -> p c r k", r=BT)[:, :, :, rows]).then_inc(s.cut_act, 1)

                def exps(n):
                    act.wait_ge(s.shift, n + 1)
                    nc.scalar.activation(m.prob[:].rearrange("p h k -> p (h k)"), m.score[:].rearrange("p h k -> p (h k)"), ACT.Exp).then_inc(s.p, 1)

                def step(n, k, ahead):
                    exps(n)
                    if ahead >= 2:
                        inner(n + 2, k)
                    act.wait_ge(s.y_ps, n + 1)
                    past(act, s.o_ps, n)
                    nc.scalar.copy(m.yT[:].rearrange("p f t -> p (f t)"), kit.psum(1)[:, 0:D]).then_inc(s.yT, 1)
                    if ahead >= 2:
                        value_rows(n + 2, k)
                    if ahead >= 1:
                        cut(n + 1)
                    if ahead >= 3:
                        norm_T(n + 3, 1 - k)
                    if ahead >= 2:
                        queries_keys_T(n + 2)

                norm_T(0, 0)
                inner(0, 0)
                value_rows(0, 0)
                norm_T(1, 1)
                queries_keys_T(0)
                inner(1, 1)
                value_rows(1, 1)
                cut(0)
                norm_T(2, 0)
                queries_keys_T(1)
                steps(act, step)

            @block.tensor
            def _(pe):
                if not rotary:
                    pe.wait_ge(s.w_in, n_w)

                def norm_T(n, k):
                    pe.wait_ge(s.xl, n + 1)
                    past(pe, s.x_add, n - 3 if isinstance(n, int) else n + (-3))
                    for f in range(FC):
                        mm = nc.tensor.transpose(kit.psum(0)[:, f * P:(f + 1) * P], m.xl[:, k, f * P:(f + 1) * P], kit.ident[:])
                    mm.then_inc(s.xlT_ps, 1)

                def project(n, k):
                    pe.wait_ge(s.xlT, n + 1)
                    past(pe, s.lat if rotary else s.raw_q, n)
                    past(pe, s.v, n * FC)
                    for sem in (s.cut_act, s.cut_dve):
                        past(pe, sem, (n - 1) * 4 if isinstance(n, int) else n * 4 + (-4))
                    parts = ((4, 0, 512), (5, 512, 512), (7, 1024, 256)) if rotary else ((4, 0, 512), (7, 512, 256))
                    for bank, at, wide in parts:
                        for f in range(FC):
                            mm = nc.tensor.matmul(kit.psum(bank)[:, 0:wide], m.xlT[:, k, f, :], m.w[:, f, at:at + wide], start=(f == 0), stop=(f == FC - 1))
                    mm.then_inc(s.qk_ps, 1)

                def queries_keys_T(n, k):
                    pe.wait_ge(s.qk, n + 1)
                    for i in range(2):
                        for c in range(HC):
                            mm = nc.tensor.transpose(kit.psum(2 + i)[:, c * P:(c + 1) * P], m.qk[:, k, (i * HC + c) * BT:(i * HC + c + 1) * BT, :].rearrange("p h l -> p (h l)"), kit.ident[:])
                        mm.then_inc(s.qT_ps, 1)

                def latent_T(n):
                    if rotary:
                        pe.wait_ge(s.qrT, n + 1)
                        nc.tensor.matmul(kit.psum(2), r.wqk[:], r.qrT[:], start=True, stop=True).then_inc(s.qrT_ps, 1)

                def scores(n, last):
                    pe.wait_ge(s.qT, n + 1)
                    pe.wait_ge(s.kT_act, n * 2 + 2)
                    pe.wait_ge(s.kT_dve, n * 2 + 2)
                    if not last:
                        pe.wait_ge(s.lat if rotary else s.raw_q, n + 2)
                        pe.wait_ge(s.v, n * FC + 2 * FC)
                    for c in range(HC):
                        mm = nc.tensor.matmul(kit.psum(4 + c), m.qT[:, c * P:(c + 1) * P], m.kT[:, c].rearrange("p r t -> p (r t)"), start=True, stop=True)
                    mm.then_inc(s.s_ps, 1)

                def mix(n, k):
                    pe.wait_ge(s.spread, n * BT + BT)
                    past(pe, s.yT, n)
                    for h in range(H):
                        mm = nc.tensor.matmul(kit.psum(1)[:, h // HF * P:(h // HF + 1) * P], m.v[:, k, h // HF, h % HF * P:(h % HF + 1) * P], m.spread[:, h, :], start=(h % HF == 0), stop=(h % HF == HF - 1))
                    mm.then_inc(s.y_ps, 1)

                def output(n, more):
                    pe.wait_ge(s.yT, n + 1)
                    if more:
                        pe.wait_ge(s.xlT, n + 4)
                    past(pe, s.x_add, n)
                    for f in range(FC):
                        mm = nc.tensor.matmul(kit.psum(0)[:, D:2 * D], m.yT[:, f, :], m.wo[:, f, :], start=(f == 0), stop=(f == FC - 1))
                    mm.then_inc(s.o_ps, 1)

                def step(n, k, ahead):
                    if ahead >= 2:
                        project(n + 2, k)
                    if ahead >= 1:
                        latent_T(n + 1)
                    mix(n, k)
                    if ahead >= 1:
                        scores(n + 1, ahead == 1)
                    if ahead >= 3:
                        norm_T(n + 3, 1 - k)
                    if ahead >= 2:
                        queries_keys_T(n + 2, k)
                    output(n, ahead >= 3)

                norm_T(0, 0)
                project(0, 0)
                norm_T(1, 1)
                queries_keys_T(0, 0)
                project(1, 1)
                latent_T(0)
                scores(0, False)
                norm_T(2, 0)
                queries_keys_T(1, 1)
                steps(pe, step)


def tanh_map(kit):
    nc, d = kit.nc, kit.dram
    X = kit.X
    with kit.stage() as st:
        norm = Norm(kit, "map", st)
        m = kit.buffers(st, wT=([P, FC, D], F32), a1T=([P, FC, D], F32), a2=([P, FC, D], F32), a12=([P, FC, D], F32), w=([P, FC, D], F32), b=([P, D], F32),
                        xl=([P, 2, D], F32), xlT=([P, 2, FC, P], F32), h=([P, 2, D], F32), y=([P, 2, D], F32), out=([P, 2, D], F32))
        s = kit.sems("map", "w_in a12_ps a12 w_ps w xl xlT_ps xlT h_ps h y out")
        stored = kit.pair("map", "stored")
        with nc.Block() as block:
            @block.sync
            def _(sp):
                for sb, src in ((m.wT, d.weightT), (m.a1T, d.aux1T), (m.a2, d.aux2)):
                    sp.dma_start(sb[:], src.rearrange("(f p) n -> p f n", p=P)).then_inc(s.w_in, 16)
                sp.dma_start(m.b[:], d.map_b.partition_broadcast(P)).then_inc(s.w_in, 16)
                with sp.Fori(0, NT // 2) as u:
                    for k in range(2):
                        n = u * 2 + k
                        sp.wait_ge(s.out, n + 1)
                        sp.dma_start(d.out_tiles[n], m.out[:, k, :]).then_inc(stored[k], 16)
                for k in range(2):
                    sp.wait_ge(stored[k], 16 * (NT // 2 + 1))

            @block.vector
            def _(dve):
                for k in range(2):
                    dve.sem_inc(stored[k], 16)
                dve.wait_ge(s.a12_ps, 1)
                nc.vector.tensor_copy(m.a12[:], kit.psum(0).rearrange("p (f n) -> p f n", f=FC)).then_inc(s.a12, 1)
                dve.wait_ge(s.w_ps, 1)
                nc.vector.tensor_copy(m.w[:], kit.psum(1).rearrange("p (f n) -> p f n", f=FC)).then_inc(s.w, 1)
                norm.vector_part(dve)
                dve.wait_ge(s.w_in, 64)
                norm.rows(m.xl[:, 0, :], 0).then_inc(s.xl, 1)

                def tile(n, k, more):
                    if more:
                        dve.wait_ge(s.xlT_ps, n)
                        norm.rows(m.xl[:, 1 - k, :], n + 1).then_inc(s.xl, 1)
                    dve.wait_ge(s.h_ps, n + 1)
                    nc.vector.tensor_tensor(m.h[:, k, :], kit.psum(4 + k)[:, 0:D], m.b[:], ALU.add).then_inc(s.h, 1)
                    dve.wait_ge(s.y, n + 1)
                    dve.wait_ge(stored[k], stores(n, k))
                    nc.vector.tensor_tensor(m.out[:, k, :], X[:, n, :], m.y[:, k, :], ALU.add).then_inc(s.out, 1)

                def stores(n, k):
                    return (n + (2 - k)) * 8

                with dve.Fori(0, NT // 2 - 1) as u:
                    for k in range(2):
                        tile(u * 2 + k, k, True)
                tile(NT - 2, 0, True)
                tile(NT - 1, 1, False)

            @block.gpsimd
            def _(pool):
                norm.pool_part(pool)

            @block.scalar
            def _(act):
                with act.Fori(0, NT // 2) as u:
                    for k in range(2):
                        n = u * 2 + k
                        act.wait_ge(s.xlT_ps, n + 1)
                        nc.scalar.copy(m.xlT[:, k].rearrange("p f t -> p (f t)"), kit.psum(2 + k)[:, 0:D]).then_inc(s.xlT, 1)
                        act.wait_ge(s.h, n + 1)
                        nc.scalar.activation(m.y[:, k, :], m.h[:, k, :], ACT.Tanh).then_inc(s.y, 1)

            @block.tensor
            def _(pe):
                pe.wait_ge(s.w_in, 64)
                for lhsT, rhs, bank, done, ready in ((m.a1T, m.a2, 0, s.a12_ps, None), (m.wT, m.a12, 1, s.w_ps, s.a12)):
                    if ready is not None:
                        pe.wait_ge(ready, 1)
                    for i in range(FC):
                        for f in range(FC):
                            mm = nc.tensor.matmul(kit.psum(bank)[:, i * D:(i + 1) * D], lhsT[:, f, i * P:(i + 1) * P], rhs[:, f, :], start=(f == 0), stop=(f == FC - 1))
                    mm.then_inc(done, 1)
                pe.wait_ge(s.w, 1)
                with pe.Fori(0, NT // 2) as u:
                    for k in range(2):
                        n = u * 2 + k
                        pe.wait_ge(s.xl, n + 1)
                        for f in range(FC):
                            mm = nc.tensor.transpose(kit.psum(2 + k)[:, f * P:(f + 1) * P], m.xl[:, k, f * P:(f + 1) * P], kit.ident[:])
                        mm.then_inc(s.xlT_ps, 1)
                        pe.wait_ge(s.xlT, n + 1)
                        for f in range(FC):
                            mm = nc.tensor.matmul(kit.psum(4 + k)[:, 0:D], m.xlT[:, k, f, :], m.w[:, f, :], start=(f == 0), stop=(f == FC - 1))
                        mm.then_inc(s.h_ps, 1)


E_, TOPK, CAP = 64, 8, 128
I_, IS = 128, 512
ROUTED = D + E_
GS = 512


def mixture(kit):
    nc, d = kit.nc, kit.dram
    X = kit.X
    with kit.stage() as st:
        kept = kit.buffers(st, token=([CAP, E_], U32), address=([P, NT, TOPK], U32))
        route(kit, kept)
        experts(kit, kept)


def route(kit, kept):
    nc, d = kit.nc, kit.dram
    X = kit.X
    with kit.stage() as st:
        norm = Norm(kit, "moe", st)
        m = kit.buffers(
            st, wg=([P, FC, E_ + 1], F32), sgu=([P, FC, 2 * IS], F32), sd=([P, IS // P, D], F32), before=([P, P], F32), ones=([P, P], F32),
            rank=([P, NT], F32), first=([P, E_], F32), routed=([P, 2, ROUTED], F32), xlT=([P, 2, FC, P], F32), xlT_all=([P, FC, B * S], F32),
            logit=([P, E_ + 1], F32), best=([P, TOPK], F32), nbest=([P, 1], F32), rest=([P, E_], F32), chosen=([P, 2, E_], F32), count=([P, 2, E_], F32),
            gate=([P, E_], F32), mass=([P, 1], F32), rmass=([P, 1], F32), keep=([P, E_], F32), place=([P, E_], F32), key=([P, E_], F32), spot=([P, TOPK], F32),
            keyT=([E_, B * S], F32), order=([E_, CAP], F32), token=([CAP, E_], F32), sgate=([P, NT], F32), up=([P, 2, GS], F32), hid=([P, 2, IS // P, GS], F32))
        s = kit.sems("moe", "w_in c_set xl xlT_ps xlT xlT_kept lg_ps logit best nbest rest chosen e mass rmass w place_ps keep placed place spot address key keyT_ps keyT "
                     "count sgate_e sgate1 sgate order struck order_ps tok1 tok su_ps silu hid so_ps x_add passed passed_pe")
        stored = kit.pair("moe", "stored")
        with nc.Block() as block:
            @block.sync
            def _(sp):
                for sb, src in ((m.wg[:], d.gates_w), (m.sgu[:], d.shared_gu), (m.sd[:], d.shared_down)):
                    sp.dma_start(sb, src.rearrange("(f p) n -> p f n", p=P)).then_inc(s.w_in, 16)
                for sb, src in ((m.before, d.before), (m.rank, d.rank), (m.first, d.first)):
                    sp.dma_start(sb[:], src).then_inc(s.w_in, 16)
                with sp.Fori(0, NT // 2) as u:
                    for k in range(2):
                        n = u * 2 + k
                        sp.wait_ge(s.w, n + 1)
                        sp.dma_start(d.routed_tiles[n], m.routed[:, k, :]).then_inc(stored[k], 16)
                for k in range(2):
                    sp.wait_ge(stored[k], 16 * (NT // 2 + 1))

            @block.vector
            def _(dve):
                for k in range(2):
                    dve.sem_inc(stored[k], 16)
                nc.vector.memset(m.ones[:], 1.0).then_inc(s.c_set, 1)
                nc.vector.memset(m.count[:], 0.0).then_inc(s.c_set, 1)
                norm.vector_part(dve)
                dve.wait_ge(s.w_in, 96)
                dve.wait_ge(s.c_set, 2)

                def tile(n, u, k):
                    dve.wait_ge(stored[k], u * 16 + 16)
                    norm.rows(m.routed[:, k, 0:D], n).then_inc(s.xl, 1)
                    dve.wait_ge(s.lg_ps, n + 1)
                    nc.vector.tensor_copy(m.logit[:], kit.psum(1)[:, 0:E_ + 1]).then_inc(s.logit, 1)
                    hold(dve, s.logit, n + 1, s.passed)
                    nc.vector.max(m.best[:], m.logit[:, 0:E_]).then_inc(s.best, 1)
                    hold(dve, s.best, n + 1, s.passed)
                    nc.vector.match_replace(m.rest[:], m.best[:], m.logit[:, 0:E_], -3.0e38).then_inc(s.rest, 1)
                    nc.vector.tensor_scalar(m.nbest[:], m.best[:, 0:1], -1.0, None, ALU.mult).then_inc(s.nbest, 1)
                    dve.wait_ge(s.rest, n + 1)
                    nc.vector.tensor_tensor(m.chosen[:, k, :], m.rest[:], m.logit[:, 0:E_], ALU.not_equal).then_inc(s.chosen, 1)
                    dve.wait_ge(s.e, n + 1)
                    dve.wait_ge(s.chosen, n + 1)
                    nc.vector.scalar_tensor_tensor(m.gate[:], m.gate[:], 1.0, m.chosen[:, k, :], ALU.mult, ALU.mult, accum_out=m.mass[:]).then_inc(s.mass, 1)
                    dve.wait_ge(s.mass, n + 1)
                    nc.vector.reciprocal(m.rmass[:], m.mass[:]).then_inc(s.rmass, 1)
                    dve.wait_ge(s.rmass, n + 1)
                    nc.vector.tensor_scalar(m.routed[:, k, D:ROUTED], m.gate[:], m.rmass[:], None, ALU.mult).then_inc(s.w, 1)
                    dve.wait_ge(s.place_ps, n + 1)
                    nc.vector.scalar_tensor_tensor(m.keep[:], kit.psum(2)[:, 0:E_], float(CAP), m.chosen[:, k, :], ALU.is_lt, ALU.mult).then_inc(s.keep, 1)
                    nc.vector.tensor_tensor(m.place[:], kit.psum(2)[:, 0:E_], m.first[:], ALU.add).then_inc(s.placed, 1)
                    nc.vector.tensor_tensor(m.count[:, 1 - k, :], m.count[:, k, :], m.chosen[:, k, :], ALU.add).then_inc(s.count, 1)
                    dve.wait_ge(s.keep, n + 1)
                    dve.wait_ge(s.placed, n + 1)
                    nc.vector.tensor_tensor(m.place[:], m.place[:], m.keep[:], ALU.mult).then_inc(s.place, 1)
                    dve.wait_ge(s.keyT_ps, n)
                    nc.vector.tensor_scalar(m.key[:], m.keep[:], m.rank[:, bass.ds(n, 1)], None, ALU.mult).then_inc(s.key, 1)
                    hold(dve, s.place, n + 1, s.passed)
                    nc.vector.max(m.spot[:], m.place[:]).then_inc(s.spot, 1)
                    dve.wait_ge(s.spot, n + 1)
                    nc.vector.tensor_copy(kept.address[:, n, :], m.spot[:]).then_inc(s.address, 1)

                with dve.Fori(0, NT // 2) as u:
                    for k in range(2):
                        tile(u * 2 + k, u, k)
                dve.wait_ge(s.sgate_e, NT)
                nc.vector.tensor_scalar(m.sgate[:], m.sgate[:], 1.0, None, ALU.add).then_inc(s.sgate1, 1)
                dve.wait_ge(s.sgate1, 1)
                nc.vector.reciprocal(m.sgate[:], m.sgate[:]).then_inc(s.sgate, 1)
                dve.wait_ge(s.keyT, NT)
                rounds = CAP // 8
                groups = B * S // GS
                for g in range(groups):
                    for i in range(IS // P):
                        r = g * (rounds // groups) + i
                        if r > 0:
                            dve.wait_ge(s.struck, r)
                        nc.vector.max(m.order[:, 8 * r:8 * r + 8], m.keyT[:]).then_inc(s.order, 1)
                        n = g * (IS // P) + i
                        dve.wait_ge(s.silu, n + 1)
                        dve.wait_ge(s.su_ps, 2 * n + 2)
                        if g >= 2:
                            dve.wait_ge(s.so_ps, 4 * (g - 1))
                        nc.vector.tensor_tensor(m.hid[:, g % 2, i, :], m.up[:, n % 2, :], kit.psum(4 + n % 2), ALU.mult).then_inc(s.hid, 1)
                        dve.wait_ge(s.order, r + 1)
                        nc.vector.match_replace(m.keyT[:], m.order[:, 8 * r:8 * r + 8], m.keyT[:], 0.0).then_inc(s.struck, 1)
                    if g == 0:
                        dve.wait_ge(s.sgate, 1)
                    for i in range(GS // P):
                        n = g * (GS // P) + i
                        dve.wait_ge(s.so_ps, n + 1)
                        nc.vector.scalar_tensor_tensor(X[:, n, :], kit.psum(6 + n % 2)[:, 0:D], m.sgate[:, n:n + 1], X[:, n, :], ALU.mult, ALU.add).then_inc(s.x_add, 1)
                dve.wait_ge(s.order_ps, 1)
                nc.vector.tensor_scalar(m.token[:], kit.psum(0)[:, 0:E_], -1.0, float(B * S), ALU.mult, ALU.add).then_inc(s.tok1, 1)
                dve.wait_ge(s.tok1, 1)
                nc.vector.tensor_scalar(kept.token[:], m.token[:], float(B * S - 1), None, ALU.min).then_inc(s.tok, 1)
                dve.wait_ge(s.tok, 1)
                dve.wait_ge(s.address, NT)
                dve.wait_ge(s.x_add, NT)

            @block.gpsimd
            def _(pool):
                norm.pool_part(pool)
                with pool.Fori(0, NT // 2) as u:
                    for k in range(2):
                        n = u * 2 + k
                        pool.wait_ge(s.xlT, n + 1)
                        nc.gpsimd.tensor_copy(m.xlT_all[:, :, bass.ts(n, P)], m.xlT[:, k]).then_inc(s.xlT_kept, 1)

            @block.scalar
            def _(act):
                with act.Fori(0, NT // 2) as u:
                    for k in range(2):
                        n = u * 2 + k
                        act.wait_ge(s.xlT_ps, n + 1)
                        act.wait_ge(s.xlT_kept, u * 2)
                        nc.scalar.copy(m.xlT[:, k].rearrange("p f t -> p (f t)"), kit.psum(0)[:, 0:D]).then_inc(s.xlT, 1)
                        act.wait_ge(s.logit, n + 1)
                        nc.scalar.activation(m.sgate[:, bass.ds(n, 1)], m.logit[:, E_:E_ + 1], ACT.Exp, scale=-1.0).then_inc(s.sgate_e, 1)
                        act.wait_ge(s.nbest, n + 1)
                        nc.scalar.activation(m.gate[:], m.logit[:, 0:E_], ACT.Exp, bias=m.nbest[:]).then_inc(s.e, 1)
                        act.wait_ge(s.keyT_ps, n + 1)
                        nc.scalar.copy(m.keyT[:, bass.ts(n, P)], kit.psum(3)[0:E_, 0:P]).then_inc(s.keyT, 1)
                with act.Fori(0, B * S // GS * (IS // P) // 2) as u:
                    for k in range(2):
                        n = u * 2 + k
                        act.wait_ge(s.su_ps, n * 2 + 1)
                        act.wait_ge(s.hid, u * 2)
                        nc.scalar.activation(m.up[:, k, :], kit.psum(2 + k), ACT.Silu).then_inc(s.silu, 1)

            @block.tensor
            def _(pe):
                pe.wait_ge(s.w_in, 96)
                pe.wait_ge(s.c_set, 2)
                with pe.Fori(0, NT // 2) as u:
                    for k in range(2):
                        n = u * 2 + k
                        pe.wait_ge(s.xl, n + 1)
                        for f in range(FC):
                            mm = nc.tensor.transpose(kit.psum(0)[:, f * P:(f + 1) * P], m.routed[:, k, f * P:(f + 1) * P], kit.ident[:])
                        mm.then_inc(s.xlT_ps, 1)
                        pe.wait_ge(s.xlT, n + 1)
                        pe.wait_ge(s.logit, n)
                        for f in range(FC):
                            mm = nc.tensor.matmul(kit.psum(1)[:, 0:E_ + 1], m.xlT[:, k, f, :], m.wg[:, f, :], start=(f == 0), stop=(f == FC - 1))
                        mm.then_inc(s.lg_ps, 1)
                        pe.wait_ge(s.chosen, n + 1)
                        pe.wait_ge(s.count, n)
                        nc.tensor.matmul(kit.psum(2)[:, 0:E_], m.before[:], m.chosen[:, k, :], start=True, stop=False)
                        nc.tensor.matmul(kit.psum(2)[:, 0:E_], m.ones[:], m.count[:, k, :], start=False, stop=True).then_inc(s.place_ps, 1)
                        pe.wait_ge(s.keyT, n)
                        hold(pe, s.key, n + 1, s.passed_pe)
                        nc.tensor.transpose(kit.psum(3)[0:E_, 0:P], m.key[:], kit.ident[:]).then_inc(s.keyT_ps, 1)
                pe.wait_ge(s.keyT, NT)
                pe.wait_ge(s.xlT_kept, NT)
                with pe.Fori(0, B * S // GS // 2) as u:
                    for k in range(2):
                        g = u * 2 + k
                        for i in range(IS // P):
                            n = g * (IS // P) + i
                            pe.wait_ge(s.hid, g * (IS // P) + max(i - 1, 0))
                            for part, bank in ((0, 2 + i % 2), (1, 4 + i % 2)):
                                for f in range(FC):
                                    mm = nc.tensor.matmul(kit.psum(bank), m.sgu[:, f, part * IS + i * P:part * IS + (i + 1) * P], m.xlT_all[:, f, bass.ts(g, GS)],
                                                          start=(f == 0), stop=(f == FC - 1))
                                mm.then_inc(s.su_ps, 1)
                        pe.wait_ge(s.hid, g * (IS // P) + (IS // P))
                        for i in range(GS // P):
                            pe.wait_ge(s.x_add, g * (GS // P) + max(i - 1, 0))
                            for c in range(IS // P):
                                mm = nc.tensor.matmul(kit.psum(6 + i % 2)[:, 0:D], m.hid[:, k, c, i * P:(i + 1) * P], m.sd[:, c, :], start=(c == 0), stop=(c == IS // P - 1))
                            mm.then_inc(s.so_ps, 1)
                pe.wait_ge(s.order, CAP // 8)
                nc.tensor.transpose(kit.psum(0)[:, 0:E_], m.order[:], kit.ident[0:E_, 0:E_]).then_inc(s.order_ps, 1)


def experts(kit, kept):
    nc, d = kit.nc, kit.dram
    X = kit.X
    with kit.stage() as st:
        m = kit.buffers(
            st, index=([CAP, 2, 1], U32), rows=([CAP, 2, ROUTED], F32), rowsT=([P, 2, FC, CAP], F32), wgu=([P, 2, FC, 2 * I_], F32), wd=([I_, 2, D], F32),
            silu=([I_, 2, CAP], F32), hid=([I_, 2, CAP], F32), out=([CAP, 2, D], F32), zero=([2, D], F32),
            where=([P, 2, TOPK], U32), parts=([P, 2, TOPK, D], F32), total=([P, 2, D], F32))
        s = kit.sems("exp", "zero zero_out index where w_free rT_ps rT gu_ps silu hid y_ps out total x_add passed")
        w_in, rows_in, stored, parts_in = (kit.pair("exp", n) for n in ("w_in", "rows_in", "stored", "parts_in"))
        with nc.Block() as block:
            @block.sync
            def _(sp):
                sp.wait_ge(s.zero, 1)
                sp.dma_start(d.expert_rows[0:1, :], m.zero[0:1, :]).then_inc(s.zero_out, 16)
                with sp.Fori(0, E_ // 2) as u:
                    for k in range(2):
                        e = u * 2 + k
                        sp.wait_ge(s.w_free, e + 1)
                        sp.dma_start(m.wgu[:, k], d.expert_gu[e].rearrange("(f p) n -> p f n", p=P)).then_inc(w_in[k], 16)
                        sp.dma_start(m.wd[:, k, :], d.expert_down[e]).then_inc(w_in[k], 16)

            @block.gpsimd
            def _(pool):
                with pool.Fori(0, E_ // 2) as u:
                    for k in range(2):
                        e = u * 2 + k
                        pool.wait_ge(s.out, e)
                        nc.gpsimd.tensor_copy(m.index[:, k, :], kept.token[:, bass.ds(e, 1)]).then_inc(s.index, 1)
                        hold(pool, s.index, e + 1, s.passed)
                        nc.gpsimd.indirect_dma_start(m.rows[:, k, :], None, d.routed, bass.IndirectOffsetOnAxis(m.index[:, k, :], 0)).then_inc(rows_in[k], 16)
                for k in range(2):
                    pool.wait_ge(stored[k], 16 * (E_ // 2 + 1))
                pool.wait_ge(s.zero_out, 16)
                with pool.Fori(0, NT // 2) as u:
                    for k in range(2):
                        n = u * 2 + k
                        pool.wait_ge(s.total, n)
                        nc.gpsimd.tensor_copy(m.where[:, k, :], kept.address[:, n, :]).then_inc(s.where, 1)
                        hold(pool, s.where, n + 1, s.passed)
                        for c in range(TOPK):
                            nc.gpsimd.indirect_dma_start(m.parts[:, k, c, :], None, d.expert_rows, bass.IndirectOffsetOnAxis(m.where[:, k, c:c + 1], 0)).then_inc(parts_in[k], 16)

            @block.vector
            def _(dve):
                nc.vector.memset(m.zero[:], 0.0).then_inc(s.zero, 1)
                for k in range(2):
                    dve.sem_inc(stored[k], 16)
                dve.sem_inc(s.w_free, 2)
                dve.sem_inc(s.out, 1)
                dve.sem_inc(s.total, 1)

                def gated(e, k):
                    dve.wait_ge(s.silu, e + 1)
                    nc.vector.tensor_tensor(m.hid[:, k, :], m.silu[:, k, :], kit.psum(2 + k)[:, CAP:2 * CAP], ALU.mult).then_inc(s.hid, 1)

                def weighted(e, k, u):
                    dve.wait_ge(s.y_ps, e + 1)
                    dve.sem_inc(s.w_free, 1)
                    dve.wait_ge(stored[k], u * 16 + 16)
                    nc.vector.tensor_scalar(m.out[:, k, :], kit.psum(4 + k)[:, 0:D], m.rows[:, k, bass.ds(e + D, 1)], None, ALU.mult).then_inc(s.out, 1)

                gated(0, 0)
                with dve.Fori(0, E_ // 2 - 1) as u:
                    for k in range(2):
                        gated(u * 2 + (k + 1), 1 - k)
                        weighted(u * 2 + k, k, u)
                gated(E_ - 1, 1)
                weighted(E_ - 2, 0, E_ // 2 - 1)
                weighted(E_ - 1, 1, E_ // 2 - 1)
                with dve.Fori(0, NT // 2) as u:
                    for k in range(2):
                        n = u * 2 + k
                        dve.wait_ge(parts_in[k], u * 128 + 128)
                        nc.vector.tensor_reduce(m.total[:, k, :], m.parts[:, k].rearrange("p c d -> p d c"), AX.X, ALU.add).then_inc(s.total, 1)
                        dve.wait_ge(s.total, n + 2)
                        nc.vector.tensor_tensor(X[:, n, :], X[:, n, :], m.total[:, k, :], ALU.add).then_inc(s.x_add, 1)
                dve.wait_ge(s.x_add, NT)

            @block.scalar
            def _(act):
                def front(e, k):
                    act.wait_ge(s.rT_ps, e + 1)
                    nc.scalar.copy(m.rowsT[:, k].rearrange("p f t -> p (f t)"), kit.psum(k)[:, 0:FC * CAP]).then_inc(s.rT, 1)
                    act.wait_ge(s.gu_ps, e + 1)
                    nc.scalar.activation(m.silu[:, k, :], kit.psum(2 + k)[:, 0:CAP], ACT.Silu).then_inc(s.silu, 1)

                def store(e, k):
                    act.wait_ge(s.out, e + 2)
                    act.dma_start(d.expert_tiles[e], m.out[:, k, :]).then_inc(stored[k], 16)

                front(0, 0)
                with act.Fori(0, E_ // 2 - 1) as u:
                    for k in range(2):
                        front(u * 2 + (k + 1), 1 - k)
                        store(u * 2 + k, k)
                front(E_ - 1, 1)
                store(E_ - 2, 0)
                store(E_ - 1, 1)

            @block.tensor
            def _(pe):
                def front(e, k, u):
                    pe.wait_ge(rows_in[k], u * 16 + 16)
                    for f in range(FC):
                        mm = nc.tensor.transpose(kit.psum(k)[:, f * CAP:(f + 1) * CAP], m.rows[:, k, f * P:(f + 1) * P], kit.ident[:])
                    mm.then_inc(s.rT_ps, 1)
                    pe.wait_ge(w_in[k], u * 32 + 32)
                    pe.wait_ge(s.rT, e + 1)
                    for part in range(2):
                        for f in range(FC):
                            mm = nc.tensor.matmul(kit.psum(2 + k)[:, part * CAP:(part + 1) * CAP], m.wgu[:, k, f, part * I_:(part + 1) * I_], m.rowsT[:, k, f, :],
                                                  start=(f == 0), stop=(f == FC - 1))
                    mm.then_inc(s.gu_ps, 1)

                def back(e, k):
                    pe.wait_ge(s.hid, e + 1)
                    nc.tensor.matmul(kit.psum(4 + k)[:, 0:D], m.hid[:, k, :], m.wd[:, k, :], start=True, stop=True).then_inc(s.y_ps, 1)

                front(0, 0, 0)
                with pe.Fori(0, E_ // 2 - 1) as u:
                    for k in range(2):
                        front(u * 2 + (k + 1), 1 - k, u + k)
                        pe.wait_ge(s.out, u * 2 + k)
                        back(u * 2 + k, k)
                front(E_ - 1, 1, E_ // 2 - 1)
                pe.wait_ge(s.out, E_ - 2)
                back(E_ - 2, 0)
                back(E_ - 1, 1)



def build(nc, dram):
    d = dram
    with ExitStack() as ctx:
        kit = Kit(nc, ctx, dram)
        load_inputs(kit)
        with kit.stage() as st:
            kit.tail_rk = st.enter_context(nc.sbuf_tensor("tail_rk", [H, B, S + LEFT], F32))
            latent_queries(kit)
            cross_attention(kit, "xa0", True, d.WkT, d.Wkv[:, INNER:2 * INNER], d.Wout, d.bout, (d.qn_g, d.kn_g))
        self_attention(kit, "sa0", False)
        mixture(kit)
        plain_queries(kit, "lq1", d.wq1)
        cross_attention(kit, "xa1", False, d.wkT1, d.wv1, d.wo1, d.bo1, ())
        self_attention(kit, "sa1", True)
        tanh_map(kit)


def kernel(**inputs):
    import concourse.bacc as bacc
    from concourse.bass_utils import run_bass_kernel_spmd

    a = {k: np.asarray(v) for k, v in inputs.items()}
    x0, s0, f0, x1, s1, f1 = (f"L{i}_{n}_" for i in range(2) for n in ("xattn", "attn", "ffn"))
    head, row = np.arange(H), np.arange(P)
    freq = np.outer(row % S, 1.0 / 10000.0 ** (np.arange(0, 32, 2, dtype=np.float32) / np.float32(32))).astype(np.float32)
    constants = {
        "ident": np.eye(P), "sel": head[:, None, None] == BT * np.arange(HC)[None, :, None] + row[None, None, :] // S,
        "cos": np.cos(freq), "sin": np.stack([-np.sin(freq), np.sin(freq)], 1),
        "causal": np.where(np.arange(S)[None, :] <= (row % S)[:, None], 0.0, -3.0e38), "blk": row[:, None] // 16 == row[None, :] // 16,
        "before": row[:, None] < row[None, :], "rank": B * S - (np.arange(NT)[None, :] * P + row[:, None]),
        "first": np.broadcast_to(1.0 + CAP * np.arange(E_), (P, E_)),
    }
    arrays = {k: v.astype(np.float32) for k, v in constants.items()}
    arrays |= {
        "x": a["x"].reshape(B * S, D), "ctx": a["ctx_1024"], "mask": a["mask_BxS2_bf1"].view(np.uint8),
        "ln_x_g": a[x0 + "ln_x_g"], "ln_x_b": a[x0 + "ln_x_b"], "ln_l_g": a[x0 + "ln_l_g"], "ln_l_b": a[x0 + "ln_l_b"],
        "qn_g": a[x0 + "qn_g"], "kn_g": a[x0 + "kn_g"], "Wq": a[x0 + "Wq"], "Wkv": a[x0 + "Wkv"],
        "WkT": a[x0 + "Wkv"][:, :INNER].T, "Wout": a[x0 + "Wout"], "bout": a[x0 + "bout"],
        "WqT": a[s0 + "Wq"].T, "WkT0": a[s0 + "Wk"].T, "WvT": a[s0 + "Wv"].T, "WoT": a[s0 + "Wo"].T, "qn_w": a[s0 + "qn_w"], "kn_w": a[s0 + "kn_w"],
        "gates_w": np.concatenate([a[f0 + "gate_w"], a[f0 + "shared_gate_w"]], 1), "shared_gu": a[f0 + "shared_gate_up_w"], "shared_down": a[f0 + "shared_down_w"],
        "expert_gu": a[f0 + "expert_gate_up_w"], "expert_down": a[f0 + "expert_down_w"],
        "wq1": a[x1 + "wq"].reshape(D, INNER), "wkT1": a[x1 + "wk"].reshape(D, INNER).T, "wv1": a[x1 + "wv"].reshape(D, INNER),
        "wo1": a[x1 + "wo"].reshape(INNER, D), "bo1": a[x1 + "bo"],
        "cw": a[s1 + "c_attn_w"], "cb": a[s1 + "c_attn_b"].reshape(6, P).T, "q2lT": a[s1 + "q2l_w"].T, "q2lb": a[s1 + "q2l_b"], "kv2l": a[s1 + "kv2l_w"], "kv2lT": a[s1 + "kv2l_w"].T,
        "kvb": a[s1 + "kv2l_b"], "l2oT": a[s1 + "l2o_w"].T, "l2ob": a[s1 + "l2o_b"], "wqkT": a[s1 + "wqk_w"].T, "wqkb": a[s1 + "wqk_b"],
        "cprojT": a[s1 + "cproj_w"].T, "cprojb": a[s1 + "cproj_b"],
        "weightT": a[f1 + "weight"].T, "aux1T": a[f1 + "aux_weight1"].T, "aux2": a[f1 + "aux_weight2"], "map_b": a[f1 + "bias"],
    }
    arrays = {k: np.ascontiguousarray(v) for k, v in arrays.items()}
    nc = bacc.Bacc("TRN2", target_bir_lowering=False, num_devices=1)
    handles = {k: nc.dram_tensor(f"in_{k}", v.shape, mybir.dt.from_np(v.dtype), kind="ExternalInput").ap() for k, v in arrays.items()}
    out = nc.dram_tensor("out_x", (B * S, D), F32, kind="ExternalOutput").ap()
    handles["out"] = out
    handles["out_tiles"] = out.rearrange("(t p) d -> t p d", p=P)
    handles["qT"] = nc.dram_tensor("scratch_qT", (P, NP_, B * S), F32, kind="Internal").ap()
    lat = nc.dram_tensor("scratch_lat", (B * S, D), F32, kind="Internal").ap()
    handles["tail_lat"] = lat.rearrange("(t p) d -> t p d", p=P)
    handles["tail_lat_b"] = lat.rearrange("(b s) d -> b s d", s=S)
    handles["tail_last"] = nc.dram_tensor("scratch_last", (B, D), F32, kind="Internal").ap()
    handles["routed"] = nc.dram_tensor("scratch_routed", (B * S, ROUTED), F32, kind="Internal").ap()
    handles["routed_tiles"] = handles["routed"].rearrange("(t p) d -> t p d", p=P)
    handles["expert_rows"] = nc.dram_tensor("scratch_expert", (1 + E_ * CAP, D), F32, kind="Internal").ap()
    handles["expert_tiles"] = handles["expert_rows"][1:1 + E_ * CAP, :].rearrange("(e c) d -> e c d", c=CAP)
    build(nc, named(handles))
    res = run_bass_kernel_spmd(nc, [{f"in_{k}": v for k, v in arrays.items()}], core_ids=[0])
    return res.results[0]["out_x"].reshape(B, S, D)
```

```python
from collections import namedtuple
from contextlib import ExitStack, contextmanager

import numpy as np
import concourse.bass as bass
from concourse import mybir

F32 = mybir.dt.float32
BF16 = mybir.dt.bfloat16
U32 = mybir.dt.uint32
F32R = mybir.dt.float32r
U8 = mybir.dt.uint8
ALU = mybir.AluOpType
ACT = mybir.ActivationFunctionType
AX = mybir.AxisListType

P = 128
B, S, D = 64, 32, 256
NT = B * S // P
BT = P // S
FC = D // P
H, DH = 16, 64
INNER = H * DH
NP_ = INNER // P
CTX = 257
KF = 2
LEFT = CTX - KF * P
GB = 8
NG = B // GB
GT = GB * S
HC = H // BT
LN_EPS = 1e-5
MASKED = 1e30
H3 = 96
HIGH = 0xFFFFF000
PARTS = 3
PAIRS = PARTS * PARTS


def named(things):
    return namedtuple("Named", list(things))(**things)


class Kit:

    def __init__(self, nc, ctx, dram):
        self.nc, self.dram, self.used = nc, dram, []
        self.bank = [ctx.enter_context(nc.psum_tensor(f"bank{i}", [P, 2, 512], F32)) for i in range(4)]
        self.X = ctx.enter_context(nc.sbuf_tensor("residual", [P, NT, D], F32))
        self.ident = ctx.enter_context(nc.sbuf_tensor("ident", [P, P], F32))
        self.ident16 = ctx.enter_context(nc.sbuf_tensor("ident16", [P, P], BF16))
        self.neg_half = ctx.enter_context(nc.sbuf_tensor("neg_half", [P, 2 * H], F32))

    @contextmanager
    def stage(self):
        outer, self.used = self.used, []
        with ExitStack() as stack:
            yield stack
            self.nc.clear_and_free_semaphores(self.used)
            self.nc.all_engine_barrier()
        self.used = outer

    def semaphore(self, name):
        self.used.append(self.nc.alloc_semaphore(name=name))
        return self.used[-1]

    def psum(self, i):
        return self.bank[i // 2][:, i % 2, :]

    def buffers(self, stack, **shapes):
        made = {}
        for name, (shape, dtype) in shapes.items():
            made[name] = stack.enter_context(self.nc.sbuf_tensor(f"{name}_{self.nc.next_id()}", shape, dtype))
        return named(made)

    def sems(self, stage, names):
        return named({n: self.semaphore(f"{stage}_{n}") for n in names.split()})

    def several(self, stage, name, count):
        return [self.semaphore(f"{stage}_{name}{i}") for i in range(count)]

    def pair(self, stage, name):
        return self.several(stage, name, 2)


def hold(engine, sem, value, passed):
    engine.wait_ge(sem, value)
    engine.sem_inc(passed, 1)


def row_stats(nc, dve, rows, stats, mean_var, stats_done, aggr_done, base=0):
    for t, r in enumerate(rows):
        nc.vector.bn_stats(stats[:, t, :], r).then_inc(stats_done, 1)
    for t in range(len(rows)):
        dve.wait_ge(stats_done, base + t + 1)
        nc.vector.bn_aggr(mean_var[:, t, :], stats[:, t, :]).then_inc(aggr_done, 1)


def inv_root(nc, pool, neg_half, out, value, scale, shift, op, done_scaled, n_scaled, done):
    nc.gpsimd.tensor_scalar(out, value, scale, shift, ALU.mult, op).then_inc(done_scaled, 1)
    pool.wait_ge(done_scaled, n_scaled)
    nc.gpsimd.tensor_tensor(out, out, neg_half, ALU.pow).then_inc(done, 1)


class Norm:

    def __init__(self, kit, stage, stack):
        self.kit, self.nc = kit, kit.nc
        self.m = kit.buffers(stack, stats=([P, 6], F32), pair=([P, 2], F32), mv=([P, NT, 2], F32), rstd=([P, NT], F32))
        self.s = kit.sems(f"{stage}_norm", "stats aggr kept eps rstd passed passed_pool")

    def tile(self, dve, n, added, count):
        hold(dve, added, count, self.s.passed)
        self.nc.vector.bn_stats(self.m.stats[:], self.kit.X[:, n, :]).then_inc(self.s.stats, 1)
        hold(dve, self.s.stats, n + 1, self.s.passed)
        self.nc.vector.bn_aggr(self.m.pair[:], self.m.stats[:]).then_inc(self.s.aggr, 1)
        dve.wait_ge(self.s.aggr, n + 1)
        self.nc.vector.tensor_copy(self.m.mv[:, n, :], self.m.pair[:]).then_inc(self.s.kept, 1)

    def inverse(self, pool):
        hold(pool, self.s.kept, NT, self.s.passed_pool)
        inv_root(self.nc, pool, self.kit.neg_half[:, 0:NT], self.m.rstd[:], self.m.mv[:, :, 1], 1.0, LN_EPS, ALU.add, self.s.eps, 1, self.s.rstd)

    def ready(self, dve):
        dve.wait_ge(self.s.rstd, 1)

    def rows(self, out, n, rstd=None):
        rstd = self.m.rstd[:, bass.ds(n, 1)] if rstd is None else rstd
        return self.nc.vector.tensor_scalar(out, self.kit.X[:, n, :], self.m.mv[:, n, 0:1], rstd, ALU.subtract, ALU.mult)


def thirds(ap):
    return [ap[..., 32 * i:32 * i + H] for i in range(3)]


def split3(nc, pool, parts, rest, value, done, count, passed):
    nc.gpsimd.tensor_copy(parts[0], value).then_inc(done, 1)
    pool.wait_ge(done, count + 1)
    nc.gpsimd.tensor_tensor(rest, value, parts[0], ALU.subtract).then_inc(done, 1)
    hold(pool, done, count + 2, passed)
    nc.gpsimd.tensor_copy(parts[1], rest).then_inc(done, 1)
    pool.wait_ge(done, count + 3)
    nc.gpsimd.tensor_tensor(parts[2], rest, parts[1], ALU.subtract).then_inc(done, 1)


def latent_queries(kit, cross, ahead):
    nc, d = kit.nc, kit.dram
    X = kit.X
    XP = 4
    with kit.stage() as st:
        m = kit.buffers(
            st, stats=([P, NT + 1, 6], F32), mv=([P, NT, 2], F32), r1=([P, NT], F32), var2=([P, NT], F32), r2=([P, NT], F32), r=([P, NT], F32),
            g_l=([P, D], F32), b_l=([P, D], F32), g_x=([B, D], F32), b_x=([B, D], F32),
            wq=([P, FC, INNER], F32), wk=([P, FC, INNER], F32), cent=([P, 2, D], F32), ln=([P, 2, D], F32),
            lnT=([P, 2, FC, P], F32), ksq=([P, INNER], F32), qsq=([P, INNER], F32), q=([P, 2, INNER], F32),
            ssk=([P, 2, H], F32), ssq=([P, 2, H], F32), rq=([P, 2, H], F32), rk=([P, 2, H], F32), qh=([P, 2, INNER], F32),
            qT=([P, 2, NP_, P], F32), last=([B, D], F32), mvl=([B, 1, 2], F32), rl=([B, 1], F32),
            lastn=([B, D], F32), lastT=([P, FC, B], F32), ssl=([B, H], F32), rkl=([B, H], F32),
            rk3=([P, 2, H3], BF16), rest=([P, H], F32), rkl3=([B, H3], BF16), last3=([B, PARTS, D], BF16), lrest=([B, D], F32),
            high=([P, FC, INNER], F32), sel=([H3, HC, P], F32))
        s = kit.sems("lat", "w_in last_in half set rk3 rkl3 ident16 stats aggr eps r1 r1sq var2 r2 r xlast cent ln_ready lnT_ps lnT k_ps k_sq kss "
                     "q_ps q_sq q_copied qss rq_scaled rq rk_scaled rk qh qT_ps qT last_cent passed lastn lastT_ps lastT kl_ps kl_sq "
                     "kl_ss rkl tail_ps tail_sb last3 last3_out sel_in high split")
        tail = kit.tail_rk
        x_in = kit.several("lat", "x_in", XP)
        ln_stored, qT_stored = kit.pair("lat", "ln_stored"), kit.pair("lat", "qT_stored")

        with nc.Block() as block:
            @block.sync
            def _(sp):
                x_tiles = d.x.rearrange("(t p) d -> p t d", p=P)
                for i in range(XP):
                    part = slice(i * NT // XP, (i + 1) * NT // XP)
                    sp.dma_start(X[:, part, :], x_tiles[:, part, :]).then_inc(x_in[i], 16)
                sp.dma_start(m.last[:], d.ctx[:, CTX - 1, :]).then_inc(s.last_in, 16)
                for sb, src in ((m.g_l, d.ln_l_g), (m.b_l, d.ln_l_b)):
                    sp.dma_start(sb[:], src.partition_broadcast(P)).then_inc(s.w_in, 16)
                for sb, src in ((m.g_x, d.ln_x_g), (m.b_x, d.ln_x_b)):
                    sp.dma_start(sb[:], src.partition_broadcast(B)).then_inc(s.w_in, 16)
                sp.dma_start(kit.ident[:], d.ident).then_inc(s.w_in, 16)
                sp.dma_start(m.wq[:], d.Wq.rearrange("(f p) n -> p f n", p=P)).then_inc(s.w_in, 16)
                sp.dma_start(m.wk[:], d.Wkv[:, 0:INNER].rearrange("(f p) n -> p f n", p=P)).then_inc(s.w_in, 16)
                sp.dma_start(m.sel[:], d.sel).then_inc(s.sel_in, 16)
                with sp.Fori(0, NT // 2) as u:
                    for k in range(2):
                        n = u * 2 + k
                        sp.wait_ge(s.ln_ready, n + 1)
                        sp.dma_start(d.tail_lat[n], m.ln[:, k, :]).then_inc(ln_stored[k], 16)
                        sp.wait_ge(s.qT, n + 1)
                        sp.dma_start(d.qT[:, :, bass.ts(n, P)], m.qT[:, k]).then_inc(qT_stored[k], 16)
                sp.wait_ge(s.last3, 4)
                for i in range(PARTS):
                    sp.dma_start(d.last_parts[i], m.last3[:]).then_inc(s.last3_out, 16)
                sp.wait_ge(s.lastn, 1)
                sp.dma_start(d.tail_last, m.lastn[:]).then_inc(s.last_in, 16)
                sp.wait_ge(s.last_in, 32)
                sp.wait_ge(s.last3_out, 16 * PARTS)
                for k in range(2):
                    sp.wait_ge(ln_stored[k], 16 * (NT // 2 + 1))
                    sp.wait_ge(qT_stored[k], 16 * (NT // 2 + 1))

            @block.vector
            def _(dve):
                nc.vector.memset(kit.neg_half[:], -0.5).then_inc(s.half, 1)
                nc.vector.memset(m.rk3[:], 0.0).then_inc(s.set, 1)
                nc.vector.memset(m.rkl3[:], 0.0).then_inc(s.set, 1)
                for t in range(NT):
                    dve.wait_ge(x_in[t * XP // NT], 16)
                    nc.vector.bn_stats(m.stats[:, t, :], X[:, t, :]).then_inc(s.stats, 1)
                for t in range(NT):
                    dve.wait_ge(s.stats, t + 1)
                    nc.vector.bn_aggr(m.mv[:, t, :], m.stats[:, t, :]).then_inc(s.aggr, 1)
                dve.wait_ge(s.last_in, 16)
                row_stats(nc, dve, [m.last[:]], m.stats[0:B, NT:NT + 1, :], m.mvl, s.stats, s.aggr, NT)
                dve.wait_ge(s.r1, 1)
                nc.vector.tensor_tensor(m.var2[:], m.r1[:], m.r1[:], ALU.mult).then_inc(s.r1sq, 1)
                dve.wait_ge(s.r1sq, 1)
                nc.vector.tensor_tensor(m.var2[:], m.var2[:], m.mv[:, :, 1], ALU.mult).then_inc(s.var2, 1)
                dve.wait_ge(s.r2, 1)
                nc.vector.tensor_tensor(m.r[:], m.r1[:], m.r2[:], ALU.mult).then_inc(s.r, 1)
                dve.wait_ge(s.r, 1)
                dve.wait_ge(s.w_in, 112)
                nc.vector.tensor_copy(kit.ident16[:], kit.ident[:]).then_inc(s.ident16, 1)
                for k in range(2):
                    dve.sem_inc(ln_stored[k], 16)
                    dve.sem_inc(qT_stored[k], 16)

                def normed(n, k, stores):
                    nc.vector.scalar_tensor_tensor(m.cent[:, k, :], X[:, n, :], m.mv[:, n, 0:1], m.g_l[:], ALU.subtract, ALU.mult).then_inc(s.cent, 1)
                    dve.wait_ge(s.cent, n + 1)
                    dve.wait_ge(ln_stored[k], stores * 16)
                    nc.vector.scalar_tensor_tensor(m.ln[:, k, :], m.cent[:, k, :], m.r[:, bass.ds(n, 1)], m.b_l[:], ALU.mult, ALU.add).then_inc(s.ln_ready, 1)

                def query_sums(n, k):
                    dve.wait_ge(s.q_sq, n + 1)
                    nc.vector.tensor_reduce(m.ssq[:, k, :], m.qsq[:].rearrange("p (h e) -> p h e", h=H), AX.X, ALU.add).then_inc(s.qss, 1)

                def key_sums(n, k):
                    dve.wait_ge(s.k_sq, n + 1)
                    nc.vector.tensor_reduce(m.ssk[:, k, :], m.ksq[:].rearrange("p (h e) -> p h e", h=H), AX.X, ALU.add).then_inc(s.kss, 1)

                def queries(n, k):
                    dve.wait_ge(s.rq, n + 1)
                    dve.wait_ge(s.q_copied, n + 1)
                    nc.vector.tensor_tensor(m.qh[:, k, :].rearrange("p (h e) -> p h e", h=H), m.q[:, k, :].rearrange("p (h e) -> p h e", h=H),
                                            m.rq[:, k, :].unsqueeze(2).to_broadcast([P, H, DH]), ALU.mult).then_inc(s.qh, 1)

                def queries_T(n, k, stores):
                    dve.wait_ge(s.qT_ps, n + 1)
                    dve.wait_ge(qT_stored[k], stores * 16)
                    nc.vector.tensor_copy(m.qT[:, k].rearrange("p a t -> p (a t)"), kit.bank[3][:].rearrange("p a t -> p (a t)")).then_inc(s.qT, 1)

                def norms_T(n):
                    dve.wait_ge(s.tail_ps, n + 1)
                    nc.vector.tensor_copy(tail[:, bass.ds(n * BT, BT), 0:S], kit.psum(1)[0:H3, 0:P].rearrange("h (b k) -> h b k", b=BT)).then_inc(s.tail_sb, 1)

                def step(n, k, u, ahead):
                    if ahead >= 2:
                        normed(n + 2, k, u + 2)
                    if ahead >= 1:
                        query_sums(n + 1, 1 - k)
                    queries_T(n, k, u + 1)
                    norms_T(n)
                    if ahead >= 1:
                        key_sums(n + 1, 1 - k)
                        queries(n + 1, 1 - k)

                normed(0, 0, 1)
                normed(1, 1, 1)
                query_sums(0, 0)
                key_sums(0, 0)
                queries(0, 0)
                nc.vector.tensor_scalar(m.high[:].bitcast(U32), m.wk[:].bitcast(U32), HIGH, None, ALU.bitwise_and).then_inc(s.high, 1)
                dve.wait_ge(s.high, 1)
                nc.vector.tensor_copy(cross.mk.wk_hi[:], m.high[:]).then_inc(s.split, 1)
                nc.vector.tensor_tensor(cross.mk.wk_lo[:], m.wk[:], m.high[:], ALU.subtract).then_inc(s.split, 1)
                dve.wait_ge(s.sel_in, 16)
                nc.vector.tensor_copy(cross.mk.sel[:], m.sel[:]).then_inc(s.split, 1)
                nc.vector.scalar_tensor_tensor(m.lastn[:], m.last[:], m.mvl[:, 0, 0:1], m.g_x[:], ALU.subtract, ALU.mult).then_inc(s.last_cent, 1)
                dve.wait_ge(s.last_cent, 1)
                dve.wait_ge(s.r2, 2)
                nc.vector.scalar_tensor_tensor(m.lastn[:], m.lastn[:], m.rl[:, 0:1], m.b_x[:], ALU.mult, ALU.add).then_inc(s.lastn, 1)
                with dve.Fori(0, NT // 2 - 1) as u:
                    for k in range(2):
                        step(u * 2 + k, k, u, 2)
                step(NT - 2, 0, NT // 2 - 1, 1)
                dve.wait_ge(s.kl_sq, 1)
                nc.vector.tensor_reduce(m.ssl[:], m.ksq[0:B, :].rearrange("p (h e) -> p h e", h=H), AX.X, ALU.add).then_inc(s.kl_ss, 1)
                step(NT - 1, 1, NT // 2 - 1, 0)
                dve.wait_ge(s.tail_ps, NT + 1)
                nc.vector.tensor_copy(tail[:, :, S:S + 1], kit.psum(1)[0:H3, 0:B].unsqueeze(2)).then_inc(s.tail_sb, 1)

            @block.gpsimd
            def _(pool):
                pool.wait_ge(s.half, 1)
                pool.wait_ge(s.aggr, NT)
                inv_root(nc, pool, kit.neg_half[:, 0:NT], m.r1[:], m.mv[:, :, 1], 1.0, LN_EPS, ALU.add, s.eps, 1, s.r1)
                hold(pool, s.var2, 1, s.passed)
                inv_root(nc, pool, kit.neg_half[:, 0:NT], m.r2[:], m.var2[:], 1.0, LN_EPS, ALU.add, s.eps, 2, s.r2)
                hold(pool, s.aggr, NT + 1, s.passed)
                inv_root(nc, pool, kit.neg_half[0:B, 0:1], m.rl[:], m.mvl[:, :, 1], 1.0, LN_EPS, ALU.add, s.eps, 3, s.r2)
                split3(nc, pool, [m.last3[:, i, :] for i in range(PARTS)], m.lrest[:], m.last[:], s.last3, 0, s.passed)

                def inverse_norms(n, k):
                    hold(pool, s.qss, n + 1, s.passed)
                    inv_root(nc, pool, kit.neg_half[:, 0:H], m.rq[:, k, :], m.ssq[:, k, :], 1.0 / DH, 1e-16, ALU.max, s.rq_scaled, n + 1, s.rq)
                    hold(pool, s.kss, n + 1, s.passed)
                    inv_root(nc, pool, kit.neg_half[:, 0:H], m.rk[:, k, :], m.ssk[:, k, :], 1.0 / DH, 1e-16, ALU.max, s.rk_scaled, n + 1, s.rk)
                    hold(pool, s.rk, n + 1, s.passed)
                    if not isinstance(n, int):
                        hold(pool, s.tail_ps, n + (-1), s.passed)
                    elif n >= 2:
                        pool.wait_ge(s.tail_ps, n - 1)
                    split3(nc, pool, thirds(m.rk3[:, k, :]), m.rest[:], m.rk[:, k, :], s.rk3, n * 4, s.passed)

                pool.wait_ge(s.set, 2)
                inverse_norms(0, 0)
                inverse_norms(1, 1)
                with pool.Fori(0, NT // 2 - 1) as u:
                    for k in range(2):
                        inverse_norms(u * 2 + (k + 2), k)
                hold(pool, s.kl_ss, 1, s.passed)
                inv_root(nc, pool, kit.neg_half[0:B, 0:H], m.rkl[:], m.ssl[:], 1.0 / DH, 1e-16, ALU.max, s.eps, 4, s.rkl)
                pool.wait_ge(s.rkl, 1)
                split3(nc, pool, thirds(m.rkl3[:]), m.rest[0:B], m.rkl[:], s.rkl3, 0, s.passed)

            @block.scalar
            def _(act):
                def rows_T(n, k):
                    act.wait_ge(s.lnT_ps, n + 1)
                    nc.scalar.copy(m.lnT[:, k].rearrange("p f t -> p (f t)"), kit.psum(0)[:, 0:FC * P]).then_inc(s.lnT, 1)

                def query_squares(n, k):
                    act.wait_ge(s.q_ps, n + 1)
                    if not isinstance(n, int) or n > 0:
                        act.wait_ge(s.qss, n)
                    nc.scalar.activation(m.qsq[:], kit.bank[2][:].rearrange("p a t -> p (a t)"), ACT.Square).then_inc(s.q_sq, 1)
                    nc.scalar.copy(m.q[:, k, :], kit.bank[2][:].rearrange("p a t -> p (a t)")).then_inc(s.q_copied, 1)

                def key_squares(n):
                    act.wait_ge(s.k_ps, n + 1)
                    if not isinstance(n, int) or n > 0:
                        act.wait_ge(s.kss, n)
                    nc.scalar.activation(m.ksq[:], kit.bank[1][:].rearrange("p a t -> p (a t)"), ACT.Square).then_inc(s.k_sq, 1)

                def last_rows_T():
                    act.wait_ge(s.lastT_ps, 1)
                    nc.scalar.copy(m.lastT[:], kit.psum(0)[:, 0:FC * B].rearrange("p (f t) -> p f t", f=FC)).then_inc(s.lastT, 1)

                def last_squares():
                    act.wait_ge(s.kl_ps, 1)
                    act.wait_ge(s.kss, NT)
                    nc.scalar.activation(m.ksq[0:B, :], kit.bank[2][0:B].rearrange("p a t -> p (a t)"), ACT.Square).then_inc(s.kl_sq, 1)

                rows_T(0, 0)
                ahead(act)
                query_squares(0, 0)
                key_squares(0)
                rows_T(1, 1)
                with act.Fori(0, NT // 2 - 1) as u:
                    for k in range(2):
                        query_squares(u * 2 + (k + 1), 1 - k)
                        key_squares(u * 2 + (k + 1))
                        rows_T(u * 2 + (k + 2), k)
                query_squares(NT - 1, 1)
                key_squares(NT - 1)
                last_rows_T()
                last_squares()

            @block.tensor
            def _(pe):
                pe.wait_ge(s.w_in, 112)
                pe.wait_ge(s.ident16, 1)

                def rows_T(n, k):
                    pe.wait_ge(s.ln_ready, n + 1)
                    for f in range(FC):
                        mm = nc.tensor.transpose(kit.psum(0)[:, f * P:(f + 1) * P], m.ln[:, k, f * P:(f + 1) * P], kit.ident[:])
                    mm.then_inc(s.lnT_ps, 1)

                def product(lhsT, rows, bank, w, done):
                    for half in range(2):
                        for f in range(FC):
                            mm = nc.tensor.matmul(kit.psum(bank + half)[0:rows, :], lhsT[:, f, :], w[:, f, half * 512:(half + 1) * 512], start=(f == 0), stop=(f == FC - 1))
                    mm.then_inc(done, 1)

                def queries(n, k):
                    pe.wait_ge(s.lnT, n + 1)
                    if not isinstance(n, int) or n > 0:
                        pe.wait_ge(s.q_copied, n)
                    product(m.lnT[:, k], P, 4, m.wq, s.q_ps)

                def keys(n, k):
                    if not isinstance(n, int) or n > 0:
                        pe.wait_ge(s.k_sq, n)
                    product(m.lnT[:, k], P, 2, m.wk, s.k_ps)

                def queries_T(n, k):
                    pe.wait_ge(s.qh, n + 1)
                    pe.wait_ge(s.qT, n)
                    for pr in range(NP_):
                        mm = nc.tensor.transpose(kit.psum(6 + pr // 4)[:, (pr % 4) * P:(pr % 4 + 1) * P], m.qh[:, k, pr * P:(pr + 1) * P], kit.ident[:])
                    mm.then_inc(s.qT_ps, 1)

                def norms_T(n, k):
                    pe.wait_ge(s.rk3, n * 4 + 4)
                    pe.wait_ge(s.tail_sb, n)
                    nc.tensor.matmul(kit.psum(1)[0:H3, 0:P], m.rk3[:, k, :], kit.ident16[:], start=True, stop=True).then_inc(s.tail_ps, 1)

                def step(n, k, ahead):
                    if ahead >= 1:
                        queries(n + 1, 1 - k)
                    queries_T(n, k)
                    norms_T(n, k)
                    if ahead >= 1:
                        keys(n + 1, 1 - k)
                    if ahead >= 2:
                        rows_T(n + 2, k)

                rows_T(0, 0)
                queries(0, 0)
                keys(0, 0)
                rows_T(1, 1)
                with pe.Fori(0, NT // 2 - 1) as u:
                    for k in range(2):
                        step(u * 2 + k, k, 2)
                step(NT - 2, 0, 1)
                pe.wait_ge(s.lastn, 1)
                for f in range(FC):
                    mm = nc.tensor.transpose(kit.psum(0)[:, f * B:(f + 1) * B], m.lastn[:, f * P:(f + 1) * P], kit.ident[0:B, 0:B])
                mm.then_inc(s.lastT_ps, 1)
                pe.wait_ge(s.lastT, 1)
                pe.wait_ge(s.q_copied, NT)
                product(m.lastT, B, 4, m.wk, s.kl_ps)
                step(NT - 1, 1, 0)
                pe.wait_ge(s.rkl3, 4)
                pe.wait_ge(s.tail_sb, NT)
                nc.tensor.matmul(kit.psum(1)[0:H3, 0:B], m.rkl3[:], kit.ident16[0:B, 0:B], start=True, stop=True).then_inc(s.tail_ps, 1)


class CrossWeights:

    def __init__(self, kit, stack, stage, keyed):
        self.kit, self.keyed = kit, keyed
        self.m = kit.buffers(stack, wkT=([P, NP_, D], F32), wv=([P, FC, INNER], F32), wo=([P, NP_, D], F32), bo=([P, D], F32))
        if keyed:
            self.mk = kit.buffers(stack, wk_hi=([P, FC, INNER], F32R), wk_lo=([P, FC, INNER], F32R), sel=([H3, HC, P], BF16),
                                  g_x=([P, D], F32), b_x=([P, D], F32), gain=([P, 4], F32))
        self.loaded = kit.semaphore(f"{stage}_loaded")
        self.count = 16 * (10 if keyed else 4)

    def load(self, engine, wk_t, w_v, w_out, bias):
        m, d = self.m, self.kit.dram
        engine.dma_start(m.wkT[:], wk_t.rearrange("(a p) n -> p a n", p=P)).then_inc(self.loaded, 16)
        engine.dma_start(m.wv[:], w_v.rearrange("(f p) n -> p f n", p=P)).then_inc(self.loaded, 16)
        engine.dma_start(m.wo[:], w_out.rearrange("(a p) n -> p a n", p=P)).then_inc(self.loaded, 16)
        engine.dma_start(m.bo[:], bias.partition_broadcast(P)).then_inc(self.loaded, 16)
        if self.keyed:
            mk = self.mk
            engine.dma_start(mk.g_x[:], d.ln_x_g.partition_broadcast(P)).then_inc(self.loaded, 16)
            engine.dma_start(mk.b_x[:], d.ln_x_b.partition_broadcast(P)).then_inc(self.loaded, 16)
            for half in range(2):
                for i, g in enumerate((d.qn_g, d.kn_g)):
                    engine.dma_start(mk.gain[half * DH:(half + 1) * DH, i:i + 1], g.unsqueeze(1)).then_inc(self.loaded, 16)


def cross_attention(kit, stage, weights, ahead, after):
    nc, d = kit.nc, kit.dram
    X = kit.X
    keyed, wm = weights.keyed, weights.m
    TAIL = LEFT + (S if keyed else 0)
    NK = KF * P + TAIL
    TILES = [(0, P), (P, P), (KF * P, TAIL)]
    RB = 4
    TB = 4 if keyed else 2
    PB = 1 if keyed else 2
    score_bank, spread_bank = [4, 5, 4, 5], [7, 6, 7, 6]
    prob_bank, mix_bank = ([4, 5, 6], [7, 5]) if keyed else ([2, 3, 6], [7, 6])
    with kit.stage() as st:
        m = kit.buffers(
            st, qT=([P, NP_, GT], F32), qk=([P, FC, GB, H, S], F32), mix=([P, FC, H, GT], F32),
            rows=([P, RB, KF + 1, D], F32), rowsT=([P, TB, FC, NK], F32),
            prob=([P, PB, HC, NK], F32), top=([P, 2, HC], F32), ntop=([P, 2, HC], F32),
            mass=([P, 2, HC], F32), rmass=([P, 2, HC], F32))
        oT = m.qT
        if keyed:
            wk = weights.mk
            mk = kit.buffers(
                st, probT=([P, 3, 512], F32), raw=([P, 2, KF, D], F32),
                stats=([P, KF, 6], F32), mv=([P, 2, KF, 2], F32), rstd=([P, 2, KF], F32), ksq=([P, 2, 512], F32), high=([P, FC, KF * P], F32), hi=([P, FC, KF * P], F32R), lo=([P, FC, KF * P], F32R),
                ss=([P, KF * H], F32), rk=([P, 2, KF * H], F32), rk3=([P, 2, KF, H3], BF16), rest=([P, KF, H], F32), rkT=([H3, NK], BF16), rkb=([P, HC, NK], F32), score=([P, HC, NK], F32),
                valid=([1, RB, CTX], U8), mask=([1, 2, NK], BF16), one=([1, P], BF16))
        else:
            tl = kit.buffers(st, rows=([PAIRS, RB, D], BF16), prob=([P, 2, HC, PAIRS], BF16), rest=([P, HC, PARTS], F32), probT=([PAIRS, 512], BF16))
            rp = kit.buffers(st, high=([P, KF, D], F32), hi=([P, 2, KF, D], F32R), lo=([P, 2, KF, D], F32R))
            pp = kit.buffers(st, high=([P, KF, 512], F32), hi=([P, KF, 512], F32R), lo=([P, KF, 512], F32R))
        s = kit.sems(stage, "set mask tail3 rk3 gain wkT raw_free rows_free stats aggr eps rstd cent rows rT_ps rT high hi lo phigh k_ps k_sq ss rk_scaled rk "
                     "rkT_ps rkT rkT_tail rkb_ps rkb s_ps score ntop p mass normed pT_ps pT pT1 mix_ps mix0 mix1 o_ps o_act o_dve x_ps x_add "
                     "q_in qk_ps qk_act qk_dve qT_free passed_dve passed_pool")
        raw_in = kit.several(stage, "raw_in", 2)
        rows_in = kit.several(stage, "rows_in", RB)
        row_loads = 48

        def uses(g, j, buffers):
            return g * (GB // buffers) + (j // buffers + 1)

        def past(engine, sem, value):
            if not isinstance(value, int) or value > 0:
                engine.wait_ge(sem, value)

        def groups(engine, group):
            with engine.Fori(0, NG - 1) as g:
                group(g, lambda j: True)
            group(NG - 1, lambda j: j < GB)

        with nc.Block() as block:
            @block.sync
            def _(sp):
                def group(g):
                    sp.wait_ge(s.qT_free, g + 1)
                    sp.dma_start(m.qT[:], d.qT[:, :, bass.ts(g, GT)]).then_inc(s.q_in, 16)
                    for j in range(GB):
                        n, k, b = g * GB + j, j % 2, j % RB
                        if keyed:
                            sp.wait_ge(s.raw_free, n + 1)
                            sp.dma_start(mk.raw[:, k], d.ctx[n, 0:KF * P, :].rearrange("(c p) d -> p c d", p=P)).then_inc(raw_in[k], 16)
                        sp.wait_ge(s.rows_free, n + 1)
                        if keyed:
                            sp.dma_start(m.rows[0:S, b, KF, :], d.tail_lat_b[n]).then_inc(rows_in[b], 16)
                            sp.dma_start(m.rows[S:S + 1, b, KF, :], d.tail_last[bass.ds(n, 1), :]).then_inc(rows_in[b], 16)
                            sp.dma_start(mk.valid[:, b, :], d.mask[bass.ds(n, 1), :]).then_inc(rows_in[b], 16)
                        else:
                            sp.dma_start(m.rows[:, b, 0:KF, :], d.ctx[n, 0:KF * P, :].rearrange("(c p) d -> p c d", p=P)).then_inc(rows_in[b], 16)
                            sp.dma_start(m.rows[0:LEFT, b, KF, :], d.ctx[n, KF * P:CTX, :]).then_inc(rows_in[b], 16)
                            sp.dma_start(tl.rows[:, b, :], d.last_parts_b[n]).then_inc(rows_in[b], 16)

                with sp.Fori(0, NG) as g:
                    group(g)

            @block.vector
            def _(dve):
                dve.sem_inc(s.qT_free, 1)
                dve.sem_inc(s.raw_free, 2)
                dve.sem_inc(s.rows_free, RB)
                if keyed:
                    nc.vector.memset(mk.mask[:], 0.0).then_inc(s.set, 1)
                    nc.vector.memset(mk.one[:], 1.0).then_inc(s.set, 1)
                    nc.vector.memset(mk.rk3[:], 0.0).then_inc(s.set, 1)
                dve.wait_ge(weights.loaded, weights.count)
                if keyed:
                    nc.vector.scalar_tensor_tensor(wk.gain[:, 2:3], wk.gain[:, 0:1], DH ** -0.5, wk.gain[:, 1:2], ALU.mult, ALU.mult).then_inc(s.gain, 1)
                    dve.wait_ge(s.gain, 1)
                    nc.vector.tensor_scalar(wm.wkT[:], wm.wkT[:], wk.gain[:, 2:3], None, ALU.mult).then_inc(s.wkT, 1)
                else:
                    nc.vector.tensor_scalar(wm.wkT[:], wm.wkT[:], DH ** -0.5, None, ALU.mult).then_inc(s.wkT, 1)
                nc.vector.tensor_tensor(X[:], X[:], wm.bo[:].unsqueeze(1).to_broadcast([P, NT, D]), ALU.add).then_inc(s.x_add, 1)

                def norm_stats(n, k, loads):
                    if isinstance(n, int):
                        past(dve, s.aggr, n * KF)
                    dve.wait_ge(raw_in[k], loads * 16)
                    for c in range(KF):
                        nc.vector.bn_stats(mk.stats[:, c, :], mk.raw[:, k, c, :]).then_inc(s.stats, 1)
                    hold(dve, s.stats, (n + 1) * KF, s.passed_dve)
                    for c in range(KF):
                        nc.vector.bn_aggr(mk.mv[:, k, c, :], mk.stats[:, c, :]).then_inc(s.aggr, 1)

                def norm_rows(n, k, b):
                    dve.wait_ge(s.rstd, n + 1)
                    dve.wait_ge(s.rows_free, n + 1)
                    for c in range(KF):
                        nc.vector.scalar_tensor_tensor(m.rows[:, b, c, :], mk.raw[:, k, c, :], mk.mv[:, k, c, 0:1], wk.g_x[:],
                                                       ALU.subtract, ALU.mult).then_inc(s.cent, 1)
                    dve.wait_ge(s.cent, (n + 1) * KF)
                    dve.sem_inc(s.raw_free, 1)
                    for c in range(KF):
                        nc.vector.scalar_tensor_tensor(m.rows[:, b, c, :], m.rows[:, b, c, :], mk.rstd[:, k, c:c + 1], wk.b_x[:],
                                                       ALU.mult, ALU.add).then_inc(s.rows, 1)

                def key_sums(n):
                    past(dve, s.rk_scaled, n)
                    for i in range(4):
                        dve.wait_ge(s.k_sq, n * 4 + (i + 1))
                        nc.vector.tensor_reduce(mk.ss[:, i * (H // 2):(i + 1) * (H // 2)], mk.ksq[:, i % 2, :].rearrange("p (h e) -> p h e", e=DH), AX.X, ALU.add).then_inc(s.ss, 1)

                def split(n, j):
                    rows = m.rowsT[:, j % TB, :, 0:KF * P]
                    dve.wait_ge(s.rT, n + 1)
                    past(dve, s.k_ps, n * 4)
                    past(dve, s.hi, n)
                    past(dve, s.lo, n)
                    nc.vector.tensor_scalar(mk.high[:].bitcast(U32), rows.bitcast(U32), HIGH, None, ALU.bitwise_and).then_inc(s.high, 1)
                    dve.wait_ge(s.high, n + 1)
                    nc.vector.tensor_copy(mk.hi[:], mk.high[:]).then_inc(s.hi, 1)
                    nc.vector.tensor_tensor(mk.lo[:], rows, mk.high[:], ALU.subtract).then_inc(s.lo, 1)

                def maxima(n, k, chunks):
                    for c in chunks:
                        if keyed:
                            hold(dve, s.s_ps, n * HC + (c + 1), s.passed_dve)
                            hold(dve, s.rkb, n * HC + (c + 1), s.passed_dve)
                            nc.vector.tensor_tensor_reduce(mk.score[:, c, :], kit.psum(score_bank[c])[:, 0:NK], mk.rkb[:, c, :], 1.0, -3.0e38,
                                                           ALU.mult, ALU.max, m.top[:, k, c:c + 1]).then_inc(s.score, 1)
                        else:
                            dve.wait_ge(s.s_ps, n * HC + (c + 1))
                            nc.vector.reduce_max(m.top[:, k, c:c + 1], kit.psum(score_bank[c])[:, 0:NK], AX.X).then_inc(s.score, 1)
                        dve.wait_ge(s.score, n * HC + (c + 1))
                        nc.vector.tensor_scalar(m.ntop[:, k, c:c + 1], m.top[:, k, c:c + 1], -1.0, None, ALU.mult).then_inc(s.ntop, 1)

                def normed(n, k):
                    for c in range(HC):
                        dve.wait_ge(s.p, n * HC + (c + 1))
                        nc.vector.reciprocal(m.rmass[:, k, c:c + 1], m.mass[:, k, c:c + 1]).then_inc(s.mass, 1)
                    for c in range(HC):
                        dve.wait_ge(s.mass, n * HC + (c + 1))
                        nc.vector.tensor_scalar(m.prob[:, k % PB, c, :], m.prob[:, k % PB, c, :], m.rmass[:, k, c:c + 1], None, ALU.mult).then_inc(s.normed, 1)

                def probs_T(n):
                    if keyed:
                        for c, size in ((0, P), (2, TAIL)):
                            dve.wait_ge(s.pT_ps, n * 3 + (c + 1))
                            nc.vector.tensor_copy(mk.probT[0:size, c, :], kit.psum(prob_bank[c])[0:size, :]).then_inc(s.pT, 1)
                        return
                    past(dve, s.pT, n * KF)
                    past(dve, s.pT1, n * 3)
                    for c in range(KF):
                        dve.wait_ge(s.pT_ps, n * 3 + (c + 1))
                        nc.vector.tensor_scalar(pp.high[:, c, :].bitcast(U32), kit.psum(prob_bank[c]).bitcast(U32), HIGH, None, ALU.bitwise_and).then_inc(s.phigh, 1)
                    for c in range(KF):
                        dve.wait_ge(s.phigh, n * KF + (c + 1))
                        nc.vector.tensor_tensor(pp.lo[:, c, :], kit.psum(prob_bank[c]), pp.high[:, c, :], ALU.subtract).then_inc(s.pT, 1)

                def rows_high(n, b, loads):
                    dve.wait_ge(rows_in[b], loads * row_loads)
                    past(dve, s.hi, n)
                    past(dve, s.lo, n)
                    nc.vector.tensor_scalar(rp.high[:].bitcast(U32), m.rows[:, b, 0:KF, :].bitcast(U32), HIGH, None, ALU.bitwise_and).then_inc(s.high, 1)

                def mixed(n, j):
                    dve.wait_ge(s.mix_ps, n * FC + FC)
                    dve.sem_inc(s.rows_free, 1)
                    if keyed:
                        nc.vector.tensor_copy(m.mix[:, 1, :, j * S:(j + 1) * S], kit.psum(mix_bank[1]).rearrange("p (h q) -> p h q", h=H)).then_inc(s.mix1, 1)

                def queries(g):
                    for i in range(1, H, 2):
                        dve.wait_ge(s.qk_ps, g * H + (i + 1))
                        nc.vector.tensor_copy(m.qk[:, :, :, i, :], kit.psum(3).rearrange("p (f b q) -> p f b q", f=FC, b=GB)).then_inc(s.qk_dve, 1)

                def group(g, is_in):
                    for j in range(GB):
                        n, k = g * GB + j, j % 2
                        if keyed:
                            maxima(n, k, range(2))
                            if is_in(j + 2):
                                split(n + 2, j + 2)
                            maxima(n, k, range(2, HC))
                            normed(n, k)
                            if is_in(j + 3):
                                norm_rows(n + 3, 1 - k, (j + 3) % RB)
                            probs_T(n)
                            if is_in(j + 2):
                                key_sums(n + 2)
                            if is_in(j + 4):
                                norm_stats(n + 4, k, uses(g, j + 4, 2))
                        else:
                            if j + 1 == GB and is_in(GB):
                                queries(g + 1)
                            if is_in(j + 1):
                                maxima(n + 1, 1 - k, range(0, 2))
                            probs_T(n)
                            if is_in(j + 1):
                                rows_high(n + 1, (j + 1) % RB, uses(g, j + 1, RB))
                                maxima(n + 1, 1 - k, range(2, HC))
                                normed(n + 1, 1 - k)
                        mixed(n, j)
                    if keyed and is_in(GB):
                        queries(g + 1)
                    for i in range(1, NP_ // 2, 2):
                        dve.wait_ge(s.o_ps, g * (NP_ // 2) + (i + 1))
                        nc.vector.tensor_copy(oT[:, 2 * i:2 * i + 2, :], kit.psum(2 + i % 2).rearrange("p (a t) -> p a t", a=2)).then_inc(s.o_dve, 1)
                    for i in range(GT // P):
                        dve.wait_ge(s.x_ps, g * (GT // P) + (i + 1))
                        if i == 0:
                            dve.wait_ge(s.x_add, 1)
                        nc.vector.tensor_tensor(X[:, g * (GT // P) + i, :], X[:, g * (GT // P) + i, :], kit.psum(i)[:, 0:D], ALU.add).then_inc(s.x_add, 1)
                    dve.sem_inc(s.qT_free, 1)
                    for i in range(GT // P):
                        after.tile(dve, g * (GT // P) + i, s.x_add, g * (GT // P) + (i + 2))

                if keyed:
                    for n in range(2):
                        norm_stats(n, n, 1)
                    for n in range(2):
                        norm_rows(n, n, n)
                    split(0, 0)
                    norm_stats(2, 0, 2)
                    norm_rows(2, 0, 2)
                    key_sums(0)
                    split(1, 1)
                    norm_stats(3, 1, 2)
                    key_sums(1)
                queries(0)
                dve.sem_inc(s.qT_free, 1)
                if not keyed:
                    rows_high(0, 0, 1)
                    maxima(0, 0, range(HC))
                    normed(0, 0)
                groups(dve, group)

            @block.gpsimd
            def _(pool):
                def rstd(n, k):
                    hold(pool, s.aggr, (n + 1) * KF, s.passed_pool)
                    inv_root(nc, pool, kit.neg_half[:, 0:KF], mk.rstd[:, k, :], mk.mv[:, k, :, 1], 1.0, LN_EPS, ALU.add, s.eps, n + 1, s.rstd)

                def key_norms(n, k):
                    hold(pool, s.ss, (n + 1) * 4, s.passed_pool)
                    inv_root(nc, pool, kit.neg_half[:, 0:KF * H], mk.rk[:, k, :], mk.ss[:], 1.0 / DH, 1e-16, ALU.max, s.rk_scaled, n + 1, s.rk)
                    hold(pool, s.rk, n + 1, s.passed_pool)
                    split3(nc, pool, thirds(mk.rk3[:, k]), mk.rest[:], mk.rk[:, k, :].rearrange("p (c h) -> p c h", c=KF), s.rk3, n * 4, s.passed_pool)

                def tail(n):
                    past(pool, s.rkb_ps, n * HC)
                    nc.gpsimd.tensor_copy(mk.rkT[:, KF * P:NK], kit.tail_rk[:, n, :]).then_inc(s.rkT_tail, 1)

                def mask(n, k, b, loads):
                    hold(pool, rows_in[b], loads * row_loads, s.passed_pool)
                    for at, rows in ((0, slice(0, KF * P)), (NK - LEFT, slice(KF * P, CTX))):
                        nc.gpsimd.tensor_scalar(mk.mask[:, k, at:at + rows.stop - rows.start], mk.valid[:, b, rows], 1.0, MASKED, ALU.subtract, ALU.mult).then_inc(s.mask, 1)

                def tail_parts(n, k):
                    hold(pool, s.normed, (n + 1) * HC, s.passed_pool)
                    if not isinstance(n, int) or n >= 2:
                        hold(pool, s.pT_ps, n * 3 + (-3), s.passed_pool)
                    split3(nc, pool, [tl.prob[:, k, :, PARTS * i:PARTS * (i + 1)] for i in range(PARTS)], tl.rest[:],
                           m.prob[:, k, :, NK - LEFT:NK].to_broadcast([P, HC, PARTS]), s.tail3, n * 4, s.passed_pool)

                def rows_parts(n, k, b):
                    hold(pool, s.high, n + 1, s.passed_pool)
                    if not isinstance(n, int) or n >= 2:
                        hold(pool, s.mix_ps, n * FC + (-FC), s.passed_pool)
                    nc.gpsimd.tensor_copy(rp.hi[:, k], rp.high[:]).then_inc(s.hi, 1)
                    nc.gpsimd.tensor_tensor(rp.lo[:, k], m.rows[:, b, 0:KF, :], rp.high[:], ALU.subtract).then_inc(s.lo, 1)

                def group(g, is_in):
                    for j in range(GB):
                        n, k = g * GB + j, j % 2
                        if not keyed:
                            if is_in(j + 1):
                                rows_parts(n + 1, 1 - k, (j + 1) % RB)
                                tail_parts(n + 1, 1 - k)
                            continue
                        if is_in(j + 1):
                            tail(n + 1)
                            mask(n + 1, 1 - k, (j + 1) % RB, uses(g, j + 1, RB))
                        if is_in(j + 2):
                            key_norms(n + 2, k)
                        if is_in(j + 4):
                            rstd(n + 4, k)

                if keyed:
                    pool.wait_ge(s.set, 3)
                    for n in range(4):
                        rstd(n, n % 2)
                    tail(0)
                    mask(0, 0, 0, 1)
                    key_norms(0, 0)
                    key_norms(1, 1)
                ahead(pool)
                if not keyed:
                    rows_parts(0, 0, 0)
                    tail_parts(0, 0)
                groups(pool, group)
                after.inverse(pool)

            @block.scalar
            def _(act):
                def rows_T(n, j):
                    act.wait_ge(s.rT_ps, n + 1)
                    nc.scalar.copy(m.rowsT[:, j % TB], kit.bank[0][:, :, 0:NK]).then_inc(s.rT, 1)

                def norms_T(n):
                    act.wait_ge(s.rkT_ps, n + 1)
                    past(act, s.rkb_ps, n * HC)
                    nc.scalar.copy(mk.rkT[:, 0:KF * P].rearrange("h (c p) -> h c p", c=KF), kit.bank[0][0:H3, :, NK:NK + P]).then_inc(s.rkT, 1)

                def key_squares(n, c):
                    for i in range(2 * c, 2 * c + 2):
                        act.wait_ge(s.k_ps, n * 4 + (i + 1))
                        past(act, s.ss, n * 4 + (i - 1))
                        nc.scalar.activation(mk.ksq[:, i % 2, :], kit.psum(2 + i % 2), ACT.Square).then_inc(s.k_sq, 1)

                def spread(n, c):
                    act.wait_ge(s.rkb_ps, n * HC + (c + 1))
                    nc.scalar.copy(mk.rkb[:, c, :], kit.psum(spread_bank[c])[:, 0:NK]).then_inc(s.rkb, 1)

                def exps(n, k, c):
                    act.wait_ge(s.ntop, n * HC + (c + 1))
                    src = mk.score[:, c, :] if keyed else kit.psum(score_bank[c])[:, 0:NK]
                    nc.scalar.activation(m.prob[:, k % PB, c, :], src, ACT.Exp, bias=m.ntop[:, k, c:c + 1], accum_out=m.mass[:, k, c:c + 1]).then_inc(s.p, 1)

                def probs_T(n):
                    if not keyed:
                        for c in range(KF):
                            act.wait_ge(s.phigh, n * KF + (c + 1))
                            nc.scalar.copy(pp.hi[:, c, :], pp.high[:, c, :]).then_inc(s.pT1, 1)
                        act.wait_ge(s.pT_ps, n * 3 + 3)
                        nc.scalar.copy(tl.probT[:], kit.psum(prob_bank[KF])[0:PAIRS, :]).then_inc(s.pT1, 1)
                        return
                    act.wait_ge(s.pT_ps, n * 3 + 2)
                    nc.scalar.copy(mk.probT[:, 1, :], kit.psum(prob_bank[1])).then_inc(s.pT1, 1)

                def mixed(n, j):
                    act.wait_ge(s.mix_ps, n * FC + 1)
                    nc.scalar.copy(m.mix[:, 0, :, j * S:(j + 1) * S], kit.psum(mix_bank[0]).rearrange("p (h q) -> p h q", h=H)).then_inc(s.mix0, 1)
                    if not keyed:
                        act.wait_ge(s.mix_ps, n * FC + FC)
                        nc.scalar.copy(m.mix[:, 1, :, j * S:(j + 1) * S], kit.psum(mix_bank[1]).rearrange("p (h q) -> p h q", h=H)).then_inc(s.mix1, 1)

                def queries(g):
                    for i in range(0, H, 2):
                        act.wait_ge(s.qk_ps, g * H + (i + 1))
                        nc.scalar.copy(m.qk[:, :, :, i, :], kit.psum(2).rearrange("p (f b q) -> p f b q", f=FC, b=GB)).then_inc(s.qk_act, 1)

                def group(g, is_in):
                    for j in range(GB):
                        n, k = g * GB + j, j % 2
                        if keyed:
                            spread(n, 0)
                            spread(n, 1)
                            past(act, s.pT_ps, n * 3)
                            if is_in(j + 2):
                                rows_T(n + 2, j + 2)
                            for c in range(2):
                                exps(n, k, c)
                                spread(n, c + 2)
                            for c in range(2, HC):
                                exps(n, k, c)
                            if is_in(j + 2):
                                key_squares(n + 2, 0)
                            probs_T(n)
                            if is_in(j + 2):
                                key_squares(n + 2, 1)
                            if is_in(j + 1):
                                norms_T(n + 1)
                        else:
                            if j + 1 == GB and is_in(GB):
                                queries(g + 1)
                            if is_in(j + 1):
                                past(act, s.pT_ps, n * 3)
                                for c in range(0, 2):
                                    exps(n + 1, 1 - k, c)
                            probs_T(n)
                            if is_in(j + 1):
                                for c in range(2, HC):
                                    exps(n + 1, 1 - k, c)
                            if is_in(j + 2):
                                rows_T(n + 2, j + 2)
                        mixed(n, j)
                    if keyed and is_in(GB):
                        queries(g + 1)
                    for i in range(0, NP_ // 2, 2):
                        act.wait_ge(s.o_ps, g * (NP_ // 2) + (i + 1))
                        nc.scalar.copy(oT[:, 2 * i:2 * i + 2, :], kit.psum(2 + i % 2).rearrange("p (a t) -> p a t", a=2)).then_inc(s.o_act, 1)

                for n in range(2):
                    rows_T(n, n)
                    if keyed:
                        key_squares(n, 0)
                        key_squares(n, 1)
                if keyed:
                    norms_T(0)
                queries(0)
                if not keyed:
                    for c in range(HC):
                        exps(0, 0, c)
                groups(act, group)

            @block.tensor
            def _(pe):
                def rows_T(n, k, b, loads):
                    if keyed:
                        pe.wait_ge(s.rows, (n + 1) * KF)
                    pe.wait_ge(rows_in[b], loads * row_loads)
                    past(pe, s.rT, n)
                    for f in range(FC):
                        for c, (a, size) in enumerate(TILES):
                            mm = nc.tensor.transpose(kit.psum(f)[:, a:a + size], m.rows[0:size, b, c, f * P:(f + 1) * P], kit.ident[0:size, 0:size])
                    mm.then_inc(s.rT_ps, 1)

                def keys(n, j, c):
                    pe.wait_ge(s.hi, n + 1)
                    pe.wait_ge(s.lo, n + 1)
                    for half in range(2):
                        i = 2 * c + half
                        past(pe, s.k_sq, n * 4 + (i - 1))
                        products = [(r, w, f) for r, w in ((mk.hi, wk.wk_hi), (mk.hi, wk.wk_lo), (mk.lo, wk.wk_hi)) for f in range(FC)]
                        for at, (r, w, f) in enumerate(products):
                            mm = nc.tensor.matmul(kit.psum(2 + half), r[:, f, c * P:(c + 1) * P], w[:, f, half * 512:(half + 1) * 512],
                                                  start=(at == 0), stop=(at == len(products) - 1))
                        mm.then_inc(s.k_ps, 1)

                def norms_T(n, k):
                    pe.wait_ge(s.rk3, n * 4 + 4)
                    for c in range(KF):
                        mm = nc.tensor.matmul(kit.psum(c)[0:H3, NK:NK + P], mk.rk3[:, k, c, :], kit.ident16[:], start=True, stop=True)
                    mm.then_inc(s.rkT_ps, 1)

                def scores(n, k, j, chunks):
                    if not keyed:
                        pe.wait_ge(s.rT, n + 1)
                    for c in chunks:
                        if keyed:
                            if c == 0:
                                pe.wait_ge(s.rkT, n + 1)
                                pe.wait_ge(s.rkT_tail, n + 1)
                                pe.wait_ge(s.mask, (n + 1) * 2)
                                past(pe, s.mix0, n)
                            if c >= 2:
                                pe.wait_ge(s.rkb, n * HC + (c - 1))
                            nc.tensor.matmul(kit.psum(spread_bank[c])[:, 0:NK], wk.sel[:, c, :], mk.rkT[:], start=True, stop=True).then_inc(s.rkb_ps, 1)
                            if c >= 2:
                                pe.wait_ge(s.score, n * HC + (c - 1))
                            if c == 1:
                                past(pe, s.mix1, n)
                        else:
                            past(pe, s.p, n * HC + (c - 1))
                        for f in range(FC):
                            mm = nc.tensor.matmul(kit.psum(score_bank[c])[:, 0:NK], m.qk[:, f, j % GB, c * BT:(c + 1) * BT, :].rearrange("p h q -> p (h q)"),
                                                  m.rowsT[:, j % TB, f, :], start=(f == 0), stop=(f == FC - 1 and not keyed))
                        if keyed:
                            mm = nc.tensor.matmul(kit.psum(score_bank[c])[:, 0:NK], mk.one[:], mk.mask[:, k, :], start=False, stop=True)
                        mm.then_inc(s.s_ps, 1)

                def probs_T(n, k):
                    pe.wait_ge(s.normed, (n + 1) * HC)
                    if not keyed:
                        past(pe, s.mix1, n)
                    for t, (a, size) in enumerate(TILES):
                        if t == KF and not keyed:
                            pe.wait_ge(s.tail3, n * 4 + 4)
                        for c in range(HC):
                            if t == KF and not keyed:
                                mm = nc.tensor.matmul(kit.psum(prob_bank[t])[0:PAIRS, c * P:(c + 1) * P], tl.prob[:, k, c, :], kit.ident16[:], start=True, stop=True)
                                continue
                            mm = nc.tensor.transpose(kit.psum(prob_bank[t])[0:size, c * P:(c + 1) * P], m.prob[:, k % PB, c, a:a + size], kit.ident[:])
                        mm.then_inc(s.pT_ps, 1)

                def mix(n, k, b):
                    if keyed:
                        pe.wait_ge(s.pT, (n + 1) * 2)
                        pe.wait_ge(s.pT1, n + 1)
                    else:
                        pe.wait_ge(s.pT1, n * 3 + KF)
                        pe.wait_ge(s.hi, n + 1)
                        pe.wait_ge(s.lo, n + 1)
                        past(pe, s.mix0, n)
                    for f in range(FC):
                        part = slice(f * P, (f + 1) * P)
                        if keyed:
                            terms = [(m.rows[0:size, b, t, part], mk.probT[0:size, t, :]) for t, (a, size) in enumerate(TILES)]
                        else:
                            terms = [(r[:, k, t, part], q[:, t, :]) for r, q in ((rp.hi, pp.hi), (rp.lo, pp.hi), (rp.hi, pp.lo)) for t in range(KF)]
                            terms.append((tl.rows[:, b, part], tl.probT[:]))
                        for at, (lhsT, rhs) in enumerate(terms):
                            if not keyed and f == 0 and at == 2 * KF:
                                pe.wait_ge(s.pT, (n + 1) * KF)
                            if not keyed and f == 0 and at == 3 * KF:
                                pe.wait_ge(s.pT1, (n + 1) * 3)
                            mm = nc.tensor.matmul(kit.psum(mix_bank[f]), lhsT, rhs, start=(at == 0), stop=(at == len(terms) - 1))
                        mm.then_inc(s.mix_ps, 1)

                def queries(g):
                    pe.wait_ge(s.q_in, (g + 1) * 16)
                    if keyed:
                        pe.wait_ge(s.k_sq, g * (GB * 4) + 8)
                    for i in range(H):
                        if i >= 2:
                            pe.wait_ge(s.qk_dve if i % 2 else s.qk_act, g * (H // 2) + i // 2)
                        pr, half = i // 2, i % 2
                        for f in range(FC):
                            mm = nc.tensor.matmul(kit.psum(2 + i % 2)[:, f * GT:(f + 1) * GT], wm.wkT[half * DH:(half + 1) * DH, pr, f * P:(f + 1) * P],
                                                  m.qT[half * DH:(half + 1) * DH, pr, :], start=True, stop=True)
                        mm.then_inc(s.qk_ps, 1)
                    pe.wait_ge(s.qk_act, (g + 1) * (H // 2))
                    pe.wait_ge(s.qk_dve, (g + 1) * (H // 2))

                def project(g, more):
                    pe.wait_ge(s.mix0, (g + 1) * GB)
                    pe.wait_ge(s.mix1, (g + 1) * GB)
                    for i in range(NP_ // 2):
                        if i >= 2:
                            pe.wait_ge(s.o_dve if i % 2 else s.o_act, g * (NP_ // 4) + i // 2)
                        for pr in (2 * i, 2 * i + 1):
                            for half in range(2):
                                h = 2 * pr + half
                                for f in range(FC):
                                    mm = nc.tensor.matmul(kit.psum(2 + i % 2)[half * DH:(half + 1) * DH, (pr % 2) * GT:(pr % 2 + 1) * GT],
                                                          wm.wv[:, f, h * DH:(h + 1) * DH], m.mix[:, f, h, :], start=(f == 0), stop=(f == FC - 1),
                                                          skip_group_check=True)
                        mm.then_inc(s.o_ps, 1)
                    pe.wait_ge(s.rT, (g + 1) * GB + (2 if more else 0))
                    for i in range(GT // P):
                        for pr in range(NP_):
                            if i == 0 and pr % 2 == 0:
                                pe.wait_ge(s.o_dve if pr // 2 % 2 else s.o_act, g * (NP_ // 4) + (pr // 4 + 1))
                            mm = nc.tensor.matmul(kit.psum(i)[:, 0:D], oT[:, pr, i * P:(i + 1) * P], wm.wo[:, pr, :], start=(pr == 0), stop=(pr == NP_ - 1))
                        mm.then_inc(s.x_ps, 1)

                def group(g, is_in):
                    for j in range(GB):
                        n, k, b = g * GB + j, j % 2, j % RB
                        if keyed:
                            scores(n, k, j, range(0, 2))
                        else:
                            if j + 1 == GB and is_in(GB):
                                queries(g + 1)
                            if is_in(j + 1):
                                scores(n + 1, 1 - k, j + 1, range(0, 2))
                            probs_T(n, k)
                            if is_in(j + 1):
                                scores(n + 1, 1 - k, j + 1, range(2, HC))
                        if j == 0:
                            pe.wait_ge(s.x_add, g * (GT // P) + 1)
                        if is_in(j + 2):
                            rows_T(n + 2, k, (j + 2) % RB, uses(g, j + 2, RB))
                        if keyed:
                            scores(n, k, j, range(2, HC))
                            if is_in(j + 2):
                                keys(n + 2, j + 2, 0)
                            probs_T(n, k)
                            if is_in(j + 2):
                                keys(n + 2, j + 2, 1)
                            if is_in(j + 1):
                                norms_T(n + 1, 1 - k)
                        mix(n, k, b)
                    if keyed and is_in(GB):
                        queries(g + 1)
                    project(g, is_in(GB))

                pe.wait_ge(weights.loaded, weights.count)
                pe.wait_ge(s.wkT, 1)
                if keyed:
                    pe.wait_ge(s.set, 3)
                for n in range(2):
                    rows_T(n, n, n, 1)
                    if keyed:
                        keys(n, n, 0)
                        keys(n, n, 1)
                if keyed:
                    norms_T(0, 0)
                queries(0)
                if not keyed:
                    scores(0, 0, 0, range(HC))
                groups(pe, group)


class PlainWeights:
    rotary = False

    def __init__(self, kit, stack):
        self.kit = kit
        self.m = kit.buffers(stack, w=([P, FC, 3 * D], F32), wo=([P, FC, D], F32), gq=([P, 2, 16], F32))
        self.loaded, self.count = kit.semaphore("plain_loaded"), 96

    def load(self, engine):
        m, d = self.m, self.kit.dram
        for i, w in enumerate((d.WqT, d.WkT0, d.WvT)):
            engine.dma_start(m.w[:, :, i * D:(i + 1) * D], w.rearrange("(f p) n -> p f n", p=P)).then_inc(self.loaded, 16)
        engine.dma_start(m.wo[:], d.WoT.rearrange("(f p) n -> p f n", p=P)).then_inc(self.loaded, 16)
        engine.dma_start(m.gq[:, 0, :], d.qn_w.partition_broadcast(P)).then_inc(self.loaded, 16)
        engine.dma_start(m.gq[:, 1, :], d.kn_w.partition_broadcast(P)).then_inc(self.loaded, 16)


class RotaryWeights:
    rotary = True

    def __init__(self, kit, stack):
        self.kit = kit
        self.m = kit.buffers(
            stack, wo=([P, FC, D], F32), bo=([P, D], F32), cos=([P, 16], F32), sin=([P, 2, 16], F32), causal=([P, S], F32), wqk=([P, P], F32), wqkb=([P, 1], F32),
            cw=([P, 6, D], F32), cb=([P, 6], F32), bd=([P, 2, 8, 32], F32), blk=([P, P], F32),
            kvr=([32, 8, 16], F32), lor=([32, 8, 16], F32), kvb=([32, 1], F32), qlb=([P, 32], F32), klb=([P, 32], F32), lob=([P, 16], F32))
        self.zeroed, self.loaded, self.count = kit.semaphore("rotary_zeroed"), kit.semaphore("rotary_loaded"), 16 * (14 + 16 + 8)

    def zero(self, pool):
        self.kit.nc.gpsimd.memset(self.m.bd[:], 0.0).then_inc(self.zeroed, 1)
        self.kit.nc.gpsimd.memset(self.m.wqk[:], 0.0).then_inc(self.zeroed, 1)

    def load(self, engine):
        m, d = self.m, self.kit.dram
        engine.wait_ge(self.zeroed, 2)
        for src, dst in ((d.cw.rearrange("(c p) n -> p c n", p=P), m.cw[:]), (d.cb, m.cb[:]), (d.blk, m.blk[:]), (d.kvb.unsqueeze(1), m.kvb[:]),
                         (d.kv2l.unsqueeze(1).to_broadcast([32, 8, 16]), m.kvr[:]), (d.l2oT.unsqueeze(1).to_broadcast([32, 8, 16]), m.lor[:]),
                         (d.q2lb.partition_broadcast(P), m.qlb[:]), (d.kvb.partition_broadcast(P), m.klb[:]), (d.l2ob.partition_broadcast(P), m.lob[:]),
                         (d.cprojT.rearrange("(f p) n -> p f n", p=P), m.wo[:]), (d.cprojb.partition_broadcast(P), m.bo[:]),
                         (d.cos, m.cos[:]), (d.sin, m.sin[:]), (d.causal, m.causal[:])):
            engine.dma_start(dst, src).then_inc(self.loaded, 16)
        for j in range(8):
            engine.dma_start(m.bd[16 * j:16 * j + 16, 0, j, :], d.q2lT).then_inc(self.loaded, 16)
            engine.dma_start(m.bd[16 * j:16 * j + 16, 1, j, :], d.kv2lT).then_inc(self.loaded, 16)
        for j in range(4):
            engine.dma_start(m.wqk[32 * j:32 * j + 32, 32 * j:32 * j + 32], d.wqkT).then_inc(self.loaded, 16)
            engine.dma_start(m.wqkb[32 * j:32 * j + 32, :], d.wqkb.unsqueeze(1)).then_inc(self.loaded, 16)


def rotary_weights(kit, weights, w, bias):
    nc, m = kit.nc, weights.m
    with kit.stage() as st:
        t = kit.buffers(st, cbb=([P, 6, P], F32), bdv=([P, P], F32), kvbb=([32, P], F32))
        s = kit.sems("rotary_w", "m2_ps bdv cbb out_ps out ready")
        with nc.Block() as block:
            @block.vector
            def _(dve):
                dve.wait_ge(weights.loaded, weights.count)
                nc.vector.tensor_copy(t.cbb[:], m.cb[:].unsqueeze(2).to_broadcast([P, 6, P])).then_inc(s.cbb, 1)
                nc.vector.tensor_copy(t.kvbb[:], m.kvb[:].to_broadcast([32, P])).then_inc(s.cbb, 1)
                dve.wait_ge(s.m2_ps, 1)
                nc.vector.tensor_tensor(t.bdv[:], kit.psum(0)[:, 0:P], m.blk[:], ALU.mult).then_inc(s.bdv, 1)
                for f in range(FC):
                    dve.wait_ge(s.out_ps, f + 1)
                    nc.vector.tensor_copy(w[:, f, 0:512], kit.psum(3 * f + 1)).then_inc(s.out, 1)
                    nc.vector.tensor_copy(w[:, f, 512:1024], kit.psum(3 * f + 2)).then_inc(s.out, 1)
                    nc.vector.tensor_copy(w[:, f, 1024:1280], kit.psum(3 * f + 3)[:, 0:256]).then_inc(s.out, 1)
                dve.wait_ge(s.out_ps, FC + 1)
                nc.vector.tensor_tensor(bias[:, 0:512].rearrange("p (h l) -> p h l", l=32), kit.psum(1).rearrange("p (h l) -> p h l", l=32),
                                        m.qlb[:].unsqueeze(1).to_broadcast([P, 16, 32]), ALU.add).then_inc(s.ready, 1)
                nc.vector.tensor_tensor(bias[:, 512:1024].rearrange("p (h l) -> p h l", l=32), kit.psum(2).rearrange("p (h l) -> p h l", l=32),
                                        m.klb[:].unsqueeze(1).to_broadcast([P, 16, 32]), ALU.add).then_inc(s.ready, 1)
                nc.vector.tensor_tensor(bias[:, 1024:1280].rearrange("p (h l) -> p h l", l=16), kit.psum(3)[:, 0:256].rearrange("p (h l) -> p h l", l=16),
                                        m.lob[:].unsqueeze(1).to_broadcast([P, 16, 16]), ALU.add).then_inc(s.ready, 1)
                dve.wait_ge(s.ready, 3)

            @block.tensor
            def _(pe):
                pe.wait_ge(weights.loaded, weights.count)
                nc.tensor.matmul(kit.psum(0)[:, 0:P], m.kvr[:].rearrange("p a b -> p (a b)"), m.lor[:].rearrange("p a b -> p (a b)"),
                                 start=True, stop=True).then_inc(s.m2_ps, 1)
                pe.wait_ge(s.bdv, 1)

                def rows(c):
                    return t.bdv[:] if c >= 4 else m.bd[:, c // 2].rearrange("p a b -> p (a b)")

                for f in range(FC):
                    for c in range(6):
                        wide = P if c >= 4 else 256
                        mm = nc.tensor.matmul(kit.psum(3 * f + 1 + c // 2)[:, (c % 2) * wide:(c % 2 + 1) * wide], m.cw[:, c, f * P:(f + 1) * P], rows(c),
                                              start=True, stop=True)
                    mm.then_inc(s.out_ps, 1)
                pe.wait_ge(s.out, 3)
                pe.wait_ge(s.cbb, 2)
                for c in range(6):
                    wide = P if c >= 4 else 256
                    out = kit.psum(1 + c // 2)[:, (c % 2) * wide:(c % 2 + 1) * wide]
                    mm = nc.tensor.matmul(out, t.cbb[:, c, :], rows(c), start=True, stop=(c < 4))
                    if c >= 4:
                        mm = nc.tensor.matmul(out, t.kvbb[:], m.lor[:].rearrange("p a b -> p (a b)"), start=False, stop=True)
                mm.then_inc(s.out_ps, 1)


def self_attention(kit, stage, weights, norm, ahead, after):
    nc = kit.nc
    X = kit.X
    rotary, wm = weights.rotary, weights.m
    WIDE = 1280 if rotary else 768
    HF = H // FC
    LS = S ** -0.5
    EV = D // H
    with kit.stage() as st:
        m = kit.buffers(
            st, xl=([P, 2, D], F32), xlT=([P, 2, FC, P], F32),
            qk=([P, 2, 2 * H, S], F32), v=([P, 2, FC, HF * (P + EV)], F32), qT=([P, 512], F32), kT=([P, HC, BT, P], F32), score=([P, H, S], F32), top=([P, H], F32),
            prob=([P, H, S], F32), mass=([P, H], F32), rmass=([P, H], F32), spread=([P, H, P], F32), yT=([P, FC, P], F32))
        if rotary:
            r = kit.buffers(st, w=([P, FC, WIDE], F32), b=([P, WIDE], F32), lat=([P, 2 * H, S], F32), turn=([P, 2 * H, S], F32), qrT=([P, 512], F32), qb=([P, 1], F32))
            w = r.w
            rotary_weights(kit, weights, r.w, r.b)
        else:
            r = kit.buffers(st, raw=([P, 512], F32), sq=([P, 512], F32), ss=([P, 2 * H], F32), rss=([P, 2, 2 * H], F32), gain=([P, 16], F32))
            w = wm.w
        s = kit.sems(stage, "zero gain qb xl xlT_ps xlT qk_ps v_ps raw_q sq v ss scaled rss qk_n qk lat turned cosed qT_ps qT kT_act kT_dve qrT_ps qrT s_ps cut_act cut_dve masked "
                     "top shift p mass rmass prob spread y_ps yT o_ps biased x_add passed")

        n_zero = 3 if rotary else 4

        def own(v, f):
            return v[:, f, :].rearrange("p (h c) -> p h c", h=HF)[:, :, 0:EV]

        def values(buffer, f):
            return buffer[:, f * HF * EV:(f + 1) * HF * EV].rearrange("p (h e) -> p h e", h=HF)

        def steps(engine, step):
            with engine.Fori(0, NT // 2 - 2) as u:
                for k in range(2):
                    step(u * 2 + k, k, 4)
            for n in range(NT - 4, NT):
                step(n, n % 2, NT - 1 - n)

        def past(engine, sem, value):
            if not isinstance(value, int) or value > 0:
                engine.wait_ge(sem, value)

        with nc.Block() as block:
            @block.vector
            def _(dve):
                norm.ready(dve)

                def rows(n, k):
                    past(dve, s.xlT_ps, n + (-1))
                    norm.rows(m.xl[:, k, :], n).then_inc(s.xl, 1)

                def latent(n):
                    if rotary:
                        dve.wait_ge(s.qk_ps, n + 1)
                        nc.vector.tensor_tensor(r.lat[:].rearrange("p h l -> p (h l)"), kit.bank[2][:].rearrange("p a t -> p (a t)"), r.b[:, 0:1024], ALU.add).then_inc(s.lat, 1)

                def inner(n, k):
                    if rotary:
                        dve.wait_ge(s.lat, n + 1)
                        nc.vector.tensor_tensor(m.qk[:, k].rearrange("p h (i e) -> p h i e", e=2), r.lat[:].rearrange("p h (i e) -> p h i e", e=2),
                                                wm.cos[:].unsqueeze(1).unsqueeze(3).to_broadcast([P, 32, 16, 2]), ALU.mult).then_inc(s.cosed, 1)
                    else:
                        dve.wait_ge(s.sq, n + 1)
                        nc.vector.tensor_reduce(r.ss[:], r.sq[:].rearrange("p (h e) -> p h e", e=16), AX.X, ALU.add).then_inc(s.ss, 1)

                def value_rows(n, k):
                    if rotary:
                        dve.wait_ge(s.v_ps, n + 1)
                        past(dve, s.yT, n + (-1))
                        for f in range(FC):
                            nc.vector.tensor_tensor(own(m.v[:, k], f), values(kit.psum(1)[:, D:2 * D], f), values(r.b[:, 1024:1280], f), ALU.add).then_inc(s.v, 1)

                def queries_keys(n, k):
                    if rotary:
                        dve.wait_ge(s.cosed, n + 1)
                        dve.wait_ge(s.turned, n * 2 + 2)
                        nc.vector.tensor_tensor(m.qk[:, k], m.qk[:, k], r.turn[:], ALU.add).then_inc(s.qk, 1)
                    else:
                        dve.wait_ge(s.raw_q, n + 1)
                        dve.wait_ge(s.rss, n + 1)
                        nc.vector.tensor_tensor(m.qk[:, k, :, 0:16], r.raw[:].rearrange("p (h e) -> p h e", e=16),
                                                r.rss[:, k, :].unsqueeze(2).to_broadcast([P, 32, 16]), ALU.mult).then_inc(s.qk_n, 1)
                        dve.wait_ge(s.qk_n, n + 1)
                        nc.vector.tensor_tensor(m.qk[:, k, 0:H, 0:16], m.qk[:, k, 0:H, 0:16], r.gain[:].unsqueeze(1).to_broadcast([P, H, 16]), ALU.mult).then_inc(s.qk, 1)

                def keys_T(n):
                    dve.wait_ge(s.qT_ps, n * 2 + 2)
                    past(dve, s.s_ps, n)
                    for j in range(2, BT):
                        rows = slice(j * S, (j + 1) * S)
                        nc.vector.tensor_copy(m.kT[rows, :, j, :], kit.psum(3)[rows].rearrange("p (c t) -> p c t", c=HC)).then_inc(s.kT_dve, 1)

                def cut(n):
                    dve.wait_ge(s.s_ps, n + 1)
                    for j in range(2, BT):
                        rows = slice(j * S, (j + 1) * S)
                        for i in range(2):
                            nc.vector.tensor_copy(m.score[rows, i * 8:i * 8 + 8, :].rearrange("p (c r) k -> p c r k", c=2),
                                                  kit.bank[2 + i][rows].rearrange("p c (r k) -> p c r k", r=BT)[:, :, :, rows]).then_inc(s.cut_dve, 1)

                def shifted(n):
                    if rotary:
                        dve.wait_ge(s.masked, n + 1)
                    else:
                        dve.wait_ge(s.cut_act, (n + 1) * 4)
                        dve.wait_ge(s.cut_dve, (n + 1) * 4)
                    nc.vector.tensor_reduce(m.top[:], m.score[:], AX.X, ALU.max).then_inc(s.top, 1)
                    dve.wait_ge(s.top, n + 1)
                    nc.vector.tensor_tensor(m.score[:], m.score[:], m.top[:].unsqueeze(2).to_broadcast([P, H, S]), ALU.subtract).then_inc(s.shift, 1)

                def softmax(n):
                    dve.wait_ge(s.p, n + 1)
                    nc.vector.tensor_reduce(m.mass[:], m.prob[:], AX.X, ALU.add).then_inc(s.mass, 1)
                    dve.wait_ge(s.mass, n + 1)
                    nc.vector.reciprocal(m.rmass[:], m.mass[:]).then_inc(s.rmass, 1)
                    dve.wait_ge(s.rmass, n + 1)
                    nc.vector.tensor_tensor(m.prob[:], m.prob[:], m.rmass[:].unsqueeze(2).to_broadcast([P, H, S]), ALU.mult).then_inc(s.prob, 1)

                def spread(n):
                    dve.wait_ge(s.prob, n + 1)
                    past(dve, s.y_ps, n)
                    for j in range(BT):
                        rows = slice(j * S, (j + 1) * S)
                        nc.vector.transpose(m.spread[rows, :, rows], m.prob[rows]).then_inc(s.spread, 1)

                def add(n):
                    dve.wait_ge(s.o_ps, n + 1)
                    if rotary:
                        dve.wait_ge(s.biased, n + 1)
                    nc.vector.tensor_tensor(X[:, n, :], X[:, n, :], kit.psum(0)[:, D:2 * D], ALU.add).then_inc(s.x_add, 1)
                    after.tile(dve, n, s.x_add, n + 1)

                def step(n, k, ahead):
                    if ahead >= 4:
                        rows(n + 4, k)
                    if ahead >= 1:
                        cut(n + 1)
                        shifted(n + 1)
                    if ahead >= 2:
                        queries_keys(n + 2, k)
                    if ahead >= 1:
                        softmax(n + 1)
                    if ahead >= 2:
                        value_rows(n + 2, k)
                    if ahead >= 3:
                        latent(n + 3)
                    if ahead >= 2:
                        keys_T(n + 2)
                    if ahead >= 1:
                        spread(n + 1)
                    if ahead >= 3:
                        inner(n + 3, 1 - k)
                    add(n)

                rows(0, 0)
                rows(1, 1)
                nc.vector.memset(m.v[:], 0.0).then_inc(s.zero, 1)
                nc.vector.memset(m.spread[:], 0.0).then_inc(s.zero, 1)
                if rotary:
                    nc.vector.tensor_scalar(r.qb[:], wm.wqkb[:], LS, None, ALU.mult).then_inc(s.qb, 1)
                else:
                    dve.wait_ge(weights.loaded, weights.count)
                    nc.vector.scalar_tensor_tensor(r.gain[:], wm.gq[:, 0, :], 16 ** -0.5, wm.gq[:, 1, :], ALU.mult, ALU.mult).then_inc(s.gain, 1)
                    dve.wait_ge(s.gain, 1)
                dve.wait_ge(s.zero, n_zero)
                latent(0)
                inner(0, 0)
                value_rows(0, 0)
                queries_keys(0, 0)
                rows(2, 0)
                rows(3, 1)
                keys_T(0)
                latent(1)
                inner(1, 1)
                value_rows(1, 1)
                queries_keys(1, 1)
                cut(0)
                shifted(0)
                softmax(0)
                latent(2)
                keys_T(1)
                spread(0)
                inner(2, 0)
                steps(dve, step)

            @block.gpsimd
            def _(pool):
                nc.gpsimd.memset(m.kT[:], 0.0).then_inc(s.zero, 1)
                if not rotary:
                    nc.gpsimd.memset(m.qk[:], 0.0).then_inc(s.zero, 1)

                def inner(n, k):
                    if rotary:
                        pool.wait_ge(s.lat, n + 1)
                        past(pool, s.qk, n)
                        lat, turn = (x[:].rearrange("p h (i e) -> p h i e", e=2) for x in (r.lat, r.turn))
                        for e in range(2):
                            nc.gpsimd.tensor_tensor(turn[:, :, :, e], lat[:, :, :, 1 - e], wm.sin[:, e, :].unsqueeze(1).to_broadcast([P, 32, 16]), ALU.mult).then_inc(s.turned, 1)
                    else:
                        hold(pool, s.ss, n + 1, s.passed)
                        inv_root(nc, pool, kit.neg_half[:, 0:32], r.rss[:, k, :], r.ss[:], 1.0 / 16, float(np.finfo(np.float32).eps), ALU.add, s.scaled, n + 1, s.rss)

                def mask(n):
                    if rotary:
                        pool.wait_ge(s.cut_act, (n + 1) * 4)
                        pool.wait_ge(s.cut_dve, (n + 1) * 4)
                        nc.gpsimd.tensor_tensor(m.score[:], m.score[:], wm.causal[:].unsqueeze(1).to_broadcast([P, H, S]), ALU.add).then_inc(s.masked, 1)

                def bias(n):
                    if rotary:
                        pool.wait_ge(s.xl, n + 1)
                        nc.gpsimd.tensor_tensor(X[:, n, :], X[:, n, :], wm.bo[:], ALU.add).then_inc(s.biased, 1)

                def step(n, k, ahead):
                    bias(n)
                    if ahead >= 1:
                        mask(n + 1)
                    if ahead >= 3:
                        inner(n + 3, 1 - k)

                inner(0, 0)
                inner(1, 1)
                mask(0)
                inner(2, 0)
                ahead(pool)
                steps(pool, step)
                after.inverse(pool)

            @block.scalar
            def _(act):
                def norm_T(n, k):
                    act.wait_ge(s.xlT_ps, n + 1)
                    nc.scalar.copy(m.xlT[:, k].rearrange("p f t -> p (f t)"), kit.psum(0)[:, 0:D]).then_inc(s.xlT, 1)

                def inner(n, k):
                    if not rotary:
                        act.wait_ge(s.qk_ps, n + 1)
                        past(act, s.qk, n)
                        nc.scalar.activation(r.sq[:], kit.psum(4), ACT.Square).then_inc(s.sq, 1)
                        nc.scalar.copy(r.raw[:], kit.psum(4)).then_inc(s.raw_q, 1)

                def value_rows(n, k):
                    if not rotary:
                        act.wait_ge(s.v_ps, n + 1)
                        if isinstance(n, int) and n < 2:
                            act.wait_ge(s.zero, n_zero)
                        past(act, s.y_ps, n + (-1))
                        for f in range(FC):
                            nc.scalar.copy(own(m.v[:, k], f), values(kit.psum(1)[:, D:2 * D], f)).then_inc(s.v, 1)

                def queries_keys_T(n):
                    if isinstance(n, int) and n == 0:
                        act.wait_ge(s.zero, n_zero)
                    act.wait_ge(s.qT_ps, n * 2 + 1)
                    past(act, s.s_ps, n)
                    if rotary:
                        nc.scalar.copy(r.qrT[:], kit.psum(2)).then_inc(s.qrT, 1)
                    else:
                        nc.scalar.copy(m.qT[:], kit.psum(2)).then_inc(s.qT, 1)
                    act.wait_ge(s.qT_ps, n * 2 + 2)
                    for j in range(2):
                        rows = slice(j * S, (j + 1) * S)
                        nc.scalar.copy(m.kT[rows, :, j, :], kit.psum(3)[rows].rearrange("p (c t) -> p c t", c=HC)).then_inc(s.kT_act, 1)
                    if rotary:
                        act.wait_ge(s.qrT_ps, n + 1)
                        nc.scalar.activation(m.qT[:], kit.psum(2), ACT.Identity, bias=r.qb[:], scale=LS).then_inc(s.qT, 1)

                def cut(n):
                    act.wait_ge(s.s_ps, n + 1)
                    past(act, s.p, n)
                    for j in range(2):
                        rows = slice(j * S, (j + 1) * S)
                        for i in range(2):
                            nc.scalar.copy(m.score[rows, i * 8:i * 8 + 8, :].rearrange("p (c r) k -> p c r k", c=2),
                                           kit.bank[2 + i][rows].rearrange("p c (r k) -> p c r k", r=BT)[:, :, :, rows]).then_inc(s.cut_act, 1)

                def exps(n):
                    act.wait_ge(s.shift, n + 1)
                    nc.scalar.activation(m.prob[:].rearrange("p h k -> p (h k)"), m.score[:].rearrange("p h k -> p (h k)"), ACT.Exp).then_inc(s.p, 1)

                def step(n, k, ahead):
                    if ahead >= 1:
                        cut(n + 1)
                        exps(n + 1)
                    act.wait_ge(s.y_ps, n + 1)
                    past(act, s.o_ps, n)
                    nc.scalar.copy(m.yT[:].rearrange("p f t -> p (f t)"), kit.psum(1)[:, 0:D]).then_inc(s.yT, 1)
                    if ahead >= 4:
                        norm_T(n + 4, k)
                    if ahead >= 2:
                        value_rows(n + 2, k)
                    if ahead >= 3:
                        inner(n + 3, 1 - k)
                    if ahead >= 2:
                        queries_keys_T(n + 2)

                norm_T(0, 0)
                inner(0, 0)
                value_rows(0, 0)
                norm_T(1, 1)
                if rotary:
                    act.wait_ge(s.qb, 1)
                queries_keys_T(0)
                inner(1, 1)
                value_rows(1, 1)
                cut(0)
                norm_T(2, 0)
                exps(0)
                norm_T(3, 1)
                inner(2, 0)
                queries_keys_T(1)
                steps(act, step)

            @block.tensor
            def _(pe):
                if not rotary:
                    pe.wait_ge(weights.loaded, weights.count)

                def norm_T(n, k):
                    pe.wait_ge(s.xl, n + 1)
                    past(pe, s.xlT, n)
                    past(pe, s.x_add, n + (-4))
                    for f in range(FC):
                        mm = nc.tensor.transpose(kit.psum(0)[:, f * P:(f + 1) * P], m.xl[:, k, f * P:(f + 1) * P], kit.ident[:])
                    mm.then_inc(s.xlT_ps, 1)

                def project(n, k):
                    pe.wait_ge(s.xlT, n + 1)
                    past(pe, s.lat if rotary else s.raw_q, n)
                    for sem in (s.cut_act, s.cut_dve):
                        past(pe, sem, (n - 1) * 4 if isinstance(n, int) else n * 4 + (-4))
                    for i in range(WIDE // 512):
                        for f in range(FC):
                            mm = nc.tensor.matmul(kit.psum(4 + i), m.xlT[:, k, f, :], w[:, f, i * 512:(i + 1) * 512], start=(f == 0), stop=(f == FC - 1))
                    mm.then_inc(s.qk_ps, 1)

                def project_values(n, k):
                    past(pe, s.v, n * FC)
                    past(pe, s.yT, n + (-2))
                    for f in range(FC):
                        mm = nc.tensor.matmul(kit.psum(1)[:, D:2 * D], m.xlT[:, k, f, :], w[:, f, WIDE - D:WIDE], start=(f == 0), stop=(f == FC - 1))
                    mm.then_inc(s.v_ps, 1)

                def queries_keys_T(n, k):
                    pe.wait_ge(s.qk, n + 1)
                    for i in range(2):
                        for c in range(HC):
                            mm = nc.tensor.transpose(kit.psum(2 + i)[:, c * P:(c + 1) * P], m.qk[:, k, (i * HC + c) * BT:(i * HC + c + 1) * BT, :].rearrange("p h l -> p (h l)"), kit.ident[:])
                        mm.then_inc(s.qT_ps, 1)

                def latent_T(n):
                    if rotary:
                        pe.wait_ge(s.qrT, n + 1)
                        nc.tensor.matmul(kit.psum(2), wm.wqk[:], r.qrT[:], start=True, stop=True).then_inc(s.qrT_ps, 1)

                def scores(n, last):
                    pe.wait_ge(s.qT, n + 1)
                    pe.wait_ge(s.kT_act, n * 2 + 2)
                    pe.wait_ge(s.kT_dve, n * 2 + 2)
                    if not last:
                        pe.wait_ge(s.lat if rotary else s.raw_q, n + 2)
                    for c in range(HC):
                        mm = nc.tensor.matmul(kit.psum(4 + c), m.qT[:, c * P:(c + 1) * P], m.kT[:, c].rearrange("p r t -> p (r t)"), start=True, stop=True)
                    mm.then_inc(s.s_ps, 1)

                def mix(n, k):
                    pe.wait_ge(s.spread, n * BT + BT)
                    past(pe, s.yT, n)
                    for h in range(H):
                        mm = nc.tensor.matmul(kit.psum(1)[:, h // HF * P:(h // HF + 1) * P], m.v[:, k, h // HF, h % HF * P:(h % HF + 1) * P], m.spread[:, h, :], start=(h % HF == 0), stop=(h % HF == HF - 1))
                    mm.then_inc(s.y_ps, 1)

                def output(n, more):
                    pe.wait_ge(s.yT, n + 1)
                    if more:
                        pe.wait_ge(s.xlT, n + 5)
                    past(pe, s.x_add, n)
                    for f in range(FC):
                        mm = nc.tensor.matmul(kit.psum(0)[:, D:2 * D], m.yT[:, f, :], wm.wo[:, f, :], start=(f == 0), stop=(f == FC - 1))
                    mm.then_inc(s.o_ps, 1)

                def step(n, k, ahead):
                    if ahead >= 1:
                        latent_T(n + 1)
                        scores(n + 1, ahead == 1)
                    mix(n, k)
                    if ahead >= 4:
                        norm_T(n + 4, k)
                    if ahead >= 3:
                        project(n + 3, 1 - k)
                    output(n, ahead >= 4)
                    if ahead >= 2:
                        queries_keys_T(n + 2, k)
                    if ahead >= 3:
                        project_values(n + 3, 1 - k)

                norm_T(0, 0)
                project(0, 0)
                project_values(0, 0)
                norm_T(1, 1)
                queries_keys_T(0, 0)
                project(1, 1)
                project_values(1, 1)
                latent_T(0)
                scores(0, False)
                norm_T(2, 0)
                norm_T(3, 1)
                project(2, 0)
                queries_keys_T(1, 1)
                project_values(2, 0)
                steps(pe, step)


class MapWeights:

    def __init__(self, kit, stack):
        self.kit = kit
        self.m = kit.buffers(stack, wT=([P, FC, D], F32), a1T=([P, FC, D], F32), a2=([P, FC, D], F32), b=([P, D], F32))
        self.loaded, self.count = kit.semaphore("map_loaded"), 64

    def load(self, engine):
        m, d = self.m, self.kit.dram
        for sb, src in ((m.wT, d.weightT), (m.a1T, d.aux1T), (m.a2, d.aux2)):
            engine.dma_start(sb[:], src.rearrange("(f p) n -> p f n", p=P)).then_inc(self.loaded, 16)
        engine.dma_start(m.b[:], d.map_b.partition_broadcast(P)).then_inc(self.loaded, 16)


def tanh_map(kit, weights, norm):
    nc, d = kit.nc, kit.dram
    X = kit.X
    with kit.stage() as st:
        wm = weights.m
        m = kit.buffers(st, a12=([P, FC, D], F32), w=([P, FC, D], F32),
                        xl=([P, 2, D], F32), xlT=([P, 2, FC, P], F32), h=([P, 2, D], F32), y=([P, 2, D], F32), out=([P, 2, D], F32))
        s = kit.sems("map", "a12_ps a12 w_ps w xl xlT_ps xlT h_ps h y out")
        stored = kit.pair("map", "stored")
        with nc.Block() as block:
            @block.sync
            def _(sp):
                with sp.Fori(0, NT // 2) as u:
                    for k in range(2):
                        n = u * 2 + k
                        sp.wait_ge(s.out, n + 1)
                        sp.dma_start(d.out_tiles[n], m.out[:, k, :]).then_inc(stored[k], 16)
                for k in range(2):
                    sp.wait_ge(stored[k], 16 * (NT // 2 + 1))

            @block.vector
            def _(dve):
                for k in range(2):
                    dve.sem_inc(stored[k], 16)
                dve.wait_ge(s.a12_ps, 1)
                nc.vector.tensor_copy(m.a12[:], kit.psum(0).rearrange("p (f n) -> p f n", f=FC)).then_inc(s.a12, 1)
                dve.wait_ge(s.w_ps, 1)
                nc.vector.tensor_copy(m.w[:], kit.psum(1).rearrange("p (f n) -> p f n", f=FC)).then_inc(s.w, 1)
                norm.ready(dve)
                dve.wait_ge(weights.loaded, weights.count)
                norm.rows(m.xl[:, 0, :], 0).then_inc(s.xl, 1)

                def tile(n, k, more):
                    if more:
                        dve.wait_ge(s.xlT_ps, n)
                        norm.rows(m.xl[:, 1 - k, :], n + 1).then_inc(s.xl, 1)
                    dve.wait_ge(s.h_ps, n + 1)
                    nc.vector.tensor_tensor(m.h[:, k, :], kit.psum(4 + k)[:, 0:D], wm.b[:], ALU.add).then_inc(s.h, 1)
                    dve.wait_ge(s.y, n + 1)
                    dve.wait_ge(stored[k], stores(n, k))
                    nc.vector.tensor_tensor(m.out[:, k, :], X[:, n, :], m.y[:, k, :], ALU.add).then_inc(s.out, 1)

                def stores(n, k):
                    return (n + (2 - k)) * 8

                with dve.Fori(0, NT // 2 - 1) as u:
                    for k in range(2):
                        tile(u * 2 + k, k, True)
                tile(NT - 2, 0, True)
                tile(NT - 1, 1, False)

            @block.scalar
            def _(act):
                with act.Fori(0, NT // 2) as u:
                    for k in range(2):
                        n = u * 2 + k
                        act.wait_ge(s.xlT_ps, n + 1)
                        nc.scalar.copy(m.xlT[:, k].rearrange("p f t -> p (f t)"), kit.psum(2 + k)[:, 0:D]).then_inc(s.xlT, 1)
                        act.wait_ge(s.h, n + 1)
                        nc.scalar.activation(m.y[:, k, :], m.h[:, k, :], ACT.Tanh).then_inc(s.y, 1)

            @block.tensor
            def _(pe):
                pe.wait_ge(weights.loaded, weights.count)
                for lhsT, rhs, bank, done, ready in ((wm.a1T, wm.a2, 0, s.a12_ps, None), (wm.wT, m.a12, 1, s.w_ps, s.a12)):
                    if ready is not None:
                        pe.wait_ge(ready, 1)
                    for i in range(FC):
                        for f in range(FC):
                            mm = nc.tensor.matmul(kit.psum(bank)[:, i * D:(i + 1) * D], lhsT[:, f, i * P:(i + 1) * P], rhs[:, f, :], start=(f == 0), stop=(f == FC - 1))
                    mm.then_inc(done, 1)
                pe.wait_ge(s.w, 1)
                with pe.Fori(0, NT // 2) as u:
                    for k in range(2):
                        n = u * 2 + k
                        pe.wait_ge(s.xl, n + 1)
                        for f in range(FC):
                            mm = nc.tensor.transpose(kit.psum(2 + k)[:, f * P:(f + 1) * P], m.xl[:, k, f * P:(f + 1) * P], kit.ident[:])
                        mm.then_inc(s.xlT_ps, 1)
                        pe.wait_ge(s.xlT, n + 1)
                        for f in range(FC):
                            mm = nc.tensor.matmul(kit.psum(4 + k)[:, 0:D], m.xlT[:, k, f, :], m.w[:, f, :], start=(f == 0), stop=(f == FC - 1))
                        mm.then_inc(s.h_ps, 1)


E_, TOPK, CAP = 64, 8, 128
I_, IS = 128, 512
ROUTED = D + E_
GS = 512


class MixtureWeights:

    def __init__(self, kit, stack):
        self.kit = kit
        self.m = kit.buffers(stack, wg=([P, FC, E_ + 1], F32), sgu=([P, FC, 2 * IS], F32), sd=([P, IS // P, D], F32), before=([P, P], F32),
                             rank=([P, NT], F32), first=([P, E_], F32))
        self.loaded, self.count = kit.semaphore("moe_loaded"), 96

    def load(self, engine):
        m, d = self.m, self.kit.dram
        for sb, src in ((m.wg, d.gates_w), (m.sgu, d.shared_gu), (m.sd, d.shared_down)):
            engine.dma_start(sb[:], src.rearrange("(f p) n -> p f n", p=P)).then_inc(self.loaded, 16)
        for sb, src in ((m.before, d.before), (m.rank, d.rank), (m.first, d.first)):
            engine.dma_start(sb[:], src).then_inc(self.loaded, 16)


class ExpertWeights:

    def __init__(self, kit, stack):
        self.kit = kit
        m = kit.buffers(stack, wgu=([P, E_ // 2, FC, 2 * I_], F32), wd=([I_, E_ // 2, D], F32))
        self.wgu, self.wd = m
        self.loaded, self.count = kit.semaphore("experts_early"), 2 * 16 * (E_ // 2)

    def load_one(self, engine, e, place, loaded):
        d = self.kit.dram
        engine.dma_start(self.wgu[:, place], d.expert_gu[e].rearrange("(f p) n -> p f n", p=P)).then_inc(loaded, 16)
        engine.dma_start(self.wd[:, place, :], d.expert_down[e]).then_inc(loaded, 16)


def mixture(kit, kept, weights, norm):
    with kit.stage() as st:
        early = ExpertWeights(kit, st)
        route(kit, weights, norm, kept, early)
        experts(kit, kept, early)


def route(kit, weights, norm, kept, early):
    nc, d = kit.nc, kit.dram
    X = kit.X
    with kit.stage() as st:
        wm = weights.m
        m = kit.buffers(
            st, ones=([P, P], F32), routed=([P, 2, ROUTED], F32), xlT=([P, 2, FC, P], F32), xlT_all=([P, FC, B * S], F32),
            logit=([P, E_ + 1], F32), best=([P, TOPK], F32), nbest=([P, 1], F32), rest=([P, E_], F32), chosen=([P, 2, E_], F32), count=([P, 2, E_], F32),
            gate=([P, E_], F32), mass=([P, 1], F32), rmass=([P, 1], F32), keep=([P, E_], F32), place=([P, E_], F32), key=([P, E_], F32), spot=([P, TOPK], F32),
            keyT=([E_, B * S], F32), order=([E_, CAP], F32), token=([CAP, E_], F32), sgate=([P, NT], F32), gated=([P, 2, GS], F32), up=([P, 2, GS], F32), hid=([P, 2, IS // P, GS], F32))
        s = kit.sems("moe", "c_set xl xlT_ps xlT xlT_kept lg_ps logit best nbest rest chosen e mass rmass w place_ps keep placed place spot address key keyT_ps keyT "
                     "count sgate_e sgate1 sgate order struck order_ps tok1 tok su_ps silu hid so_ps x_add passed passed_pe")
        stored = kit.pair("moe", "stored")
        with nc.Block() as block:
            @block.sync
            def _(sp):
                with sp.Fori(0, NT // 2) as u:
                    for k in range(2):
                        n = u * 2 + k
                        sp.wait_ge(s.w, n + 1)
                        sp.dma_start(d.routed_tiles[n], m.routed[:, k, :]).then_inc(stored[k], 16)
                        for i in range(E_ // 2 // NT):
                            e = u * (E_ // NT) + (k * (E_ // 2 // NT) + i)
                            early.load_one(sp, e, e, early.loaded)
                for k in range(2):
                    sp.wait_ge(stored[k], 16 * (NT // 2 + 1))

            @block.vector
            def _(dve):
                for k in range(2):
                    dve.sem_inc(stored[k], 16)
                nc.vector.memset(m.ones[:], 1.0).then_inc(s.c_set, 1)
                nc.vector.memset(m.count[:], 0.0).then_inc(s.c_set, 1)
                norm.ready(dve)
                dve.wait_ge(weights.loaded, weights.count)
                dve.wait_ge(s.c_set, 2)

                def rows(n, k, stores):
                    dve.wait_ge(stored[k], stores * 16)
                    norm.rows(m.routed[:, k, 0:D], n).then_inc(s.xl, 1)

                def tile(n, k, ahead, stores):
                    dve.wait_ge(s.lg_ps, n + 1)
                    nc.vector.tensor_copy(m.logit[:], kit.psum(1)[:, 0:E_ + 1]).then_inc(s.logit, 1)
                    if ahead:
                        rows(n + 1, 1 - k, stores)
                    hold(dve, s.logit, n + 1, s.passed)
                    nc.vector.max(m.best[:], m.logit[:, 0:E_]).then_inc(s.best, 1)
                    hold(dve, s.best, n + 1, s.passed)
                    nc.vector.match_replace(m.rest[:], m.best[:], m.logit[:, 0:E_], -3.0e38).then_inc(s.rest, 1)
                    nc.vector.tensor_scalar(m.nbest[:], m.best[:, 0:1], -1.0, None, ALU.mult).then_inc(s.nbest, 1)
                    dve.wait_ge(s.rest, n + 1)
                    nc.vector.tensor_tensor(m.chosen[:, k, :], m.rest[:], m.logit[:, 0:E_], ALU.not_equal).then_inc(s.chosen, 1)
                    dve.wait_ge(s.e, n + 1)
                    dve.wait_ge(s.chosen, n + 1)
                    nc.vector.scalar_tensor_tensor(m.gate[:], m.gate[:], 1.0, m.chosen[:, k, :], ALU.mult, ALU.mult, accum_out=m.mass[:]).then_inc(s.mass, 1)
                    dve.wait_ge(s.mass, n + 1)
                    nc.vector.reciprocal(m.rmass[:], m.mass[:]).then_inc(s.rmass, 1)
                    dve.wait_ge(s.rmass, n + 1)
                    nc.vector.tensor_scalar(m.routed[:, k, D:ROUTED], m.gate[:], m.rmass[:], None, ALU.mult).then_inc(s.w, 1)
                    dve.wait_ge(s.place_ps, n + 1)
                    nc.vector.scalar_tensor_tensor(m.keep[:], kit.psum(2)[:, 0:E_], float(CAP), m.chosen[:, k, :], ALU.is_lt, ALU.mult).then_inc(s.keep, 1)
                    nc.vector.tensor_tensor(m.place[:], kit.psum(2)[:, 0:E_], wm.first[:], ALU.add).then_inc(s.placed, 1)
                    nc.vector.tensor_tensor(m.count[:, 1 - k, :], m.count[:, k, :], m.chosen[:, k, :], ALU.add).then_inc(s.count, 1)
                    dve.wait_ge(s.keep, n + 1)
                    dve.wait_ge(s.placed, n + 1)
                    nc.vector.tensor_tensor(m.place[:], m.place[:], m.keep[:], ALU.mult).then_inc(s.place, 1)
                    dve.wait_ge(s.keyT_ps, n)
                    nc.vector.tensor_scalar(m.key[:], m.keep[:], wm.rank[:, bass.ds(n, 1)], None, ALU.mult).then_inc(s.key, 1)
                    hold(dve, s.place, n + 1, s.passed)
                    nc.vector.max(m.spot[:], m.place[:]).then_inc(s.spot, 1)
                    dve.wait_ge(s.spot, n + 1)
                    nc.vector.tensor_copy(kept.address[:, n, :], m.spot[:]).then_inc(s.address, 1)

                rows(0, 0, 1)
                with dve.Fori(0, NT // 2 - 1) as u:
                    for k in range(2):
                        tile(u * 2 + k, k, True, u + (k + 1))
                tile(NT - 2, 0, True, NT // 2)
                tile(NT - 1, 1, False, 0)
                dve.wait_ge(s.sgate_e, NT)
                nc.vector.tensor_scalar(m.sgate[:], m.sgate[:], 1.0, None, ALU.add).then_inc(s.sgate1, 1)
                dve.wait_ge(s.sgate1, 1)
                nc.vector.reciprocal(m.sgate[:], m.sgate[:]).then_inc(s.sgate, 1)
                dve.wait_ge(s.keyT, NT)
                rounds = CAP // 8
                groups = B * S // GS
                for g in range(groups):
                    for i in range(IS // P):
                        r = g * (rounds // groups) + i
                        if r > 0:
                            dve.wait_ge(s.struck, r)
                        nc.vector.max(m.order[:, 8 * r:8 * r + 8], m.keyT[:]).then_inc(s.order, 1)
                        dve.wait_ge(s.order, r + 1)
                        nc.vector.match_replace(m.keyT[:], m.order[:, 8 * r:8 * r + 8], m.keyT[:], 0.0).then_inc(s.struck, 1)
                    if g == 0:
                        dve.wait_ge(s.sgate, 1)
                    for i in range(GS // P):
                        n = g * (GS // P) + i
                        dve.wait_ge(s.so_ps, n + 1)
                        nc.vector.scalar_tensor_tensor(X[:, n, :], kit.psum(6 + n % 2)[:, 0:D], m.sgate[:, n:n + 1], X[:, n, :], ALU.mult, ALU.add).then_inc(s.x_add, 1)
                dve.wait_ge(s.order_ps, 1)
                nc.vector.tensor_scalar(m.token[:], kit.psum(0)[:, 0:E_], -1.0, float(B * S), ALU.mult, ALU.add).then_inc(s.tok1, 1)
                dve.wait_ge(s.tok1, 1)
                nc.vector.tensor_scalar(kept.token[:], m.token[:], float(B * S - 1), None, ALU.min).then_inc(s.tok, 1)
                dve.wait_ge(s.tok, 1)
                dve.wait_ge(s.address, NT)
                dve.wait_ge(s.x_add, NT)

            @block.gpsimd
            def _(pool):
                pool.sem_inc(s.xlT_kept, 1)
                with pool.Fori(0, NT // 2) as u:
                    for k in range(2):
                        n = u * 2 + k
                        pool.wait_ge(s.xlT, n + 1)
                        nc.gpsimd.tensor_copy(m.xlT_all[:, :, bass.ts(n, P)], m.xlT[:, k]).then_inc(s.xlT_kept, 1)
                for g in range(B * S // GS):
                    for i in range(IS // P):
                        n = g * (IS // P) + i
                        pool.wait_ge(s.silu, 2 * n + 2)
                        if g >= 2:
                            pool.wait_ge(s.so_ps, 4 * (g - 1))
                        nc.gpsimd.tensor_tensor(m.hid[:, g % 2, i, :], m.gated[:, n % 2, :], m.up[:, n % 2, :], ALU.mult).then_inc(s.hid, 1)

            @block.scalar
            def _(act):
                def rows_T(n, k, kept):
                    act.wait_ge(s.xlT_ps, n + 1)
                    act.wait_ge(s.xlT_kept, kept)
                    nc.scalar.copy(m.xlT[:, k].rearrange("p f t -> p (f t)"), kit.psum(0)[:, 0:D]).then_inc(s.xlT, 1)

                def tile(n, k):
                    act.wait_ge(s.logit, n + 1)
                    nc.scalar.activation(m.sgate[:, bass.ds(n, 1)], m.logit[:, E_:E_ + 1], ACT.Exp, scale=-1.0).then_inc(s.sgate_e, 1)
                    act.wait_ge(s.nbest, n + 1)
                    nc.scalar.activation(m.gate[:], m.logit[:, 0:E_], ACT.Exp, bias=m.nbest[:]).then_inc(s.e, 1)

                def keys_T(n):
                    act.wait_ge(s.keyT_ps, n + 1)
                    nc.scalar.copy(m.keyT[:, bass.ds(n * P, P)], kit.psum(3)[0:E_, 0:P]).then_inc(s.keyT, 1)

                rows_T(0, 0, 1)
                with act.Fori(0, NT // 2 - 1) as u:
                    for k in range(2):
                        tile(u * 2 + k, k)
                        rows_T(u * 2 + (k + 1), 1 - k, u * 2 + (k + 1))
                        keys_T(u * 2 + k)
                tile(NT - 2, 0)
                rows_T(NT - 1, 1, NT - 1)
                keys_T(NT - 2)
                tile(NT - 1, 1)
                keys_T(NT - 1)
                with act.Fori(0, B * S // GS * (IS // P) // 2) as u:
                    for k in range(2):
                        n = u * 2 + k
                        act.wait_ge(s.su_ps, n * 2 + 1)
                        act.wait_ge(s.hid, u * 2)
                        nc.scalar.activation(m.gated[:, k, :], kit.psum(2 + k), ACT.Silu).then_inc(s.silu, 1)
                        act.wait_ge(s.su_ps, n * 2 + 2)
                        nc.scalar.copy(m.up[:, k, :], kit.psum(4 + k)).then_inc(s.silu, 1)

            @block.tensor
            def _(pe):
                pe.wait_ge(weights.loaded, weights.count)
                pe.wait_ge(s.c_set, 2)
                def logits(n, k):
                    pe.wait_ge(s.xl, n + 1)
                    for f in range(FC):
                        mm = nc.tensor.transpose(kit.psum(0)[:, f * P:(f + 1) * P], m.routed[:, k, f * P:(f + 1) * P], kit.ident[:])
                    mm.then_inc(s.xlT_ps, 1)
                    pe.wait_ge(s.xlT, n + 1)
                    if not isinstance(n, int) or n > 0:
                        pe.wait_ge(s.logit, n)
                    for f in range(FC):
                        mm = nc.tensor.matmul(kit.psum(1)[:, 0:E_ + 1], m.xlT[:, k, f, :], wm.wg[:, f, :], start=(f == 0), stop=(f == FC - 1))
                    mm.then_inc(s.lg_ps, 1)

                def places(n, k):
                    pe.wait_ge(s.chosen, n + 1)
                    pe.wait_ge(s.count, n)
                    nc.tensor.matmul(kit.psum(2)[:, 0:E_], wm.before[:], m.chosen[:, k, :], start=True, stop=False)
                    nc.tensor.matmul(kit.psum(2)[:, 0:E_], m.ones[:], m.count[:, k, :], start=False, stop=True).then_inc(s.place_ps, 1)
                    pe.wait_ge(s.keyT, n)
                    hold(pe, s.key, n + 1, s.passed_pe)
                    nc.tensor.transpose(kit.psum(3)[0:E_, 0:P], m.key[:], kit.ident[:]).then_inc(s.keyT_ps, 1)

                logits(0, 0)
                with pe.Fori(0, NT // 2 - 1) as u:
                    for k in range(2):
                        logits(u * 2 + (k + 1), 1 - k)
                        places(u * 2 + k, k)
                logits(NT - 1, 1)
                places(NT - 2, 0)
                places(NT - 1, 1)
                pe.wait_ge(s.keyT, NT)
                pe.wait_ge(s.xlT_kept, NT + 1)
                with pe.Fori(0, B * S // GS // 2) as u:
                    for k in range(2):
                        g = u * 2 + k
                        for i in range(IS // P):
                            n = g * (IS // P) + i
                            pe.wait_ge(s.hid, g * (IS // P) + max(i - 1, 0))
                            for part, bank in ((0, 2 + i % 2), (1, 4 + i % 2)):
                                for f in range(FC):
                                    mm = nc.tensor.matmul(kit.psum(bank), wm.sgu[:, f, part * IS + i * P:part * IS + (i + 1) * P], m.xlT_all[:, f, bass.ts(g, GS)],
                                                          start=(f == 0), stop=(f == FC - 1))
                                mm.then_inc(s.su_ps, 1)
                        pe.wait_ge(s.hid, g * (IS // P) + (IS // P))
                        for i in range(GS // P):
                            pe.wait_ge(s.x_add, g * (GS // P) + max(i - 1, 0))
                            for c in range(IS // P):
                                mm = nc.tensor.matmul(kit.psum(6 + i % 2)[:, 0:D], m.hid[:, k, c, i * P:(i + 1) * P], wm.sd[:, c, :], start=(c == 0), stop=(c == IS // P - 1))
                            mm.then_inc(s.so_ps, 1)
                pe.wait_ge(s.order, CAP // 8)
                nc.tensor.transpose(kit.psum(0)[:, 0:E_], m.order[:], kit.ident[0:E_, 0:E_]).then_inc(s.order_ps, 1)


def experts(kit, kept, weights):
    nc, d = kit.nc, kit.dram
    EB = 8
    with kit.stage() as st:
        m = kit.buffers(
            st, index=([CAP, EB, 1], U32), rows=([CAP, EB, ROUTED], F32), rowsT=([P, 2, FC, CAP], F32),
            silu=([CAP, 2, I_], F32), hid=([CAP, 2, I_], F32), hidT=([I_, 2, CAP], F32), out=([CAP, EB, D], F32), zero=([2, D], F32))
        s = kit.sems("exp", "zero zero_out index rT_ps rT gu_ps silu hid hT_ps hT y_ps out passed")
        late_in, rows_in, stored = (kit.several("exp", n, EB) for n in ("late_in", "rows_in", "stored"))

        def past(engine, sem, value):
            if not isinstance(value, int) or value > 0:
                engine.wait_ge(sem, value)

        def steps(engine, step):
            turns = E_ // EB // 2
            for half in range(2):
                with engine.Fori(half * turns, half * turns + turns - 1) as u:
                    for b in range(EB):
                        step(u * EB + b, b, 3, u, half * (E_ // 2))
                u = half * turns + turns - 1
                for b in range(EB):
                    step(u * EB + b, b, 3 if half == 0 else EB - 1 - b, u, half * (E_ // 2))

        def place(e, first):
            return e % (E_ // 2) if isinstance(e, int) else e + (-first)

        def use(u, b):
            return u + (1 + b // EB)

        with nc.Block() as block:
            @block.sync
            def _(sp):
                sp.wait_ge(s.zero, 1)
                sp.dma_start(d.expert_rows[0:1, :], m.zero[0:1, :]).then_inc(s.zero_out, 16)
                for half in range(2):
                    turns = E_ // EB // 2
                    with sp.Fori(half * turns, half * turns + turns) as u:
                        for b in range(EB):
                            e = u * EB + b
                            sp.wait_ge(s.out, e + 2)
                            sp.dma_start(d.expert_tiles[e], m.out[:, b, :]).then_inc(stored[b], 16)
                            if half == 0:
                                sp.wait_ge(late_in[b], u * 32)
                                weights.load_one(sp, u * EB + (b + E_ // 2), e, late_in[b])

            @block.gpsimd
            def _(pool):
                with pool.Fori(0, E_ // EB) as u:
                    for b in range(EB):
                        e = u * EB + b
                        pool.wait_ge(s.hid, e + 1)
                        pool.wait_ge(s.rT_ps, e + 1)
                        nc.gpsimd.tensor_copy(m.index[:, b, :], kept.token[:, bass.ds(e, 1)]).then_inc(s.index, 1)
                        hold(pool, s.index, e + 1, s.passed)
                        nc.gpsimd.indirect_dma_start(m.rows[:, b, :], None, d.routed, bass.IndirectOffsetOnAxis(m.index[:, b, :], 0)).then_inc(rows_in[b], 16)
                for b in range(EB):
                    pool.wait_ge(stored[b], 16 * (E_ // EB + 1))
                pool.wait_ge(s.zero_out, 16)

            @block.vector
            def _(dve):
                nc.vector.memset(m.zero[:], 0.0).then_inc(s.zero, 1)
                for b in range(EB):
                    dve.sem_inc(stored[b], 16)
                dve.sem_inc(s.hid, EB)
                dve.sem_inc(s.out, 1)

                def hidden(e, b, u):
                    dve.wait_ge(s.silu, e + 1)
                    past(dve, s.hT_ps, e - 1 if isinstance(e, int) else e + (-1))
                    nc.vector.scalar_tensor_tensor(m.hid[:, b % 2, :], m.silu[:, b % 2, :], m.rows[:, b % EB, bass.ds(e + D, 1)], kit.psum(2 + b % 2)[:, I_:2 * I_],
                                                   ALU.mult, ALU.mult).then_inc(s.hid, 1)

                def output(e, b, u):
                    dve.wait_ge(s.y_ps, e + EB + 1)
                    dve.wait_ge(stored[b], u * 16 + 16)
                    nc.vector.tensor_copy(m.out[:, b, :], kit.psum(6 + b % 2)[:, 0:D]).then_inc(s.out, 1)

                def step(e, b, ahead, u, first):
                    if ahead >= 2:
                        hidden(e + 2, b + 2, u)
                    output(e, b, u)

                hidden(0, 0, 0)
                hidden(1, 1, 0)
                steps(dve, step)

            @block.scalar
            def _(act):
                def rows_T(e, b):
                    act.wait_ge(s.rT_ps, e + EB + 1)
                    nc.scalar.copy(m.rowsT[:, b % 2].rearrange("p f t -> p (f t)"), kit.psum(b % 2)[:, 0:FC * CAP]).then_inc(s.rT, 1)

                def gate(e, b):
                    act.wait_ge(s.gu_ps, e + EB + 1)
                    act.wait_ge(s.hid, e + EB - 1 if isinstance(e, int) else e + (EB - 1))
                    nc.scalar.activation(m.silu[:, b % 2, :], kit.psum(2 + b % 2)[:, 0:I_], ACT.Silu).then_inc(s.silu, 1)

                def hidden_T(e, b):
                    act.wait_ge(s.hT_ps, e + 1)
                    nc.scalar.copy(m.hidT[:, b % 2, :], kit.psum(4 + b % 2)[:, 0:CAP]).then_inc(s.hT, 1)

                def step(e, b, ahead, u, first):
                    if ahead >= 3:
                        rows_T(e + 3, b + 3)
                    if ahead >= 2:
                        gate(e + 2, b)
                    if ahead >= 1:
                        hidden_T(e + 1, b + 1)

                for e in range(2):
                    rows_T(e, e)
                    gate(e, e)
                hidden_T(0, 0)
                rows_T(2, 2)
                steps(act, step)

            @block.tensor
            def _(pe):
                pe.sem_inc(s.rT_ps, EB)
                pe.sem_inc(s.gu_ps, EB)
                pe.sem_inc(s.y_ps, EB)

                def rows_T(e, b, u):
                    pe.wait_ge(rows_in[b % EB], use(u, b) * 16)
                    past(pe, s.rT, e - 1 if isinstance(e, int) else e + (-1))
                    for f in range(FC):
                        mm = nc.tensor.transpose(kit.psum(b % 2)[:, f * CAP:(f + 1) * CAP], m.rows[:, b % EB, f * P:(f + 1) * P], kit.ident[:])
                    mm.then_inc(s.rT_ps, 1)

                def products(e, b, u, first):
                    if isinstance(e, int) and e < E_ // 2 or not isinstance(e, int) and first == 0:
                        if isinstance(e, int) and e == 0:
                            pe.wait_ge(weights.loaded, weights.count)
                    else:
                        pe.wait_ge(late_in[b % EB], use(u, b) * 32 + (-E_ // EB // 2 * 32))
                    pe.wait_ge(s.rT, e + 1)
                    pe.wait_ge(s.hid, e + EB - 1 if isinstance(e, int) else e + (EB - 1))
                    for f in range(FC):
                        mm = nc.tensor.matmul(kit.psum(2 + b % 2)[:, 0:2 * I_], m.rowsT[:, b % 2, f, :], weights.wgu[:, place(e, first), f, :], start=(f == 0), stop=(f == FC - 1))
                    mm.then_inc(s.gu_ps, 1)

                def hidden_T(e, b):
                    pe.wait_ge(s.hid, e + EB + 1)
                    past(pe, s.hT, e - 1 if isinstance(e, int) else e + (-1))
                    nc.tensor.transpose(kit.psum(4 + b % 2)[:, 0:CAP], m.hid[:, b % 2, :], kit.ident[:]).then_inc(s.hT_ps, 1)

                def output(e, b, first):
                    pe.wait_ge(s.hT, e + 1)
                    past(pe, s.out, e)
                    nc.tensor.matmul(kit.psum(6 + b % 2)[:, 0:D], m.hidT[:, b % 2, :], weights.wd[:, place(e, first), :], start=True, stop=True).then_inc(s.y_ps, 1)

                def step(e, b, ahead, u, first):
                    if ahead >= 3:
                        rows_T(e + 3, b + 3, u)
                    if ahead >= 2:
                        products(e + 2, b + 2, u, first)
                    if ahead >= 1:
                        hidden_T(e + 1, b + 1)
                    output(e, b, first)

                for e in range(2):
                    rows_T(e, e, 0)
                    products(e, e, 0, 0)
                hidden_T(0, 0)
                rows_T(2, 2, 0)
                steps(pe, step)


def combine_queries(kit, kept, w_q, norm, zero, ahead):
    nc, d = kit.nc, kit.dram
    X = kit.X
    GQ = 512
    GN = GQ // P
    NQ = NT // GN
    with kit.stage() as st:
        m = kit.buffers(st, where=([P, 2, TOPK], U32), parts=([P, 2, TOPK, D], F32), total=([P, 2, D], F32), var=([P, GN], F32), rstd=([P, GN], F32),
                        wq=([P, FC, INNER], F32), xl=([P, GN, D], F32), xlT=([P, FC, GQ], F32), qT=([P, 2, NP_, GQ], F32))
        s = kit.sems("sum", "where total x_add var eps rstd xl xlT_ps xlT q_ps q w_in passed")
        parts_in, stored = kit.pair("sum", "parts_in"), kit.pair("sum", "stored")
        with nc.Block() as block:
            @block.sync
            def _(sp):
                sp.dma_start(m.wq[:], w_q.rearrange("(f p) n -> p f n", p=P)).then_inc(s.w_in, 16)
                ahead(sp)
                with sp.Fori(0, NQ // 2) as u:
                    for k in range(2):
                        g = u * 2 + k
                        sp.wait_ge(s.q, (g + 1) * NP_)
                        sp.dma_start(d.qT[:, :, bass.ts(g, GQ)], m.qT[:, k]).then_inc(stored[k], 16)
                for k in range(2):
                    sp.wait_ge(stored[k], 16 * (NQ // 2 + 1))

            @block.gpsimd
            def _(pool):
                def gather(g, i):
                    n, k = g * GN + i, i % 2
                    pool.wait_ge(s.total, n)
                    nc.gpsimd.tensor_copy(m.where[:, k, :], kept.address[:, n, :]).then_inc(s.where, 1)
                    hold(pool, s.where, n + 1, s.passed)
                    for c in range(TOPK):
                        nc.gpsimd.indirect_dma_start(m.parts[:, k, c, :], None, d.expert_rows, bass.IndirectOffsetOnAxis(m.where[:, k, c:c + 1], 0)).then_inc(parts_in[k], 16)

                def inverse(g):
                    hold(pool, s.var, g + 1, s.passed)
                    inv_root(nc, pool, kit.neg_half[:, 0:GN], m.rstd[:], m.var[:], 1.0, LN_EPS, ALU.add, s.eps, g + 1, s.rstd)

                def group(g, behind):
                    for i in range(GN):
                        gather(g, i)
                        if behind and i == 1:
                            inverse(g + (-1))

                group(0, False)
                with pool.Fori(0, NQ - 1) as u:
                    group(u + 1, True)
                inverse(NQ - 1)
                zero(pool)

            @block.vector
            def _(dve):
                for k in range(2):
                    dve.sem_inc(stored[k], 16)
                dve.sem_inc(s.total, 1)

                def total(g, i):
                    n, k = g * GN + i, i % 2
                    dve.wait_ge(parts_in[k], (g * (GN // 2) + (i // 2 + 1)) * (TOPK * 16))
                    nc.vector.tensor_reduce(m.total[:, k, :], m.parts[:, k].rearrange("p c d -> p d c"), AX.X, ALU.add).then_inc(s.total, 1)
                    dve.wait_ge(s.total, n + 2)
                    nc.vector.tensor_tensor(X[:, n, :], X[:, n, :], m.total[:, k, :], ALU.add).then_inc(s.x_add, 1)
                    norm.tile(dve, n, s.x_add, n + 1)

                def rows(g):
                    dve.wait_ge(s.rstd, g + 1)
                    dve.wait_ge(s.xlT_ps, g * GN)
                    for i in range(GN):
                        norm.rows(m.xl[:, i, :], g * GN + i, m.rstd[:, i:i + 1]).then_inc(s.xl, 1)

                def group(g, behind):
                    for i in range(GN):
                        total(g, i)
                        if behind and i == 1:
                            rows(g + (-1))
                    dve.wait_ge(norm.s.kept, (g + 1) * GN)
                    nc.vector.tensor_copy(m.var[:], norm.m.mv[:, bass.ds(g * GN, GN), 1]).then_inc(s.var, 1)

                group(0, False)
                with dve.Fori(0, NQ - 1) as u:
                    group(u + 1, True)
                rows(NQ - 1)

            @block.scalar
            def _(act):
                with act.Fori(0, NQ // 2) as u:
                    for k in range(2):
                        g = u * 2 + k
                        for i in range(GN):
                            act.wait_ge(s.xlT_ps, g * GN + (i + 1))
                            nc.scalar.copy(m.xlT[:, :, i * P:(i + 1) * P], kit.psum(i % 2)[:, 0:D].rearrange("p (f t) -> p f t", f=FC)).then_inc(s.xlT, 1)
                        act.wait_ge(stored[k], u * 16 + 16)
                        for i in range(NP_):
                            act.wait_ge(s.q_ps, g * NP_ + (i + 1))
                            nc.scalar.copy(m.qT[:, k, i, :], kit.psum(2 + i % 6)).then_inc(s.q, 1)

            @block.tensor
            def _(pe):
                pe.wait_ge(s.w_in, 16)
                with pe.Fori(0, NQ) as g:
                    for i in range(GN):
                        pe.wait_ge(s.xl, g * GN + (i + 1))
                        pe.wait_ge(s.xlT, g * GN + max(i - 1, 0))
                        for f in range(FC):
                            mm = nc.tensor.transpose(kit.psum(i % 2)[:, f * P:(f + 1) * P], m.xl[:, i, f * P:(f + 1) * P], kit.ident[:])
                        mm.then_inc(s.xlT_ps, 1)
                    pe.wait_ge(s.xlT, (g + 1) * GN)
                    for i in range(NP_):
                        pe.wait_ge(s.q, g * NP_ + max(i - 5, 0))
                        for f in range(FC):
                            mm = nc.tensor.matmul(kit.psum(2 + i % 6), m.wq[:, f, i * P:(i + 1) * P], m.xlT[:, f, :], start=(f == 0), stop=(f == FC - 1))
                        mm.then_inc(s.q_ps, 1)



def build(nc, dram):
    d = dram
    with ExitStack() as ctx:
        kit = Kit(nc, ctx, dram)
        with kit.stage() as outer:
            norms = named({stage: Norm(kit, stage, outer) for stage in ("sa0", "moe", "lq1", "sa1", "map")})
            kept = kit.buffers(outer, token=([CAP, E_], U32), address=([P, NT, TOPK], U32))
            with kit.stage() as st:
                plain = PlainWeights(kit, st)
                with kit.stage() as inner:
                    kit.tail_rk = inner.enter_context(nc.sbuf_tensor("tail_rk", [H3, B, S + LEFT], BF16))
                    cross = CrossWeights(kit, inner, "xa0", True)
                    latent_queries(kit, cross, lambda engine: cross.load(engine, d.WkT, d.Wkv[:, INNER:2 * INNER], d.Wout, d.bout))
                    cross_attention(kit, "xa0", cross, plain.load, norms.sa0)
                mix = MixtureWeights(kit, st)
                self_attention(kit, "sa0", plain, norms.sa0, mix.load, norms.moe)
                mixture(kit, kept, mix, norms.moe)
            with kit.stage() as st:
                turning = RotaryWeights(kit, st)
                with kit.stage() as inner:
                    cross = CrossWeights(kit, inner, "xa1", False)
                    combine_queries(kit, kept, d.wq1, norms.lq1, turning.zero, lambda engine: cross.load(engine, d.wkT1, d.wv1, d.wo1, d.bo1))
                    cross_attention(kit, "xa1", cross, turning.load, norms.sa1)
                last = MapWeights(kit, st)
                self_attention(kit, "sa1", turning, norms.sa1, last.load, norms.map)
                tanh_map(kit, last, norms.map)


def kernel(**inputs):
    import concourse.bacc as bacc
    from concourse.bass_utils import run_bass_kernel_spmd

    a = {k: np.asarray(v) for k, v in inputs.items()}
    x0, s0, f0, x1, s1, f1 = (f"L{i}_{n}_" for i in range(2) for n in ("xattn", "attn", "ffn"))
    row = np.arange(P)
    freq = np.outer(row % S, 1.0 / 10000.0 ** (np.arange(0, 32, 2, dtype=np.float32) / np.float32(32))).astype(np.float32)
    constants = {
        "ident": np.eye(P), "sel": np.arange(H3)[:, None, None] % S == BT * np.arange(HC)[None, :, None] + row[None, None, :] // S,
        "cos": np.cos(freq), "sin": np.stack([-np.sin(freq), np.sin(freq)], 1),
        "causal": np.where(np.arange(S)[None, :] <= (row % S)[:, None], 0.0, -3.0e38), "blk": row[:, None] // 16 == row[None, :] // 16,
        "before": row[:, None] < row[None, :], "rank": B * S - (np.arange(NT)[None, :] * P + row[:, None]),
        "first": np.broadcast_to(1.0 + CAP * np.arange(E_), (P, E_)),
    }
    arrays = {k: v.astype(np.float32) for k, v in constants.items()}
    arrays |= {
        "x": a["x"].reshape(B * S, D), "ctx": a["ctx_1024"], "mask": a["mask_BxS2_bf1"].view(np.uint8),
        "ln_x_g": a[x0 + "ln_x_g"], "ln_x_b": a[x0 + "ln_x_b"], "ln_l_g": a[x0 + "ln_l_g"], "ln_l_b": a[x0 + "ln_l_b"],
        "qn_g": a[x0 + "qn_g"], "kn_g": a[x0 + "kn_g"], "Wq": a[x0 + "Wq"], "Wkv": a[x0 + "Wkv"],
        "WkT": a[x0 + "Wkv"][:, :INNER].T, "Wout": a[x0 + "Wout"], "bout": a[x0 + "bout"],
        "WqT": a[s0 + "Wq"].T, "WkT0": a[s0 + "Wk"].T, "WvT": a[s0 + "Wv"].T, "WoT": a[s0 + "Wo"].T, "qn_w": a[s0 + "qn_w"], "kn_w": a[s0 + "kn_w"],
        "gates_w": np.concatenate([a[f0 + "gate_w"], a[f0 + "shared_gate_w"]], 1), "shared_gu": a[f0 + "shared_gate_up_w"], "shared_down": a[f0 + "shared_down_w"],
        "expert_gu": a[f0 + "expert_gate_up_w"], "expert_down": a[f0 + "expert_down_w"],
        "wq1": a[x1 + "wq"].reshape(D, INNER), "wkT1": a[x1 + "wk"].reshape(D, INNER).T, "wv1": a[x1 + "wv"].reshape(D, INNER),
        "wo1": a[x1 + "wo"].reshape(INNER, D), "bo1": a[x1 + "bo"],
        "cw": a[s1 + "c_attn_w"], "cb": a[s1 + "c_attn_b"].reshape(6, P).T, "q2lT": a[s1 + "q2l_w"].T, "q2lb": a[s1 + "q2l_b"], "kv2l": a[s1 + "kv2l_w"], "kv2lT": a[s1 + "kv2l_w"].T,
        "kvb": a[s1 + "kv2l_b"], "l2oT": a[s1 + "l2o_w"].T, "l2ob": a[s1 + "l2o_b"], "wqkT": a[s1 + "wqk_w"].T, "wqkb": a[s1 + "wqk_b"],
        "cprojT": a[s1 + "cproj_w"].T, "cprojb": a[s1 + "cproj_b"],
        "weightT": a[f1 + "weight"].T, "aux1T": a[f1 + "aux_weight1"].T, "aux2": a[f1 + "aux_weight2"], "map_b": a[f1 + "bias"],
    }
    arrays = {k: np.ascontiguousarray(v) for k, v in arrays.items()}
    nc = bacc.Bacc("TRN2", target_bir_lowering=False, num_devices=1)
    handles = {k: nc.dram_tensor(f"in_{k}", v.shape, mybir.dt.from_np(v.dtype), kind="ExternalInput").ap() for k, v in arrays.items()}
    out = nc.dram_tensor("out_x", (B * S, D), F32, kind="ExternalOutput").ap()
    handles["out"] = out
    handles["out_tiles"] = out.rearrange("(t p) d -> t p d", p=P)
    handles["qT"] = nc.dram_tensor("scratch_qT", (P, NP_, B * S), F32, kind="Internal").ap()
    lat = nc.dram_tensor("scratch_lat", (B * S, D), F32, kind="Internal").ap()
    handles["tail_lat"] = lat.rearrange("(t p) d -> t p d", p=P)
    handles["tail_lat_b"] = lat.rearrange("(b s) d -> b s d", s=S)
    handles["tail_last"] = nc.dram_tensor("scratch_last", (B, D), F32, kind="Internal").ap()
    parts = nc.dram_tensor("scratch_last_parts", (PARTS, PARTS, B, D), BF16, kind="Internal").ap()
    handles["last_parts"] = parts.rearrange("i j b d -> i b j d")
    handles["last_parts_b"] = parts.rearrange("i j b d -> b (i j) d")
    handles["routed"] = nc.dram_tensor("scratch_routed", (B * S, ROUTED), F32, kind="Internal").ap()
    handles["routed_tiles"] = handles["routed"].rearrange("(t p) d -> t p d", p=P)
    handles["expert_rows"] = nc.dram_tensor("scratch_expert", (1 + E_ * CAP, D), F32, kind="Internal").ap()
    handles["expert_tiles"] = handles["expert_rows"][1:1 + E_ * CAP, :].rearrange("(e c) d -> e c d", c=CAP)
    build(nc, named(handles))
    res = run_bass_kernel_spmd(nc, [{f"in_{k}": v for k, v in arrays.items()}], core_ids=[0])
    return res.results[0]["out_x"].reshape(B, S, D)
```
